# Optimizing a Trainium2 kernel written in Bass

```python
import numpy as np
import jax
import jax.numpy as jnp

def _softmax(x, axis=-1):
    return jax.nn.softmax(x, axis=axis)

def _gelu(x):
    return jax.nn.gelu(x, approximate=True)

def _silu(x):
    return jax.nn.silu(x)

def _sigmoid(x):
    return jax.nn.sigmoid(x)

def _layernorm(x, axis=-1, eps=1e-05):
    m = jnp.mean(x, axis=axis, keepdims=True)
    v = jnp.var(x, axis=axis, keepdims=True)
    return (x - m) / jnp.sqrt(v + eps)

def _scatter_add(tgt, idx, src, axis=0):
    return tgt.at[idx].add(src)

def _segment_sum(src, seg, n):
    return jax.ops.segment_sum(src, seg, n)
kernel_name = 'mk_seq_preln_d2_jaxref_r4_ec878d'

def setup_inputs(seed: int=0):
    np.random.seed(seed)
    _w = jnp.asarray

    def _L0_attn_setup():
        import jax, jax.numpy as jnp
        import numpy as np
        N_HEADS = 16
        D_EMBD = 256
        B, T = (2, 512)
        key = jax.random.key(seed)
        k1, k2, k3 = jax.random.split(key, 3)
        x = jax.random.normal(k1, (B, T, D_EMBD), dtype=jnp.float32)
        W1 = jax.random.normal(k2, (D_EMBD, 3 * D_EMBD), dtype=jnp.float32) / np.sqrt(D_EMBD)
        b1 = jnp.zeros((3 * D_EMBD,), dtype=jnp.float32)
        W2 = jax.random.normal(k3, (D_EMBD, D_EMBD), dtype=jnp.float32) / np.sqrt(D_EMBD)
        b2 = jnp.zeros((D_EMBD,), dtype=jnp.float32)
        return {'x': x, 'W1': W1, 'b1': b1, 'W2': W2, 'b2': b2}
    _L0_attn_in = _L0_attn_setup()

    def _L0_ffn_setup():
        import jax, jax.numpy as jnp
        import numpy as np
        B, S, D = (4, 512, 256)
        E, K = (8, 2)
        H = 352
        key = jax.random.key(seed)
        kx, kr, k1, k2, k3 = jax.random.split(key, 5)
        s = 0.02
        return {'x': jax.random.normal(kx, (B, S, D), dtype=jnp.float32), 'w_router': jax.random.normal(kr, (E, D), dtype=jnp.float32) * s, 'w1': jax.random.normal(k1, (E, D, H), dtype=jnp.float32) * s, 'w2': jax.random.normal(k2, (E, H, D), dtype=jnp.float32) * s, 'w3': jax.random.normal(k3, (E, D, H), dtype=jnp.float32) * s}
    _L0_ffn_in = _L0_ffn_setup()

    def _L1_attn_setup():
        import jax, jax.numpy as jnp
        import numpy as np
        CHUNK = 32
        HEADS = 4
        EPS_RMS = 1e-05

        def silu(x):
            return jax.nn.silu(x)

        def l2norm(x, eps=1e-06):
            return x * jax.lax.rsqrt(jnp.sum(x * x, axis=-1, keepdims=True) + eps)

        def short_conv(x, w):
            K = w.shape[1]
            L = x.shape[1]
            xp = jnp.pad(x, ((0, 0), (K - 1, 0), (0, 0)))
            out = xp[:, 0:L, :] * w[:, 0]
            for k in range(1, K):
                out = out + xp[:, k:k + L, :] * w[:, k]
            return out

        def delta_rule_chunkwise(q, k, v, beta, chunk=CHUNK):
            b, h, l, dk = q.shape
            dv = v.shape[-1]
            n = l // chunk
            q = l2norm(q)
            k = l2norm(k)
            v = v * beta[..., None]
            k_beta = k * beta[..., None]
            resh = lambda x: x.reshape(b, h, n, chunk, -1)
            q, k, v, k_beta = map(resh, (q, k, v, k_beta))
            strict_lower = jnp.tril(jnp.ones((chunk, chunk), bool), -1)
            attn = jnp.where(strict_lower, -(k_beta @ jnp.swapaxes(k, -1, -2)), 0.0)
            for i in range(1, chunk):
                row = attn[..., i, :]
                new = attn[..., i, :i] + jnp.einsum('...j,...jk->...k', row, attn[..., :, :i])
                attn = attn.at[..., i, :i].set(new)
            attn = attn + jnp.eye(chunk, dtype=attn.dtype)
            u = attn @ v
            w = attn @ k_beta
            lower_incl = jnp.tril(jnp.ones((chunk, chunk), bool))
            qc, kc, uc, wc = [jnp.moveaxis(x, 2, 0) for x in (q, k, u, w)]
            S0 = jnp.zeros((b, h, dk, dv), q.dtype)

            def step(S, inp):
                q_i, k_i, u_i, w_i = inp
                attn_i = jnp.where(lower_incl, q_i @ jnp.swapaxes(k_i, -1, -2), 0.0)
                u_adj = u_i - w_i @ S
                o_i = q_i @ S + attn_i @ u_adj
                S = S + jnp.swapaxes(k_i, -1, -2) @ u_adj
                return (S, o_i)
            S, o = jax.lax.scan(step, S0, (qc, kc, uc, wc))
            o = jnp.moveaxis(o, 0, 2).reshape(b, h, l, dv)
            return (o, S)

        def ema_rule(v, gamma):
            v_t = jnp.moveaxis(v, 2, 0)
            g_t = jnp.moveaxis(gamma, 2, 0)
            s0 = jnp.zeros(v.shape[:2] + (v.shape[-1],), v.dtype)

            def step(s, inp):
                vt, gt = inp
                s = gt[..., None] * s + (1.0 - gt[..., None]) * vt
                return (s, s)
            s_fin, out = jax.lax.scan(step, s0, (v_t, g_t))
            return (jnp.moveaxis(out, 0, 2), s_fin)

        def rms_norm(x, w, eps=EPS_RMS):
            return x * jax.lax.rsqrt(jnp.mean(x * x, axis=-1, keepdims=True) + eps) * w
        key = jax.random.key(seed)
        ks = jax.random.split(key, 16)
        b, l, d = (4, 512, 256)
        H, conv_K = (HEADS, 4)
        s = 0.02
        return {'hidden_states': jax.random.normal(ks[0], (b, l, d), jnp.float32), 'Wq': jax.random.normal(ks[1], (d, d), jnp.float32) * s, 'Wk': jax.random.normal(ks[2], (d, d), jnp.float32) * s, 'Wv': jax.random.normal(ks[3], (d, d), jnp.float32) * s, 'conv_q': jax.random.normal(ks[4], (d, conv_K), jnp.float32) * 0.3, 'conv_k': jax.random.normal(ks[5], (d, conv_K), jnp.float32) * 0.3, 'conv_v': jax.random.normal(ks[6], (d, conv_K), jnp.float32) * 0.3, 'Wb': jax.random.normal(ks[7], (d, H), jnp.float32) * s, 'Wdec': jax.random.normal(ks[8], (d, H), jnp.float32) * s, 'Wmix': jax.random.normal(ks[9], (d, H), jnp.float32) * s, 'conv_mix': jax.random.normal(ks[10], (H, conv_K), jnp.float32) * 0.3, 'mix_bias': jnp.full((H,), -2.0, jnp.float32), 'rms_w': jnp.ones((d // H,), jnp.float32), 'Wo': jax.random.normal(ks[11], (d, d), jnp.float32) * s}
    _L1_attn_in = _L1_attn_setup()

    def _L1_ffn_setup():
        import jax, jax.numpy as jnp
        import numpy as np
        from jax import lax
        T, B, I, M, O = (64, 64, 256, 256, 256)

        def _xavier(key, shape):
            fan_out, fan_in = shape
            limit = float(np.sqrt(6.0 / (fan_in + fan_out)))
            return jax.random.uniform(key, shape, jnp.float32, -limit, limit)
        key = jax.random.key(seed)
        ks = jax.random.split(key, 9)
        x = jax.random.normal(ks[0], (T, B, I), jnp.float32)
        return {'x': x, 'wf': _xavier(ks[1], (M, I)), 'uf': _xavier(ks[2], (M, M)), 'bf': jnp.zeros((M,), jnp.float32), 'wi': _xavier(ks[3], (M, I)), 'ui': _xavier(ks[4], (M, M)), 'bi': jnp.zeros((M,), jnp.float32), 'wc': _xavier(ks[5], (M, I)), 'uc': _xavier(ks[6], (M, M)), 'bc': jnp.zeros((M,), jnp.float32), 'wo': _xavier(ks[7], (O, I)), 'uo': _xavier(ks[8], (O, M)), 'bo': jnp.zeros((O,), jnp.float32), 'in_c': jnp.zeros((M,), jnp.float32)}
    _L1_ffn_in = _L1_ffn_setup()
    _d = {'L0_attn_x': _L0_attn_in['x'], 'L0_attn_W1': _L0_attn_in['W1'], 'L0_attn_b1': _L0_attn_in['b1'], 'L0_attn_W2': _L0_attn_in['W2'], 'L0_attn_b2': _L0_attn_in['b2'], 'L0_ffn_w_router': _L0_ffn_in['w_router'], 'L0_ffn_w1': _L0_ffn_in['w1'], 'L0_ffn_w2': _L0_ffn_in['w2'], 'L0_ffn_w3': _L0_ffn_in['w3'], 'L1_attn_Wq': _L1_attn_in['Wq'], 'L1_attn_Wk': _L1_attn_in['Wk'], 'L1_attn_Wv': _L1_attn_in['Wv'], 'L1_attn_conv_q': _L1_attn_in['conv_q'], 'L1_attn_conv_k': _L1_attn_in['conv_k'], 'L1_attn_conv_v': _L1_attn_in['conv_v'], 'L1_attn_Wb': _L1_attn_in['Wb'], 'L1_attn_Wdec': _L1_attn_in['Wdec'], 'L1_attn_Wmix': _L1_attn_in['Wmix'], 'L1_attn_conv_mix': _L1_attn_in['conv_mix'], 'L1_attn_mix_bias': _L1_attn_in['mix_bias'], 'L1_attn_rms_w': _L1_attn_in['rms_w'], 'L1_attn_Wo': _L1_attn_in['Wo'], 'L1_ffn_wf': _L1_ffn_in['wf'], 'L1_ffn_uf': _L1_ffn_in['uf'], 'L1_ffn_bf': _L1_ffn_in['bf'], 'L1_ffn_wi': _L1_ffn_in['wi'], 'L1_ffn_ui': _L1_ffn_in['ui'], 'L1_ffn_bi': _L1_ffn_in['bi'], 'L1_ffn_wc': _L1_ffn_in['wc'], 'L1_ffn_uc': _L1_ffn_in['uc'], 'L1_ffn_bc': _L1_ffn_in['bc'], 'L1_ffn_wo': _L1_ffn_in['wo'], 'L1_ffn_uo': _L1_ffn_in['uo'], 'L1_ffn_bo': _L1_ffn_in['bo'], 'L1_ffn_in_c': _L1_ffn_in['in_c']}
    _x0 = _d['L0_attn_x']
    _d['L0_attn_x'] = jax.random.normal(jax.random.fold_in(jax.random.key(seed), 1), (1, 4096, 256), dtype=_x0.dtype)
    del _x0
    return _d

def reference(L0_attn_x, L0_attn_W1, L0_attn_b1, L0_attn_W2, L0_attn_b2, L0_ffn_w_router, L0_ffn_w1, L0_ffn_w2, L0_ffn_w3, L1_attn_Wq, L1_attn_Wk, L1_attn_Wv, L1_attn_conv_q, L1_attn_conv_k, L1_attn_conv_v, L1_attn_Wb, L1_attn_Wdec, L1_attn_Wmix, L1_attn_conv_mix, L1_attn_mix_bias, L1_attn_rms_w, L1_attn_Wo, L1_ffn_wf, L1_ffn_uf, L1_ffn_bf, L1_ffn_wi, L1_ffn_ui, L1_ffn_bi, L1_ffn_wc, L1_ffn_uc, L1_ffn_bc, L1_ffn_wo, L1_ffn_uo, L1_ffn_bo, L1_ffn_in_c):

    def _L0_attn_ref(x, W1, b1, W2, b2):
        import jax, jax.numpy as jnp
        import numpy as np
        N_HEADS = 16
        D_EMBD = 256
        B, T = (2, 512)
        bs, t, d = x.shape
        h = N_HEADS
        kqv = x @ W1 + b1
        k, q, v = jnp.split(kqv, 3, axis=-1)

        def to_heads(z):
            return z.reshape(bs, t, h, d // h).transpose(0, 2, 1, 3)
        k, q, v = (to_heads(k), to_heads(q), to_heads(v))
        mask = jnp.tril(jnp.ones((t, t), dtype=bool))
        attn = jnp.where(mask, jnp.einsum('bhqd,bhkd->bhqk', q, k), 0.0)
        out = jnp.einsum('bhqk,bhkd->bhqd', attn, v)
        out = out.transpose(0, 2, 1, 3).reshape(bs, t, d)
        return out @ W2 + b2

    def _L0_ffn_ref(x, w_router, w1, w2, w3):
        import jax, jax.numpy as jnp
        import numpy as np
        B, S, D = (4, 512, 256)
        E, K = (8, 2)
        H = 352
        bsz, seqlen, dim = x.shape
        xf = x.reshape(-1, dim)
        scores = jax.nn.softmax(xf @ w_router.T, axis=-1)
        expert_weights, expert_indices = jax.lax.top_k(scores, K)
        h = jax.nn.silu(jnp.einsum('td,edh->eth', xf, w1)) * jnp.einsum('td,edh->eth', xf, w3)
        y = jnp.einsum('eth,ehd->etd', h, w2)
        y_t = jnp.swapaxes(y, 0, 1)
        sel = jnp.take_along_axis(y_t, expert_indices[:, :, None], axis=1)
        out = jnp.sum(expert_weights[:, :, None] * sel, axis=1)
        return out.reshape(bsz, seqlen, dim)

    def _L1_attn_ref(hidden_states, Wq, Wk, Wv, conv_q, conv_k, conv_v, Wb, Wdec, Wmix, conv_mix, mix_bias, rms_w, Wo):
        import jax, jax.numpy as jnp
        import numpy as np
        CHUNK = 32
        HEADS = 4
        EPS_RMS = 1e-05

        def silu(x):
            return jax.nn.silu(x)

        def l2norm(x, eps=1e-06):
            return x * jax.lax.rsqrt(jnp.sum(x * x, axis=-1, keepdims=True) + eps)

        def short_conv(x, w):
            K = w.shape[1]
            L = x.shape[1]
            xp = jnp.pad(x, ((0, 0), (K - 1, 0), (0, 0)))
            out = xp[:, 0:L, :] * w[:, 0]
            for k in range(1, K):
                out = out + xp[:, k:k + L, :] * w[:, k]
            return out

        def delta_rule_chunkwise(q, k, v, beta, chunk=CHUNK):
            b, h, l, dk = q.shape
            dv = v.shape[-1]
            n = l // chunk
            q = l2norm(q)
            k = l2norm(k)
            v = v * beta[..., None]
            k_beta = k * beta[..., None]
            resh = lambda x: x.reshape(b, h, n, chunk, -1)
            q, k, v, k_beta = map(resh, (q, k, v, k_beta))
            strict_lower = jnp.tril(jnp.ones((chunk, chunk), bool), -1)
            attn = jnp.where(strict_lower, -(k_beta @ jnp.swapaxes(k, -1, -2)), 0.0)
            for i in range(1, chunk):
                row = attn[..., i, :]
                new = attn[..., i, :i] + jnp.einsum('...j,...jk->...k', row, attn[..., :, :i])
                attn = attn.at[..., i, :i].set(new)
            attn = attn + jnp.eye(chunk, dtype=attn.dtype)
            u = attn @ v
            w = attn @ k_beta
            lower_incl = jnp.tril(jnp.ones((chunk, chunk), bool))
            qc, kc, uc, wc = [jnp.moveaxis(x, 2, 0) for x in (q, k, u, w)]
            S0 = jnp.zeros((b, h, dk, dv), q.dtype)

            def step(S, inp):
                q_i, k_i, u_i, w_i = inp
                attn_i = jnp.where(lower_incl, q_i @ jnp.swapaxes(k_i, -1, -2), 0.0)
                u_adj = u_i - w_i @ S
                o_i = q_i @ S + attn_i @ u_adj
                S = S + jnp.swapaxes(k_i, -1, -2) @ u_adj
                return (S, o_i)
            S, o = jax.lax.scan(step, S0, (qc, kc, uc, wc))
            o = jnp.moveaxis(o, 0, 2).reshape(b, h, l, dv)
            return (o, S)

        def ema_rule(v, gamma):
            v_t = jnp.moveaxis(v, 2, 0)
            g_t = jnp.moveaxis(gamma, 2, 0)
            s0 = jnp.zeros(v.shape[:2] + (v.shape[-1],), v.dtype)

            def step(s, inp):
                vt, gt = inp
                s = gt[..., None] * s + (1.0 - gt[..., None]) * vt
                return (s, s)
            s_fin, out = jax.lax.scan(step, s0, (v_t, g_t))
            return (jnp.moveaxis(out, 0, 2), s_fin)

        def rms_norm(x, w, eps=EPS_RMS):
            return x * jax.lax.rsqrt(jnp.mean(x * x, axis=-1, keepdims=True) + eps) * w
        b, l, d = hidden_states.shape
        H = HEADS
        dk = d // H
        dv = d // H
        q = silu(short_conv(hidden_states @ Wq, conv_q))
        k = silu(short_conv(hidden_states @ Wk, conv_k))
        v = silu(short_conv(hidden_states @ Wv, conv_v))
        mix_inp = silu(short_conv(hidden_states @ Wmix, conv_mix))
        q = silu(q)
        k = silu(k)
        to_heads = lambda x, dh: jnp.transpose(x.reshape(b, l, H, dh), (0, 2, 1, 3))
        q_d = to_heads(q, dk)
        k_d = to_heads(k, dk)
        v_d = to_heads(v, dv)
        beta = jax.nn.sigmoid(hidden_states @ Wb)
        beta_d = jnp.transpose(beta, (0, 2, 1))
        o_d, S = delta_rule_chunkwise(q_d, k_d, v_d, beta_d)
        o_d = jnp.transpose(o_d, (0, 2, 1, 3))
        gamma = jax.nn.sigmoid(hidden_states @ Wdec)
        gamma_d = jnp.transpose(gamma, (0, 2, 1))
        ema_out, ema_state = ema_rule(v_d, gamma_d)
        ema_out = jnp.transpose(ema_out, (0, 2, 1, 3))
        mix = jax.nn.sigmoid(mix_inp + mix_bias)
        o = (1.0 - mix[..., None]) * o_d + mix[..., None] * ema_out
        o = rms_norm(o, rms_w)
        out = o.reshape(b, l, H * dv) @ Wo
        return out

    def _L1_ffn_ref(x, wf, uf, bf, wi, ui, bi, wc, uc, bc, wo, uo, bo, in_c):
        import jax, jax.numpy as jnp
        import numpy as np
        from jax import lax
        T, B, I, M, O = (64, 64, 256, 256, 256)

        def _xavier(key, shape):
            fan_out, fan_in = shape
            limit = float(np.sqrt(6.0 / (fan_in + fan_out)))
            return jax.random.uniform(key, shape, jnp.float32, -limit, limit)
        batch = x.shape[1]
        c0 = jnp.broadcast_to(in_c, (batch, in_c.shape[0]))

        def step(c, xt):
            ft = jax.nn.sigmoid(xt @ wf.T + c @ uf.T + bf)
            it = jax.nn.sigmoid(xt @ wi.T + c @ ui.T + bi)
            gt = jnp.tanh(xt @ wc.T + c @ uc.T + bc)
            c = ft * c + it * gt
            return (c, None)
        c_final, _ = lax.scan(step, c0, x)
        h = jnp.tanh(jnp.einsum('tbi,oi->tbo', x, wo) + c_final @ uo.T + bo)
        return h
    x = L0_attn_x
    x = x + _L0_attn_ref(_layernorm(x, axis=-1), L0_attn_W1, L0_attn_b1, L0_attn_W2, L0_attn_b2)
    x = x + _L0_ffn_ref(_layernorm(x, axis=-1), L0_ffn_w_router, L0_ffn_w1, L0_ffn_w2, L0_ffn_w3)
    x = x + _L1_attn_ref(_layernorm(x, axis=-1), L1_attn_Wq, L1_attn_Wk, L1_attn_Wv, L1_attn_conv_q, L1_attn_conv_k, L1_attn_conv_v, L1_attn_Wb, L1_attn_Wdec, L1_attn_Wmix, L1_attn_conv_mix, L1_attn_mix_bias, L1_attn_rms_w, L1_attn_Wo)
    x = x + _L1_ffn_ref(_layernorm(x, axis=-1), L1_ffn_wf, L1_ffn_uf, L1_ffn_bf, L1_ffn_wi, L1_ffn_ui, L1_ffn_bi, L1_ffn_wc, L1_ffn_uc, L1_ffn_bc, L1_ffn_wo, L1_ffn_uo, L1_ffn_bo, L1_ffn_in_c)
    return x

_drawn_inputs = setup_inputs


def setup_inputs(seed=0):
    import zlib

    import numpy as np

    out = dict(_drawn_inputs(seed))
    spreads = {'L0_attn_b1': (0.0, 0.1),
     'L0_attn_b2': (0.0, 2.0),
     'L1_attn_mix_bias': (-2.0, 0.6),
     'L1_attn_rms_w': (1.0, 0.6),
     'L1_ffn_bf': (0.0, 2.0),
     'L1_ffn_bi': (0.0, 2.0),
     'L1_ffn_bc': (0.0, 2.0),
     'L1_ffn_bo': (0.0, 2.0),
     'L1_ffn_in_c': (0.0, 2.0)}
    factors = {'L0_ffn_w_router': 32.625,
     'L0_ffn_w1': 33.973,
     'L0_ffn_w2': 29.765,
     'L0_ffn_w3': 29.719,
     'L1_attn_Wq': 64.0,
     'L1_attn_Wk': 64.0,
     'L1_attn_Wv': 64.0,
     'L1_attn_conv_q': 64.0,
     'L1_attn_conv_k': 64.0,
     'L1_attn_conv_v': 64.0,
     'L1_attn_Wb': 64.0,
     'L1_attn_Wdec': 64.0,
     'L1_attn_Wmix': 64.0,
     'L1_attn_conv_mix': 64.0,
     'L1_attn_Wo': 64.0,
     'L1_ffn_wf': 64.0,
     'L1_ffn_uf': 64.0,
     'L1_ffn_wi': 64.0,
     'L1_ffn_ui': 64.0,
     'L1_ffn_wc': 64.0,
     'L1_ffn_uc': 64.0,
     'L1_ffn_wo': 64.0,
     'L1_ffn_uo': 64.0}
    for name, (base, spread) in spreads.items():
        noise = np.random.default_rng([zlib.crc32(name.encode()), seed]).standard_normal(out[name].shape)
        drawn = base * np.exp(spread * noise) if base else spread * noise
        out[name] = jnp.asarray(drawn.astype(out[name].dtype))
    for name, factor in factors.items():
        out[name] = (out[name] * factor).astype(out[name].dtype)
    return out
```

```python
from contextlib import ExitStack

import numpy as np
import concourse.bass as bass
from concourse import mybir

F32 = mybir.dt.float32
I32 = mybir.dt.int32
U32 = mybir.dt.uint32
ALU = mybir.AluOpType
ACT = mybir.ActivationFunctionType
AX = mybir.AxisListType

P = 128
T = 4096
D = 256
NT = T // P
KD = D // P
EPS = 1e-5

NH0 = 16
E = 8
HID = 352
HB = [(0, 128), (128, 128), (256, 96)]
SLOT_TILES = 2 * T // P + E - 1
SLOTS = SLOT_TILES * P
NH1 = 4
DH = 64


def wait(eng, sem, value, cap=None):
    if isinstance(value, int):
        if cap is not None:
            value = min(value, cap)
        if value <= 0:
            return
    eng.wait_ge(sem, value)


def wait_apart(eng, loaded, sem, value, cap=None):
    if not isinstance(value, int):
        eng.to_reg(value)
        eng.wait_ge(loaded, 16)
    wait(eng, sem, value, cap)


def pipelined(eng, n, depth, step, ahead=0, unroll=2):
    lo = -(-(depth + 1) // unroll) * unroll
    hi = n - ahead - (n - ahead - lo) % unroll
    for i in range(lo):
        step(i, i % unroll)
    with eng.Fori(lo // unroll, hi // unroll) as turn:
        for k in range(unroll):
            step(unroll * turn + k, k)
    for i in range(hi, n + depth):
        step(i, i % unroll)


def has(t, n):
    return not isinstance(t, int) or 0 <= t < n


def tile_of(ap, t):
    return ap[:, bass.ds(t, 1), :].rearrange("p a d -> p (a d)")


def linear_attention(nc, x_res, xn2_res, logits, w13, w2, x_slots, w):
    with ExitStack() as ctx:
        def sb(name, shape, dt=F32):
            return ctx.enter_context(nc.sbuf_tensor(name, shape, dt))

        def psum(name, shape):
            return ctx.enter_context(nc.psum_tensor(name, shape, F32))

        def sem(name):
            return ctx.enter_context(nc.semaphore(name))

        w_qk = sb("w_qk", [P, KD, 512])
        w_kv = sb("w_kv", [P, KD, 512])
        w_o = sb("w_o", [P, KD, D])
        w_r = sb("w_r", [P, KD, E])
        b_qk = sb("b_qk", [P, 4])
        b_kv = sb("b_kv", [P, 512])
        b_o = sb("b_o", [P, D])
        ident = sb("ident0", [P, P])
        causal = sb("causal0", [P, P])
        eo_mask = sb("eo_mask", [P, 2])
        head_mask = sb("head_mask", [P, P])

        half = sb("a_half", [P, 1])
        loaded = sem("a_loaded")
        ln1_stats = sb("ln1_stats", [P, 2, 6])
        ln1_moments = sb("ln1_moments", [P, 2, 2])
        ln1_shifted = sb("ln1_shifted", [P, 2, 1])
        ln1_rstd = sb("ln1_rstd", [P, 2, 1])
        ln1_stats_done = sem("ln1_stats_done")
        ln1_moments_done = sem("ln1_moments_done")
        ln1_shifted_done = sem("ln1_shifted_done")
        ln1_rstd_done = sem("ln1_rstd_done")
        ln1_done = sem("ln1_done")
        ln2_stats = sb("ln2_stats", [P, 2, 6])
        ln2_moments = sb("ln2_moments", [P, 2, 2])
        ln2_shifted = sb("ln2_shifted", [P, 2, 1])
        ln2_rstd = sb("ln2_rstd", [P, 2, 1])
        ln2_stats_done = sem("ln2_stats_done")
        ln2_moments_done = sem("ln2_moments_done")
        ln2_shifted_done = sem("ln2_shifted_done")
        ln2_rstd_done = sem("ln2_rstd_done")
        ln2_done = sem("ln2_done")
        xn = sb("a_xn", [P, 2, D])
        xnT = sb("a_xnT", [P, 2, KD, P])
        qkT = sb("a_qkT", [P, 2, 4, P])
        qeo = sb("a_qeo", [P, 2, 2, 2, P])
        k_tok = sb("a_ktok", [P, 2, D])
        vpad = sb("a_vpad", [P, 2, 8, 2, 32])
        stm = sb("a_stm", [P, 16, P])
        s_bd = sb("a_sbd", [P, 2, 2, P])
        oT = sb("a_oT", [P, 2, KD, P])
        xn2 = sb("a_xn2", [P, 2, D])
        xn2T = sb("a_xn2T", [P, 2, KD, P])

        ps_sc = psum("ps_sc", [P, 2048])
        ps_qk = psum("ps_qk", [P, 512])
        ps_kv = psum("ps_kv", [P, 512])
        ps_t = psum("ps_t", [P, 512])
        ps_s = psum("ps_s", [P, 512])
        ps_oo = ps_qk[:, 0:256].rearrange("p (h q) -> p h q", h=2)
        ps_y = ps_kv[:, 0:256]
        ps_lg = ps_kv[:, 256:256 + E]
        ps_tn = ps_t[:, 0:256].rearrange("p (k t) -> p k t", k=KD)
        ps_t2 = ps_t[:, 256:512].rearrange("p (k t) -> p k t", k=KD)

        x_in = sem("a_x_in")
        x_rest_in = sem("a_x_rest_in")
        zeroed = sem("a_zeroed")
        zeros = sb("a_zeros", [P, 8 * D])
        early = sem("a_early")
        t1_done = sem("a_t1")
        t1_out = sem("a_t1o")
        qk_done = sem("a_qk")
        kv_done = sem("a_kv")
        qk_out = sem("a_qko")
        kv_out = sem("a_kvo")
        qeo_done = sem("a_qeo_s")
        sc_done = sem("a_sc")
        st_done = sem("a_st")
        s_out = sem("a_so")
        stm_done = sem("a_stm_s")
        av_done = sem("a_av")
        o_out = sem("a_oo")
        y_done = sem("a_y")
        res_done = sem("a_res")
        xb_done = sem("a_xb")
        kept = sem("a_kept")
        t2_done = sem("a_t2")
        t2_out = sem("a_t2o")
        lg_done = sem("a_lg")
        lg_out = sem("a_lgo")
        block = ctx.enter_context(nc.Block())
        DEPTH = 6
        N_LOADS = 13

        @block.sync
        def _(sp):
            for c in range(8):
                sp.dma_start(x_res[:, 4 * c:4 * c + 4, :],
                             w["x"].rearrange("(t p) d -> p t d", p=P)[:, 4 * c:4 * c + 4, :]).then_inc(x_rest_in if c else x_in, 16)
                if c == 0:
                    w1 = w["W1"].rearrange("(k p) n -> p k n", p=P)
                    sp.dma_start(ident[:, :], w["c_ident"]).then_inc(loaded, 16)
                    sp.dma_start(w_qk[:, :, 0:256], w1[:, :, 256:512]).then_inc(loaded, 16)
                    sp.dma_start(w_qk[:, :, 256:512], w1[:, :, 0:256]).then_inc(loaded, 16)
                    sp.dma_start(w_kv[:, :, 0:256], w1[:, :, 0:256]).then_inc(loaded, 16)
                    sp.dma_start(w_kv[:, :, 256:512], w1[:, :, 512:768]).then_inc(loaded, 16)
                    sp.dma_start(b_qk[:, :], w["b_qk"]).then_inc(loaded, 16)
                    sp.dma_start(b_kv[:, :], w["b_kv"].partition_broadcast(P)).then_inc(loaded, 16)
                    sp.dma_start(b_o[:, :], w["b2"].partition_broadcast(P)).then_inc(loaded, 16)
                    sp.dma_start(w_o[:, :, :], w["W2"].rearrange("(k p) n -> p k n", p=P)).then_inc(loaded, 16)
                    sp.dma_start(w_r[:, :, :], w["w_rT"].rearrange("(k p) n -> p k n", p=P)).then_inc(loaded, 16)
                    sp.dma_start(causal[:, :], w["c_causal"]).then_inc(loaded, 16)
                    sp.dma_start(eo_mask[:, :], w["c_eo"]).then_inc(loaded, 16)
                    sp.dma_start(head_mask[:, :], w["c_head"]).then_inc(loaded, 16)

            n = load_experts(sp, w13, w2, w, early)
            sp.wait_ge(zeroed, 4)
            n += zero_slots(sp, zeros, x_slots, early)
            sp.wait_ge(early, n)

        @block.gpsimd
        def _(pool):
            pool.memset(zeros[:, :], 0.0).then_inc(zeroed, 1)
            pool.memset(half[:, :], -0.5).then_inc(zeroed, 1)
            pool.memset(vpad[:, :, :, :, :], 0.0).then_inc(zeroed, 1)
            pool.memset(s_bd[:, :, :, :], 0.0).then_inc(zeroed, 1)
            pool.wait_ge(loaded, 16 * N_LOADS)
            pool.wait_ge(zeroed, 4)

            def step(i, par):
                t, q = i - 5, (par - 5) % 2
                if has(t, NT):
                    wait_apart(pool, loaded, ln2_moments_done, t + 1)
                    wait_apart(pool, loaded, ln2_done, t - 1)
                    pool.tensor_scalar(ln2_shifted[:, q, :], ln2_moments[:, q, 1:2], EPS, None,
                                       ALU.add).then_inc(ln2_shifted_done, 1)
                    wait_apart(pool, loaded, ln2_shifted_done, t + 1)
                    pool.tensor_tensor(ln2_rstd[:, q, :], ln2_shifted[:, q, :], half[:, :], ALU.pow).then_inc(ln2_rstd_done, 1)
                t, q = i, par
                if has(t, NT):
                    wait_apart(pool, loaded, ln1_moments_done, t + 1)
                    wait_apart(pool, loaded, ln1_done, t - 1)
                    pool.tensor_scalar(ln1_shifted[:, q, :], ln1_moments[:, q, 1:2], EPS, None,
                                       ALU.add).then_inc(ln1_shifted_done, 1)
                    wait_apart(pool, loaded, ln1_shifted_done, t + 1)
                    pool.tensor_tensor(ln1_rstd[:, q, :], ln1_shifted[:, q, :], half[:, :], ALU.pow).then_inc(ln1_rstd_done, 1)
                t = i - 1
                if has(t, NT):
                    wait_apart(pool, loaded, ln1_done, t + 1)
                    pool.tensor_tensor(tile_of(x_res, t), tile_of(x_res, t), b_o[:, :], ALU.add).then_inc(xb_done, 1)
                t, q = i - 2, (par - 2) % 2
                if has(t, NT):
                    wait_apart(pool, loaded, qk_out, t + 1)
                    wait_apart(pool, loaded, sc_done, t - 1)
                    pool.tensor_tensor(qeo[:, q], qkT[:, q, 0:2, :].unsqueeze(2).broadcast_to([P, 2, 2, P]),
                                       eo_mask[:, :].unsqueeze(1).unsqueeze(3).broadcast_to([P, 2, 2, P]),
                                       ALU.mult).then_inc(qeo_done, 1)
                t, q = i - 6, (par - 6) % 2
                if has(t, NT):
                    wait_apart(pool, loaded, ln2_done, t + 1)
                    pool.tensor_copy(tile_of(xn2_res, t), xn2[:, q, :]).then_inc(kept, 1)

            pipelined(pool, NT, DEPTH, step)

        @block.scalar
        def _(act):
            def step(i, par):
                t, q = i - 4, (par - 4) % 2
                if has(t, NT):
                    wait(act, av_done, t + 1)
                    wait(act, y_done, t - 1)
                    act.activation(oT[:, q], ps_oo, ACT.Copy).then_inc(o_out, 1)
                t, q = i - 6, (par - 6) % 2
                if has(t, NT):
                    wait(act, t2_done, t + 1)
                    wait(act, lg_done, t - 1)
                    act.activation(xn2T[:, q], ps_t2, ACT.Copy).then_inc(t2_out, 1)
                t, q = i - 1, (par - 1) % 2
                if has(t, NT):
                    wait(act, t1_done, t + 1)
                    wait(act, kv_done, t - 1)
                    act.activation(xnT[:, q], ps_tn, ACT.Copy).then_inc(t1_out, 1)
                t = i - 6
                if has(t, NT):
                    wait(act, lg_done, t + 1)
                    act.activation(tile_of(logits, t), ps_lg, ACT.Copy).then_inc(lg_out, 1)

            pipelined(act, NT, DEPTH, step)

        @block.vector
        def _(dve):
            dve.wait_ge(loaded, 16 * N_LOADS)
            dve.wait_ge(zeroed, 4)

            def step(i, par):
                t, q = i - 5, (par - 5) % 2
                if has(t, NT):
                    wait(dve, y_done, t + 1)
                    wait(dve, xb_done, t + 1)
                    dve.tensor_tensor(tile_of(x_res, t), tile_of(x_res, t), ps_y, ALU.add).then_inc(res_done, 1)
                    wait_apart(dve, loaded, res_done, t + 1)
                    wait_apart(dve, loaded, ln2_done, t - 1)
                    dve.bn_stats(ln2_stats[:, q, :], tile_of(x_res, t)).then_inc(ln2_stats_done, 1)
                    wait_apart(dve, loaded, ln2_stats_done, t + 1)
                    dve.bn_aggr(ln2_moments[:, q, :], ln2_stats[:, q, :]).then_inc(ln2_moments_done, 1)
                t, q = i, par
                if has(t, NT):
                    if isinstance(t, int) and t == 0:
                        wait(dve, x_in, 16)
                    if isinstance(t, int) and t == 4:
                        wait(dve, x_rest_in, 16 * 7)
                    wait_apart(dve, loaded, ln1_done, t - 1)
                    dve.bn_stats(ln1_stats[:, q, :], tile_of(x_res, t)).then_inc(ln1_stats_done, 1)
                    wait_apart(dve, loaded, ln1_stats_done, t + 1)
                    dve.bn_aggr(ln1_moments[:, q, :], ln1_stats[:, q, :]).then_inc(ln1_moments_done, 1)
                t, q = i - 3, (par - 3) % 2
                if has(t, NT):
                    wait(dve, st_done, t + 1)
                    wait(dve, av_done, t)
                    dve.tensor_tensor(s_bd[:, q], ps_s[:, 0:256].rearrange("p (h c) -> p h c", h=2),
                                      head_mask[:, :].unsqueeze(1).broadcast_to([P, 2, P]), ALU.mult).then_inc(s_out, 1)
                    wait(dve, sc_done, t + 1)
                    dve.tensor_tensor(stm[:, :, :], ps_sc[:, :].rearrange("p (h q) -> p h q", h=16),
                                      causal[:, :].unsqueeze(1).broadcast_to([P, 16, P]), ALU.mult).then_inc(stm_done, 1)
                t, q = i, par
                if has(t, NT):
                    wait(dve, t1_done, t - 1)
                    wait(dve, ln1_rstd_done, t + 1)
                    dve.tensor_scalar(xn[:, q, :], tile_of(x_res, t), ln1_moments[:, q, 0:1], ln1_rstd[:, q, :], ALU.subtract,
                                      ALU.mult).then_inc(ln1_done, 1)
                t, q = i - 5, (par - 5) % 2
                if has(t, NT):
                    wait(dve, t2_done, t - 1)
                    wait(dve, kept, t - 1)
                    wait(dve, ln2_rstd_done, t + 1)
                    dve.tensor_scalar(xn2[:, q, :], tile_of(x_res, t), ln2_moments[:, q, 0:1], ln2_rstd[:, q, :], ALU.subtract,
                                      ALU.mult).then_inc(ln2_done, 1)
                t, q = i - 2, (par - 2) % 2
                if has(t, NT):
                    wait(dve, qk_done, t + 1)
                    wait(dve, av_done, t - 1)
                    wait(dve, qeo_done, t - 1)
                    dve.tensor_tensor(qkT[:, q], ps_qk[:, :].rearrange("p (b t) -> p b t", b=4),
                                      b_qk[:, :].unsqueeze(2).broadcast_to([P, 4, P]), ALU.add).then_inc(qk_out, 1)
                    wait(dve, kv_done, t + 1)
                    dve.tensor_tensor(k_tok[:, q, :], ps_kv[:, 0:256], b_kv[:, 0:256], ALU.add).then_inc(kv_out, 1)
                    for eo in range(2):
                        def part(ap):
                            return ap.rearrange("p (r e d) -> p r e d", e=2, d=16)[:, :, eo, :]
                        dve.tensor_tensor(vpad[:, q, :, eo, 16 * eo:16 * eo + 16], part(ps_kv[:, 256:512]),
                                          part(b_kv[:, 256:512]), ALU.add).then_inc(kv_out, 1)

            pipelined(dve, NT, DEPTH, step)

        @block.tensor
        def _(pe):
            pe.wait_ge(loaded, 16 * N_LOADS)
            pe.wait_ge(zeroed, 4)

            def step(i, par):
                t, q = i - 4, (par - 4) % 2
                if has(t, NT):
                    wait(pe, stm_done, t + 1)
                    wait(pe, kv_out, 3 * (t + 1))
                    wait(pe, s_out, t)
                    wait(pe, qk_out, t + 2, NT)
                    for h in range(2):
                        pe.matmul(ps_oo[:, h, :], s_bd[:, (q + 1) % 2, h, :], qkT[:, q, h, :], start=(h == 0),
                                  stop=False, skip_group_check=True)
                    for h in range(2):
                        for g in range(4):
                            for eo in range(2):
                                mm = pe.matmul(ps_oo[32 * g:32 * g + 32, h, :], vpad[:, q, 4 * h + g, eo, :],
                                               stm[:, 4 * g + 2 * h + eo, :], start=False,
                                               stop=(eo == 1), skip_group_check=True)
                    mm.then_inc(av_done, 1)
                t, q = i - 5, (par - 5) % 2
                if has(t, NT):
                    wait(pe, o_out, t + 1)
                    wait(pe, kv_out, 3 * (t + 3), 3 * NT)
                    wait(pe, lg_out, t - 1)
                    for k in range(KD):
                        mm = pe.matmul(ps_y, oT[:, q, k, :], w_o[:, k, :], start=(k == 0), stop=(k == KD - 1))
                    mm.then_inc(y_done, 1)
                t, q = i - 6, (par - 6) % 2
                if has(t, NT):
                    wait(pe, ln2_done, t + 1)
                    wait(pe, t1_out, t + 5, NT)
                    for k in range(KD):
                        mm = pe.transpose(ps_t2[:, k, :], xn2[:, q, k * P:(k + 1) * P], ident[:, :])
                    mm.then_inc(t2_done, 1)
                t, q = i - 3, (par - 3) % 2
                if has(t, NT):
                    wait(pe, kv_out, 3 * (t + 1))
                    wait(pe, s_out, t)
                    for h in range(2):
                        mm = None
                        for eo in range(2):
                            out = ps_s[:, h * P:(h + 1) * P].rearrange("p (r e d) -> p r e d", e=2, d=16)[:, :, eo, :]
                            mm = pe.matmul(out, k_tok[:, q, h * P:(h + 1) * P],
                                           vpad[:, q, 4 * h:4 * h + 4, eo, 16 * eo:16 * eo + 16],
                                           start=(isinstance(t, int) and t == 0 and h == 0 and eo == 0),
                                           stop=True, skip_group_check=True)
                    mm.then_inc(st_done, 1)
                    wait(pe, qeo_done, t + 1)
                    wait(pe, stm_done, t)
                    for h in range(2):
                        for g in range(4):
                            r = slice(32 * g, 32 * g + 32)
                            mm = pe.matmul(ps_sc[:, 512 * g + 256 * h:512 * g + 256 * h + 256], qkT[r, q, 2 + h, :],
                                           qeo[r, q, h].rearrange("p e q -> p (e q)"), start=True, stop=True)
                    mm.then_inc(sc_done, 1)

                t, q = i - 1, (par - 1) % 2
                if has(t, NT):
                    wait(pe, ln1_done, t + 1)
                    wait(pe, t1_out, t)
                    wait(pe, t2_out, t - 4)
                    for k in range(KD):
                        mm = pe.transpose(ps_tn[:, k, :], xn[:, q, k * P:(k + 1) * P], ident[:, :])
                    mm.then_inc(t1_done, 1)
                t, q = i - 6, (par - 6) % 2
                if has(t, NT):
                    wait(pe, t2_out, t + 1)
                    wait(pe, res_done, t + 2, NT)
                    for k in range(KD):
                        mm = pe.matmul(ps_lg, xn2T[:, q, k, :], w_r[:, k, :], start=(k == 0), stop=(k == KD - 1))
                    mm.then_inc(lg_done, 1)
                t, q = i - 2, (par - 2) % 2
                if has(t, NT):
                    wait(pe, t1_out, t + 1)
                    wait(pe, o_out, t - 1)
                    for b in range(4):
                        for k in range(KD):
                            mm = pe.matmul(ps_qk[:, b * P:(b + 1) * P], w_qk[:, k, b * P:(b + 1) * P],
                                           xnT[:, q, k, :], start=(k == 0), stop=(k == KD - 1))
                    mm.then_inc(qk_done, 1)
                    wait(pe, res_done, t - 2)
                    wait(pe, lg_out, t - 3)
                    for k in range(KD):
                        mm = pe.matmul(ps_kv[:, :], xnT[:, q, k, :], w_kv[:, k, :], start=(k == 0), stop=(k == KD - 1))
                    mm.then_inc(kv_done, 1)
            pipelined(pe, NT, DEPTH, step)


def zero_slots(sp, zeros, x_slots, sem):
    for c in range(0, SLOT_TILES, 8):
        n = min(8, SLOT_TILES - c)
        sp.dma_start(x_slots.rearrange("(t p) d -> p t d", p=P)[:, c:c + n, :],
                     zeros[:, 0:n * D].rearrange("p (t d) -> p t d", d=D)).then_inc(sem, 16)
    return 16 * len(range(0, SLOT_TILES, 8))


def load_experts(sp, w13, w2, w, sem):
    for k in range(KD):
        for s, name in enumerate(("w1", "w3")):
            sp.dma_start(w13[:, s, k], w[name].rearrange("e (k p) h -> k p e h", p=P)[k]).then_inc(sem, 16)
    for b, (at, n) in enumerate(HB):
        sp.dma_start(w2[0:n, b], w["w2"][:, at:at + n, :].rearrange("e p d -> p e d")).then_inc(sem, 16)
    return 16 * 7


def route(nc, xn2_res, logits, gates, slots, tile_expert, x_slots, w):
    with ExitStack() as ctx:
        def sb(name, shape, dt=F32):
            return ctx.enter_context(nc.sbuf_tensor(name, shape, dt))

        def sem(name):
            return ctx.enter_context(nc.semaphore(name))

        NS = SLOT_TILES
        strict = sb("r_strict", [P, P])
        ones = sb("r_ones", [P, P])
        prio = sb("r_prio", [P, E])
        follows = sb("r_follows", [P, E, NT])
        edges = sb("r_edges", [P, NT])
        numbers = sb("r_numbers", [P, NS])
        top = sb("r_top", [P, NT])
        p = sb("r_p", [P, NT, E])
        inv = sb("r_inv", [P, NT])
        cand = sb("r_cand", [P, NT, E])
        hot = sb("r_hot", [P, 2, NT, E])
        both = sb("r_both", [P, NT, E])
        tot = sb("r_tot", [P, E, NT])
        incl = sb("r_incl", [P, E, NT])
        full = sb("r_full", [P, E, NT])
        tiles = sb("r_tiles", [P, E])
        ends = sb("r_ends", [P, E])
        place = sb("r_place", [P, NT, E])
        posf = sb("r_posf", [P, 2, NT])
        past = sb("r_past", [P, NS, E])
        tef = sb("r_tef", [P, NS])
        ps = ctx.enter_context(nc.psum_tensor("r_ps", [P, 512], F32))

        loaded = sem("r_loaded")
        shifted = sem("r_shifted")
        exped = sem("r_exped")
        chosen = sem("r_chosen")
        counted = sem("r_counted")
        own = sem("r_own")
        placed = sem("r_placed")
        sent = sem("r_sent")
        block = ctx.enter_context(nc.Block())

        @block.sync
        def _(sp):
            sp.dma_start(strict[:, :], w["c_strict"]).then_inc(loaded, 16)
            sp.dma_start(ones[:, :], w["c_ones"]).then_inc(loaded, 16)
            sp.dma_start(prio[:, :], w["c_prio"].partition_broadcast(P)).then_inc(loaded, 16)
            sp.dma_start(follows[:, :, :], w["c_follows"].partition_broadcast(P)).then_inc(loaded, 16)
            sp.dma_start(edges[:, :], w["c_edges"].partition_broadcast(P)).then_inc(loaded, 16)
            sp.dma_start(numbers[:, :], w["c_numbers"].partition_broadcast(P)).then_inc(loaded, 16)

        @block.scalar
        def _(act):
            act.wait_ge(shifted, 1)
            act.activation(p[:, :, :], p[:, :, :], ACT.Exp).then_inc(exped, 1)

        @block.tensor
        def _(pe):
            pe.wait_ge(loaded, 96)
            pe.wait_ge(chosen, 1)
            pe.matmul(ps[:, 0:NT * E], strict[:, :], both[:, :, :].rearrange("p t e -> p (t e)"), start=True, stop=True)
            pe.matmul(ps[:, 256:256 + NT * E], ones[:, :], both[:, :, :].rearrange("p t e -> p (t e)"), start=True,
                      stop=True).then_inc(counted, 1)

        @block.vector
        def _(dve):
            count = [0]

            def link(instruction):
                count[0] += 1
                instruction.then_inc(own, 1)
                dve.wait_ge(own, count[0])

            def wide(ap):
                return ap.unsqueeze(2).broadcast_to([P, NT, E])

            dve.wait_ge(loaded, 96)
            link(dve.tensor_reduce(top[:, :], logits[:, :, :], AX.X, ALU.max))
            dve.tensor_tensor(p[:, :, :], logits[:, :, :], wide(top[:, :]), ALU.subtract).then_inc(shifted, 1)
            dve.wait_ge(exped, 1)
            link(dve.tensor_reduce(inv[:, :], p[:, :, :], AX.X, ALU.add))
            link(dve.reciprocal(inv[:, :], inv[:, :]))
            link(dve.tensor_tensor(p[:, :, :], p[:, :, :], wide(inv[:, :]), ALU.mult))
            for s in range(2):
                gate = gates[:, s, :]
                link(dve.tensor_reduce(gate, p[:, :, :], AX.X, ALU.max))
                link(dve.tensor_tensor(cand[:, :, :], p[:, :, :], wide(gate), ALU.is_equal))
                link(dve.tensor_tensor(cand[:, :, :], cand[:, :, :], prio[:, :].unsqueeze(1).broadcast_to([P, NT, E]),
                                       ALU.mult))
                link(dve.tensor_reduce(top[:, :], cand[:, :, :], AX.X, ALU.max))
                link(dve.tensor_tensor(hot[:, s], cand[:, :, :], wide(top[:, :]), ALU.is_equal))
                if s == 0:
                    link(dve.scalar_tensor_tensor(p[:, :, :], hot[:, 0], -2.0, p[:, :, :], ALU.mult, ALU.add))
            dve.tensor_tensor(both[:, :, :], hot[:, 0], hot[:, 1], ALU.add).then_inc(chosen, 1)

            dve.wait_ge(counted, 1)
            link(dve.tensor_copy(tot[:, :, :].rearrange("p e t -> p t e"),
                                 ps[:, 256:512].rearrange("p (t e) -> p t e", e=E)))
            flat = [x[:, :, :].rearrange("p e t -> p (e t)") for x in (incl, follows, tot)]
            link(dve.tensor_tensor_scan(flat[0], flat[1], flat[2], 0.0, ALU.mult, ALU.add))
            link(dve.tensor_tensor(full[:, :, :], incl[:, :, NT - 1:NT].broadcast_to([P, E, NT]),
                                   edges[:, :].unsqueeze(1).broadcast_to([P, E, NT]), ALU.is_gt))
            link(dve.tensor_reduce(tiles[:, :], full[:, :, :], AX.X, ALU.add))
            link(dve.tensor_tensor_scan(ends[:, :], ones[:, 0:E], tiles[:, :], 0.0, ALU.mult, ALU.add))
            link(dve.tensor_tensor(tiles[:, :], ends[:, :], tiles[:, :], ALU.subtract))
            link(dve.tensor_tensor(incl[:, :, :], incl[:, :, :], tot[:, :, :], ALU.subtract))
            link(dve.scalar_tensor_tensor(incl[:, :, :], tiles[:, :].unsqueeze(2).broadcast_to([P, E, NT]), float(P),
                                          incl[:, :, :], ALU.mult, ALU.add))
            link(dve.tensor_tensor(place[:, :, :], ps[:, 0:256].rearrange("p (t e) -> p t e", e=E),
                                   incl[:, :, :].rearrange("p e t -> p t e"), ALU.add))
            for s in range(2):
                link(dve.tensor_tensor(cand[:, :, :], place[:, :, :], hot[:, s], ALU.mult))
                link(dve.tensor_reduce(posf[:, s, :], cand[:, :, :], AX.X, ALU.add))
            dve.tensor_copy(slots[:, :, :], posf[:, :, :]).then_inc(placed, 1)
            link(dve.tensor_tensor(past[:, :, :], numbers[:, :].unsqueeze(2).broadcast_to([P, NS, E]),
                                   ends[:, :].unsqueeze(1).broadcast_to([P, NS, E]), ALU.is_ge))
            link(dve.tensor_reduce(tef[:, :], past[:, :, :], AX.X, ALU.add))
            link(dve.tensor_scalar(tef[:, :], tef[:, :], float(E - 1), None, ALU.min))
            link(dve.tensor_copy(tile_expert[:, :], tef[:, :]))

        @block.gpsimd
        def _(pool):
            pool.wait_ge(placed, 1)
            for t in range(NT):
                for s in range(2):
                    pool.indirect_dma_start(
                        out=x_slots, out_offset=bass.IndirectOffsetOnAxis(ap=slots[:, s, t:t + 1], axis=0),
                        in_=xn2_res[:, t, :], in_offset=None).then_inc(sent, 16)
            pool.wait_ge(sent, 16 * 2 * NT)


def experts(nc, tile_expert, x_slots, y_slots, w13, w2, w):
    with ExitStack() as ctx:
        def sb(name, shape, dt=F32):
            return ctx.enter_context(nc.sbuf_tensor(name, shape, dt))

        def psum(name):
            return ctx.enter_context(nc.psum_tensor(name, [P, 512], F32))

        def sem(name):
            return ctx.enter_context(nc.semaphore(name))

        ident = sb("e_ident", [P, P])
        x = sb("e_x", [P, 2, D])
        xT = sb("e_xT", [P, 2, KD, P])
        gate = sb("e_gate", [P, 2, HID])
        h = sb("e_h", [P, 2, 3 * P])
        hT = sb("e_hT", [P, 2, 3, P])
        y = sb("e_y", [P, 2, D])
        ps_x = psum("e_ps_x")
        ps_1 = [psum(f"e_ps_1{i}") for i in range(2)]
        ps_3 = [psum(f"e_ps_3{i}") for i in range(2)]
        ps_h = psum("e_ps_h")
        ps_y = psum("e_ps_y")
        loaded = sem("e_loaded")
        zeroed = sem("e_zeroed")
        x_in = [sem(f"e_x_in{i}") for i in range(2)]
        xt_done = sem("e_xt_done")
        xt_out = sem("e_xt_out")
        h_done = sem("e_h_done")
        gate_done = sem("e_gate_done")
        h_out = sem("e_h_out")
        ht_done = sem("e_ht_done")
        ht_out = sem("e_ht_out")
        y_done = sem("e_y_done")
        y_out = sem("e_y_out")
        y_sent = [sem(f"e_y_sent{i}") for i in range(2)]
        block = ctx.enter_context(nc.Block())
        N = SLOT_TILES
        DEPTH = 4

        def rows(ap, t):
            return ap[bass.ds(t * P, P), :]

        def nth(t, q):
            return (t - q) // 2 if isinstance(t, int) else None

        @block.sync
        def _(sp):
            sp.dma_start(ident[:, :], w["c_ident"]).then_inc(loaded, 16)

            def step(i, par):
                t, q = i, par
                if has(t, N):
                    wait_apart(sp, loaded, xt_done, t - 1)
                    sp.dma_start(x[:, q, :], rows(x_slots, t)).then_inc(x_in[q], 16)

            pipelined(sp, N, DEPTH, step)

        @block.gpsimd
        def _(pool):
            pool.memset(h[:, :, :], 0.0).then_inc(zeroed, 1)

            def step(i, par):
                t, q = i - 4, par
                if has(t, N):
                    wait_apart(pool, loaded, y_out, t + 1)
                    pool.dma_start(rows(y_slots, t), y[:, q, :]).then_inc(y_sent[q], 16)

            pipelined(pool, N, DEPTH, step)
            for q in range(2):
                pool.wait_ge(y_sent[q], 16 * ((N + 1 - q) // 2))

        @block.scalar
        def _(act):
            def step(i, par):
                t, q = i - 4, par
                if has(t, N):
                    wait(act, y_done, t + 1)
                    wait(act, y_sent[q], 8 * (t - q))
                    act.activation(y[:, q, :], ps_y[:, 0:D], ACT.Copy).then_inc(y_out, 1)
                t, q = i - 1, 1 - par
                if has(t, N):
                    wait(act, xt_done, t + 1)
                    wait(act, h_done, t - 1)
                    act.activation(xT[:, q], ps_x[:, 0:D].rearrange("p (k t) -> p k t", k=KD),
                                   ACT.Copy).then_inc(xt_out, 1)
                t, q = i - 2, par
                if has(t, N):
                    wait(act, h_done, t + 1)
                    wait(act, h_out, t - 1)
                    act.activation(gate[:, q, :], ps_1[q][:, 0:HID], ACT.Silu).then_inc(gate_done, 1)

            pipelined(act, N, DEPTH, step)

        @block.vector
        def _(dve):
            dve.wait_ge(zeroed, 1)

            def step(i, par):
                t, q = i - 3, 1 - par
                if has(t, N):
                    wait(dve, ht_done, t + 1)
                    wait(dve, y_done, t - 1)
                    dve.tensor_copy(hT[:, q], ps_h[:, 0:3 * P].rearrange("p (b t) -> p b t", b=3)).then_inc(ht_out, 1)
                t, q = i - 2, par
                if has(t, N):
                    wait(dve, gate_done, t + 1)
                    wait(dve, ht_done, t - 1)
                    dve.tensor_tensor(h[:, q, 0:HID], gate[:, q, :], ps_3[q][:, 0:HID], ALU.mult).then_inc(h_out, 1)

            pipelined(dve, N, DEPTH, step)

        @block.tensor
        def _(pe):
            pe.wait_ge(loaded, 16)
            pe.wait_ge(zeroed, 1)

            def expert_of(t):
                return pe.value_load(tile_expert[0:1, bass.ds(t, 1)], min_val=0, max_val=E - 1)

            def step(i, par):
                t, q = i - 4, par
                if has(t, N):
                    e = expert_of(t)
                    wait(pe, ht_out, t + 1)
                    wait(pe, y_out, t)
                    for b, (at, n) in enumerate(HB):
                        mm = pe.matmul(ps_y[:, 0:D], hT[0:n, q, b, :], w2[0:n, b, bass.ds(e, 1), :],
                                       start=(b == 0), stop=(b == 2))
                    mm.then_inc(y_done, 1)
                t, q = i - 3, 1 - par
                if has(t, N):
                    wait(pe, h_out, t + 1)
                    wait(pe, ht_out, t)
                    for b in range(3):
                        mm = pe.transpose(ps_h[:, b * P:(b + 1) * P], h[:, q, b * P:(b + 1) * P], ident[:, :])
                    mm.then_inc(ht_done, 1)
                t, q = i - 1, 1 - par
                if has(t, N):
                    wait(pe, x_in[q], 8 * (t - q) + 16)
                    wait(pe, xt_out, t)
                    for k in range(KD):
                        mm = pe.transpose(ps_x[:, k * P:(k + 1) * P], x[:, q, k * P:(k + 1) * P], ident[:, :])
                    mm.then_inc(xt_done, 1)
                t, q = i - 2, par
                if has(t, N):
                    e = expert_of(t)
                    wait(pe, xt_out, t + 1)
                    wait(pe, gate_done, t - 1)
                    wait(pe, h_out, t - 1)
                    for s, ps in enumerate((ps_1[q], ps_3[q])):
                        for k in range(KD):
                            mm = pe.matmul(ps[:, 0:HID], xT[:, q, k, :], w13[:, s, k, bass.ds(e, 1), :],
                                           start=(k == 0), stop=(k == KD - 1))
                    mm.then_inc(h_done, 1)

            pipelined(pe, N, DEPTH, step)


GROUP = 4
NG = NT // GROUP
GW = GROUP * P
CONV = 4
HIST = CONV - 1
SUB = 16
REC = 5 * D


def delta_inputs(nc, x_res, gates, slots, y_slots, small, rec, l_mat, t_mat, w):
    with ExitStack() as ctx:
        def sb(name, shape, dt=F32):
            return ctx.enter_context(nc.sbuf_tensor("d_" + name, shape, dt))

        def psum(name):
            return ctx.enter_context(nc.psum_tensor("d_" + name, [P, 512], F32))

        def sem(name):
            return ctx.enter_context(nc.semaphore("d_" + name))

        SM = 36
        w_p = sb("w_p", [P, KD, 6 * P])
        w_dec = sb("w_dec", [P, KD, NH1])
        w_g = sb("w_g", [P, KD, D])
        w_s = sb("w_s", [P, KD, SM])
        taps = sb("taps", [P, 6, CONV])
        taps_m = sb("taps_m", [NH1, CONV])
        mix_b = sb("mix_b", [P, NH1])
        ident = sb("ident", [P, P])
        half = sb("half", [P, 8])
        pair_mask = sb("pair_mask", [P, 2])

        idx = sb("idx", [P, 2, 2, GROUP], U32)
        got = sb("got", [P, 2, GROUP, 2, D])
        stats = sb("stats", [P, GROUP, 6])
        mom = sb("mom", [P, GROUP, 2])
        shifted = sb("shifted", [P, GROUP])
        rstd = sb("rstd", [P, GROUP])
        xn = sb("xn", [P, 2, GROUP, D])
        xT = sb("xT", [P, KD, GW])
        cin = sb("cin", [P, 2, 6, HIST + GW])
        cout = sb("cout", [P, 6, GW])
        act_out = sb("act_out", [P, 2, 6, GW])
        dec_t = sb("dec_t", [P, 2, GW])
        dec = sb("dec", [P, 2, GW])
        inp = sb("inp", [P, 2, GW])
        ema = sb("ema", [P, 2, 2, GW])
        min_ = sb("min", [NH1, 2, HIST + GW])
        mtmp = sb("mtmp", [NH1, GW])
        sm_row = sb("sm_row", [SM, 2, GW])
        sm_t = sb("sm_t", [P, 2, GROUP, NH1])
        sm_m = sb("sm_m", [P, GROUP, NH1])
        sq = sb("sq", [P, 2, 512])
        ss = sb("ss", [P, 2, 8])
        ss_e = sb("ss_e", [P, 2, 8])
        rn = sb("rn", [P, 2, 8])
        qkn = sb("qkn", [P, 2, 512])
        ve = sb("ve", [P, 2, 512])
        bT = sb("bT", [P, 2, 4, P])
        k_eo = sb("k_eo", [P, 2, 2, 2, P])
        l32 = sb("l32", [P, 2, NH1, 32])
        l_in = sb("l_in", [P, SUB, SUB])
        t_out = sb("t_out", [P, SUB, SUB])
        prod = sb("prod", [P, SUB, SUB])
        pp = [psum(f"pp{i}") for i in range(2)]
        ps_qk = [psum(f"ps_qk{i}") for i in range(2)]
        ps_ve = psum("ps_ve")
        ps_b = psum("ps_b")
        ps_g = [psum(f"ps_g{i}") for i in range(2)]

        loaded = sem("loaded")
        zeroed = sem("zeroed")
        spread = sem("spread")
        idx_done = sem("idx_done")
        got_in = [sem(f"got_in{i}") for i in range(2)]
        first_done = sem("first_done")
        x_done = sem("x_done")
        stats_done = sem("stats_done")
        mom_done = sem("mom_done")
        shift_done = sem("shift_done")
        rstd_done = sem("rstd_done")
        norm_done = sem("norm_done")
        p_done = sem("p_done")
        p_out = sem("p_out")
        carried = sem("carried")
        conv_own = sem("conv_own")
        conv_done = sem("conv_done")
        silu_own = sem("silu_own")
        silu_done = sem("silu_done")
        dec_done = sem("dec_done")
        inp_done = sem("inp_done")
        ema_done = sem("ema_done")
        m_own = sem("m_own")
        mix_done = sem("mix_done")
        sm_done = sem("sm_done")
        sm_out = sem("sm_out")
        sm_add = sem("sm_add")
        sm_tanh = sem("sm_tanh")
        small_done = sem("small_done")
        tt_done = sem("tt_done")
        sq_done = sem("sq_done")
        ve_out = sem("ve_out")
        ss_done = sem("ss_done")
        sse_done = sem("sse_done")
        rn_done = sem("rn_done")
        qkn_done = sem("qkn_done")
        bt_done = sem("bt_done")
        bt_out = sem("bt_out")
        eo_done = sem("eo_done")
        g_done = sem("g_done")
        g_out = sem("g_out")
        sent = [sem(f"sent{i}") for i in range(2)]
        l_sent = [sem(f"l_sent{i}") for i in range(2)]
        l_back = sem("l_back")
        sub_own = sem("sub_own")
        sub_done = sem("sub_done")
        t_sent = sem("t_sent")
        block = ctx.enter_context(nc.Block())
        DEPTH = 3
        N_LOADS = 13
        ORDER = [4, 5, "g0", "g1", "s", 0, 1, 2, 3]
        USES = 2 + len(ORDER)

        @block.sync
        def _(sp):
            for n, name in enumerate(("Wq", "Wk", "Wv")):
                sp.dma_start(w_p[:, :, n * D:(n + 1) * D], w[name].rearrange("(k p) n -> p k n", p=P)).then_inc(loaded, 16)
            sp.dma_start(w_dec[:, :, :], w["Wdec"].rearrange("(k p) n -> p k n", p=P)).then_inc(loaded, 16)
            sp.wait_ge(zeroed, 1)
            sp.dma_start(w_s[:, :, 0:NH1], w["Wmix"].rearrange("(k p) n -> p k n", p=P)).then_inc(loaded, 16)
            sp.dma_start(w_s[:, :, 32:32 + NH1], w["Wb"].rearrange("(k p) n -> p k n", p=P)).then_inc(loaded, 16)
            for n, name in enumerate(("conv_q", "conv_k", "conv_v")):
                sp.dma_start(taps[:, 2 * n:2 * n + 2, :], w[name].rearrange("(k p) n -> p k n", p=P)).then_inc(loaded, 16)
            sp.dma_start(taps_m[:, :], w["conv_mix"]).then_inc(loaded, 16)
            sp.dma_start(mix_b[:, :], w["mix_bias"].partition_broadcast(P)).then_inc(loaded, 16)
            sp.dma_start(ident[:, :], w["c_ident"]).then_inc(loaded, 16)

            sp.dma_start(pair_mask[:, :], w["c_pair"]).then_inc(loaded, 16)

            def step(i, par):
                u = i - 2
                if has(u, NG):
                    for j in range(GROUP):
                        t, q = GROUP * u + j, j % 2
                        row = rec[bass.ds(t * P, P), :]
                        wait_apart(sp, loaded, ve_out, t + 1)
                        sp.dma_start(row[:, D:3 * D], ve[:, q, :]).then_inc(sent[q], 16)
                        wait_apart(sp, loaded, qkn_done, t + 1)
                        sp.dma_start(row[:, 0:D], qkn[:, q, D:2 * D]).then_inc(sent[q], 16)
                        wait_apart(sp, loaded, bt_out, t + 1)
                        sp.dma_start(row[:, 3 * D:5 * D], bT[:, q].rearrange("p b t -> p (b t)")).then_inc(sent[q], 16)
                        wait_apart(sp, loaded, g_out, 4 * (t + 1))
                        sp.dma_start(l_mat[bass.ds(t * P, P), :], l32[:, q].rearrange("p h c -> p (h c)")).then_inc(l_sent[q], 16)
                u = i - 3
                if has(u, NG):
                    wait_apart(sp, loaded, sub_done, u + 1)
                    for s in range(2):
                        for h in range(NH1):
                            r = 64 * s + 16 * h
                            dst = t_mat[bass.ds(u * GW, GW), :].rearrange("(b s i) (h c) -> s h b i c", s=2, i=SUB, h=NH1)
                            sp.dma_start(dst[s, h], t_out[r:r + 16, :, :]).then_inc(t_sent, 16)
                u = i - 2
                if has(u, NG):
                    for q in range(2):
                        wait_apart(sp, loaded, l_sent[q], 16 * GROUP // 2 * (u + 1))
                    wait_apart(sp, loaded, sub_done, u)
                    for s in range(2):
                        for h in range(NH1):
                            r = 64 * s + 16 * h
                            src = l_mat[bass.ds(u * GW, GW), :].rearrange("(b s i) (h z c) -> s h z b i c", s=2, i=SUB, h=NH1, z=2)
                            sp.dma_start(l_in[r:r + 16, :, :], src[s, h, s]).then_inc(l_back, 16)

            pipelined(sp, NG, DEPTH, step)
            for q in range(2):
                sp.wait_ge(sent[q], 48 * NT // 2)
            sp.wait_ge(t_sent, 16 * 8 * NG)

        @block.gpsimd
        def _(pool):
            pool.memset(w_s[:, :, :], 0.0).then_inc(zeroed, 1)
            pool.memset(half[:, :], -0.5).then_inc(zeroed, 1)
            pool.memset(cin[:, :, :, 0:HIST], 0.0).then_inc(zeroed, 1)
            pool.memset(min_[:, :, 0:HIST], 0.0).then_inc(zeroed, 1)
            pool.memset(sm_row[:, :, :], 0.0).then_inc(zeroed, 1)
            pool.memset(t_out[:, :, :], 0.0).then_inc(zeroed, 1)
            pool.wait_ge(zeroed, 6)
            pool.memset(t_out[:, :, :].rearrange("p a b -> p (a b)")[:, 0:SUB * SUB:SUB + 1], 1.0).then_inc(zeroed, 1)
            pool.wait_ge(loaded, 16 * N_LOADS)
            pool.wait_ge(zeroed, 7)

            def gather(u, q, tiles):
                if tiles[0] == 0:
                    wait_apart(pool, loaded, x_done, GROUP * (u - 1))
                    pool.tensor_copy(idx[:, q], slots[:, :, bass.ds(GROUP * u, GROUP)]).then_inc(idx_done, 1)
                    wait_apart(pool, loaded, idx_done, u + 1)
                for j in tiles:
                    for s in range(2):
                        pool.indirect_dma_start(
                            out=got[:, q, j, s, :], out_offset=None, in_=y_slots,
                            in_offset=bass.IndirectOffsetOnAxis(ap=idx[:, q, s, j:j + 1], axis=0)).then_inc(got_in[q], 16)

            def root(t, q):
                wait_apart(pool, loaded, ss_done, t + 1)
                wait_apart(pool, loaded, qkn_done, t - 1)
                pool.tensor_scalar(ss_e[:, q, :], ss[:, q, :], 1e-6, None, ALU.add).then_inc(sse_done, 1)
                wait_apart(pool, loaded, sse_done, t + 1)
                pool.tensor_tensor(rn[:, q, :], ss_e[:, q, :], half[:, :], ALU.pow).then_inc(rn_done, 1)

            def even_odd(t, q):
                wait_apart(pool, loaded, bt_out, t + 1)
                wait_apart(pool, loaded, g_done, t - 1)
                for e in range(2):
                    pool.tensor_scalar(k_eo[:, q, :, e, :], bT[:, q, 2:4, :], pair_mask[:, e:e + 1], None,
                                       ALU.mult).then_inc(eo_done, 1)

            def step(i, par):
                if isinstance(i, int) and i == 0:
                    gather(0, 0, (0, 1, 2, 3))
                if has(i, NG):
                    wait_apart(pool, loaded, mom_done, GROUP * (i + 1))
                    wait_apart(pool, loaded, norm_done, GROUP * i)
                    pool.tensor_scalar(shifted[:, :], mom[:, :, 1], EPS, None, ALU.add).then_inc(shift_done, 1)
                    wait_apart(pool, loaded, shift_done, i + 1)
                    pool.tensor_tensor(rstd[:, :], shifted[:, :], half[:, 0:GROUP], ALU.pow).then_inc(rstd_done, 1)
                t, q = GROUP * (i - 2), (par - 2) % 2
                tiles = has(i - 2, NG)
                if tiles:
                    root(t, 0)
                    root(t + 1, 1)
                    even_odd(t, 0)
                u, q = i - 1, (par - 1) % 2
                if has(i + 1, NG):
                    gather(i + 1, 1 - par, (0, 1))
                if has(u, NG):
                    wait_apart(pool, loaded, p_out, USES * u + 2 + 5)
                    wait_apart(pool, loaded, mix_done, u)
                    wait_apart(pool, loaded, ema_done, 2 * u)
                    pool.tensor_scalar(dec[:, :, :], dec_t[:, :, :], 0.5, 0.5, ALU.mult, ALU.add).then_inc(dec_done, 1)
                    pool.tensor_scalar(inp[:, :, :], dec_t[:, :, :], -0.5, 0.5, ALU.mult, ALU.add).then_inc(dec_done, 1)
                if tiles:
                    root(t + 2, 0)
                    even_odd(t + 1, 1)
                if has(i + 1, NG):
                    gather(i + 1, 1 - par, (2, 3))
                if has(u, NG):
                    m_in, m_out, m_one = min_[:, q], sm_row[0:NH1, q, :], mtmp[:, :]
                    wait_apart(pool, loaded, sm_done, u - 1)
                    pool.tensor_scalar(m_out, m_in[:, 0:GW], taps_m[:, 0:1], None, ALU.mult).then_inc(m_own, 1)
                    for c in range(1, CONV):
                        wait_apart(pool, loaded, m_own, 7 * u + 2 * c - 1)
                        pool.tensor_scalar(m_one, m_in[:, c:c + GW], taps_m[:, c:c + 1], None, ALU.mult).then_inc(m_own, 1)
                        wait_apart(pool, loaded, m_own, 7 * u + 2 * c)
                        pool.tensor_tensor(m_out, m_out, m_one, ALU.add).then_inc(m_own, 1)
                    wait_apart(pool, loaded, m_own, 7 * u + 7)
                    pool.tensor_copy(min_[:, 1 - q, 0:HIST], m_in[:, GW:GW + HIST]).then_inc(mix_done, 1)
                if tiles:
                    root(t + 3, 1)
                    even_odd(t + 2, 0)
                    even_odd(t + 3, 1)
                if has(u, NG):
                    wait_apart(pool, loaded, p_out, USES * (u + 1))
                    wait_apart(pool, loaded, conv_done, 6 * u)
                    pool.tensor_copy(cin[:, 1 - q, :, 0:HIST], cin[:, q, :, GW:GW + HIST]).then_inc(carried, 1)

            pipelined(pool, NG, DEPTH, step, ahead=1)

        @block.scalar
        def _(act):
            act.wait_ge(loaded, 16 * N_LOADS)

            def step(i, par):
                u, q = i - 1, (par - 1) % 2
                here = has(u, NG)
                v, r = i - 2, (par - 2) % 2
                tiles = has(v, NG)

                def use(n):
                    bank = pp[n % 2]
                    wait(act, p_done, USES * u + n + 1)
                    if n < 2:
                        wait(act, p_done, USES * u)
                        act.activation(xT[:, n, :], bank[:, :], ACT.Copy).then_inc(p_out, 1)
                        return
                    what = ORDER[n - 2]
                    if what == "s":
                        wait(act, sm_done, u - 1)
                        wait(act, mix_done, u)
                        act.activation(sm_row[32:SM, q, :], bank[32:SM, :], ACT.Copy)
                        act.activation(min_[:, q, HIST:], bank[0:NH1, :], ACT.Copy).then_inc(p_out, 1)
                    elif isinstance(what, str):
                        wait(act, dec_done, 2 * u)
                        act.activation(dec_t[:, int(what[1]), :], bank[:, :], ACT.Tanh, scale=0.5).then_inc(p_out, 1)
                    else:
                        wait(act, conv_done, 6 * (u - 1))
                        wait(act, carried, u - 1)
                        act.activation(cin[:, q, what, HIST:], bank[:, :], ACT.Copy).then_inc(p_out, 1)

                def silu(u, q, b):
                    n = {4: 0, 5: 1, 0: 2, 1: 3, 2: 4, 3: 5}[b]
                    wait(act, conv_done, 6 * u + n + 1)
                    if b >= 4:
                        wait(act, ema_done, 2 * (u - 1))
                    wait(act, tt_done, GROUP * (u - 1))
                    if b < 4:
                        act.activation(act_out[:, q, b, :], cout[:, b, :], ACT.Silu).then_inc(silu_own, 1)
                        wait(act, silu_own, 4 * u + n - 1)
                        act.activation(act_out[:, q, b, :], act_out[:, q, b, :], ACT.Silu).then_inc(silu_done, 1)
                    else:
                        act.activation(act_out[:, q, b, :], cout[:, b, :], ACT.Silu).then_inc(silu_done, 1)

                def squares(j):
                    t, s = GROUP * v + j, j % 2
                    wait(act, tt_done, t + 1)
                    wait(act, ss_done, t - 1)
                    act.activation(sq[:, s, :], ps_qk[s][:, :], ACT.Square).then_inc(sq_done, 1)
                    wait(act, sent[s], 24 * (GROUP * v + j - s))
                    act.activation(ve[:, s, :], ps_ve[:, :], ACT.Copy).then_inc(ve_out, 1)

                def back(j):
                    t, s = GROUP * v + j, j % 2
                    wait(act, bt_done, t + 1)
                    wait(act, eo_done, 2 * (t - 1))
                    wait(act, sent[s], 24 * (GROUP * v + j - s))
                    wait(act, g_done, t - 1)
                    act.activation(bT[:, s], ps_b[:, :].rearrange("p (b t) -> p b t", b=4), ACT.Copy).then_inc(bt_out, 1)

                if here:
                    use(0)
                    use(1)
                if tiles:
                    silu(v, r, 2)
                    silu(v, r, 3)
                    ps_s = ps_b[:, 0:GROUP * SM].rearrange("p (j c) -> p j c", c=SM)
                    wait(act, sm_done, v + 1)
                    wait(act, small_done, 2 * v)
                    act.activation(sm_t[:, 0], ps_s[:, :, 32:SM], ACT.Tanh, scale=0.5)
                    act.activation(sm_m[:, :, :], ps_s[:, :, 0:NH1], ACT.Silu).then_inc(sm_out, 1)
                if here:
                    use(2)
                if tiles:
                    squares(0)
                if here:
                    use(3)
                    use(4)
                if tiles:
                    squares(1)
                    wait(act, sm_add, v + 1)
                    act.activation(sm_t[:, 1], sm_m[:, :, :], ACT.Tanh, scale=0.5).then_inc(sm_tanh, 1)
                if here:
                    silu(u, q, 4)
                    use(5)
                if tiles:
                    back(0)
                if here:
                    use(6)
                    silu(u, q, 5)
                if tiles:
                    squares(2)
                if here:
                    use(7)
                if tiles:
                    back(1)
                if here:
                    use(8)
                    silu(u, q, 0)
                if tiles:
                    squares(3)
                if here:
                    use(9)
                if tiles:
                    back(2)
                if here:
                    use(10)
                    silu(u, q, 1)
                if tiles:
                    back(3)

            pipelined(act, NG, DEPTH, step)

        @block.vector
        def _(dve):
            dve.wait_ge(loaded, 16 * N_LOADS)
            dve.tensor_copy(w_g[:, :, :].rearrange("p k (h c) -> p k h c", h=NH1),
                            w_dec[:, :, :].unsqueeze(3).broadcast_to([P, KD, NH1, DH])).then_inc(spread, 1)
            dve.wait_ge(zeroed, 7)

            def step(i, par):
                u, q = i - 1, (par - 1) % 2
                here = has(u, NG)
                v, r = i - 2, (par - 2) % 2
                tiles = has(v, NG)

                def conv(b):
                    n = {4: 0, 5: 1, 0: 2, 1: 3, 2: 4, 3: 5}[b]
                    use = 2 + ORDER.index(b)
                    wait(dve, p_out, USES * u + use + 1)
                    wait(dve, carried, u)
                    wait(dve, silu_done, 6 * (u - 1) + n + 1)
                    x = cin[:, q, b]
                    dve.tensor_scalar(cout[:, b, :], x[:, 0:GW], taps[:, b, 0:1], None, ALU.mult).then_inc(conv_own, 1)
                    for c in range(1, CONV):
                        wait(dve, conv_own, 18 * u + 3 * n + c)
                        dve.scalar_tensor_tensor(out=cout[:, b, :], in0=x[:, c:c + GW], scalar=taps[:, b, c:c + 1],
                                                 in1=cout[:, b, :], op0=ALU.mult, op1=ALU.add)\
                           .then_inc(conv_own if c < HIST else conv_done, 1)

                def sums(j):
                    t, s = GROUP * v + j, j % 2
                    wait(dve, sq_done, t + 1)
                    wait(dve, sse_done, t - 1)
                    dve.tensor_reduce(ss[:, s, :], sq[:, s, :].rearrange("p (h c) -> p h c", h=8), AX.X,
                                      ALU.add).then_inc(ss_done, 1)

                def scale(j):
                    t, s = GROUP * v + j, j % 2
                    wait(dve, rn_done, t + 1)
                    wait(dve, bt_done, t - 1)
                    wait(dve, sent[s], 24 * (GROUP * v + j - s))
                    dve.tensor_tensor(qkn[:, s, :].rearrange("p (h c) -> p h c", h=8),
                                      ps_qk[s][:, :].rearrange("p (h c) -> p h c", h=8),
                                      rn[:, s, :].unsqueeze(2).broadcast_to([P, 8, DH]), ALU.mult).then_inc(qkn_done, 1)

                def blocks(j):
                    t, s = GROUP * v + j, j % 2
                    wait(dve, g_done, t + 1)
                    wait(dve, small_done, 2 * (v + 1))
                    wait(dve, l_sent[s], 8 * (GROUP * v + j - s))
                    for k in range(4):
                        rows = slice(32 * k, 32 * k + 32)
                        nb = small[rows, bass.ds(t, 1), 2 * NH1:3 * NH1].rearrange("p a h -> p (a h)")
                        dve.tensor_tensor(l32[rows, s], nb.unsqueeze(2).broadcast_to([32, NH1, 32]),
                                          ps_g[s][rows, :].rearrange("p (h c) -> p h c", h=NH1)[:, :, rows],
                                          ALU.mult).then_inc(g_out, 1)

                if has(i, NG):
                    for j in range(GROUP):
                        t = GROUP * i + j
                        x = tile_of(x_res, t)
                        if j == 0:
                            wait(dve, got_in[par], 16 * 8 * ((i - par) // 2 + 1) if isinstance(i, int) else 64 * (i - par) + 128)
                        for s in range(2):
                            dve.scalar_tensor_tensor(out=x, in0=got[:, par, j, s, :], scalar=gates[:, s, bass.ds(t, 1)],
                                                     in1=x, op0=ALU.mult, op1=ALU.add).then_inc((first_done, x_done)[s], 1)
                            wait_apart(dve, loaded, (first_done, x_done)[s], t + 1)
                        wait_apart(dve, loaded, norm_done, GROUP * i)
                        dve.bn_stats(stats[:, j, :], x).then_inc(stats_done, 1)
                        wait_apart(dve, loaded, stats_done, t + 1)
                        dve.bn_aggr(mom[:, j, :], stats[:, j, :]).then_inc(mom_done, 1)
                if tiles:
                    wait(dve, sm_out, v + 1)
                    sm = small[:, bass.ds(GROUP * v, GROUP), :]
                    dve.tensor_scalar(sm[:, :, 0:NH1], sm_t[:, 0], 0.5, 0.5, ALU.mult, ALU.add)
                    dve.tensor_scalar(sm[:, :, 2 * NH1:3 * NH1], sm_t[:, 0], -0.5, -0.5, ALU.mult, ALU.add).then_inc(small_done, 1)
                    dve.tensor_tensor(sm_m[:, :, :], sm_m[:, :, :], mix_b[:, :].unsqueeze(1).broadcast_to([P, GROUP, NH1]),
                                      ALU.add).then_inc(sm_add, 1)
                if here:
                    conv(4)
                if tiles:
                    sums(0)
                if here:
                    conv(5)
                if tiles:
                    scale(0)
                    sums(1)
                    wait(dve, sm_tanh, v + 1)
                    dve.tensor_scalar(sm[:, :, NH1:2 * NH1], sm_t[:, 1], 0.5, 0.5, ALU.mult, ALU.add).then_inc(small_done, 1)
                if here:
                    conv(0)
                if tiles:
                    scale(1)
                    sums(2)
                if here:
                    wait(dve, dec_done, 2 * (u + 1))
                    wait(dve, silu_done, 6 * u + 2)
                    dve.tensor_tensor(inp[:, :, :], inp[:, :, :], act_out[:, q, 4:6, :], ALU.mult).then_inc(inp_done, 1)
                    wait(dve, inp_done, u + 1)
                    wait(dve, tt_done, GROUP * (u - 1))
                    wait(dve, ema_done, 2 * u)
                    for b in range(2):
                        first = isinstance(u, int) and u == 0
                        dve.tensor_tensor_scan(ema[:, q, b, :], dec[:, b, :], inp[:, b, :],
                                               0.0 if first else ema[:, 1 - q, b, GW - 1:GW], ALU.mult, ALU.add)\
                           .then_inc(ema_done, 1)
                if tiles:
                    blocks(0)
                if here:
                    conv(1)
                if tiles:
                    scale(2)
                    sums(3)
                    blocks(1)
                if here:
                    conv(2)
                if tiles:
                    scale(3)
                    blocks(2)
                if here:
                    conv(3)
                if tiles:
                    blocks(3)
                n = i - 3
                if has(n, NG):
                    wait(dve, l_back, 16 * 8 * (n + 1))
                    wait(dve, t_sent, 16 * 8 * n)
                    for row in range(1, SUB):
                        if row > 1:
                            wait(dve, sub_own, 29 * n + 2 * (row - 1))
                        a = prod[:, 0:row, 0:row]
                        dve.tensor_tensor(a, l_in[:, row:row + 1, 0:row].broadcast_to([P, row, row]),
                                          t_out[:, 0:row, 0:row].rearrange("p j k -> p k j"), ALU.mult).then_inc(sub_own, 1)
                        wait(dve, sub_own, 29 * n + 2 * row - 1)
                        dve.tensor_reduce(t_out[:, row, 0:row], a, AX.X, ALU.add)\
                           .then_inc(sub_own if row < SUB - 1 else sub_done, 1)
                if has(i, NG):
                    wait(dve, rstd_done, i + 1)
                    wait(dve, p_done, USES * (i - 2) + 2)
                    for j in range(GROUP):
                        dve.tensor_scalar(xn[:, par, j, :], tile_of(x_res, GROUP * i + j), mom[:, j, 0:1], rstd[:, j:j + 1],
                                          ALU.subtract, ALU.mult).then_inc(norm_done, 1)

            pipelined(dve, NG, DEPTH, step)

        @block.tensor
        def _(pe):
            pe.wait_ge(loaded, 16 * N_LOADS)
            pe.wait_ge(spread, 1)
            pe.wait_ge(zeroed, 7)

            def step(i, par):
                u, q = i - 1, (par - 1) % 2
                here = has(u, NG)
                v, r = i - 2, (par - 2) % 2
                tiles = has(v, NG)

                def use(n):
                    bank = pp[n % 2]
                    wait(pe, p_out, USES * u + (n - 1 if n else 0))
                    if n < 2:
                        wait(pe, norm_done, GROUP * (u + 1))
                        for j in range(GROUP):
                            mm = pe.transpose(bank[:, j * P:(j + 1) * P], xn[:, q, j, n * P:(n + 1) * P], ident[:, :])
                        mm.then_inc(p_done, 1)
                        return
                    what = ORDER[n - 2]
                    wait(pe, p_out, USES * u + 2)
                    for k in range(KD):
                        if what == "s":
                            lhs, out = w_s[:, k, :], bank[0:SM, :]
                        elif isinstance(what, str):
                            lhs, out = w_g[:, k, int(what[1]) * P:(int(what[1]) + 1) * P], bank[:, :]
                        else:
                            lhs, out = w_p[:, k, what * P:(what + 1) * P], bank[:, :]
                        mm = pe.matmul(out, lhs, xT[:, k, :], start=(k == 0), stop=(k == KD - 1))
                    mm.then_inc(p_done, 1)

                def to_tokens(j):
                    t, s = GROUP * v + j, j % 2
                    wait(pe, silu_done, 6 * (v + 1))
                    wait(pe, ema_done, 2 * (v + 1))
                    wait(pe, qkn_done, t - 1)
                    cols = slice(j * P, (j + 1) * P)
                    for b in range(4):
                        pe.transpose(ps_qk[s][:, b * P:(b + 1) * P], act_out[:, r, b, cols], ident[:, :])
                    wait(pe, ve_out, t)
                    for b in range(2):
                        pe.transpose(ps_ve[:, b * P:(b + 1) * P], act_out[:, r, 4 + b, cols], ident[:, :])
                    for b in range(2):
                        mm = pe.transpose(ps_ve[:, (2 + b) * P:(3 + b) * P], ema[:, r, b, cols], ident[:, :])
                    mm.then_inc(tt_done, 1)

                def back(j):
                    t, s = GROUP * v + j, j % 2
                    wait(pe, qkn_done, t + 1)
                    wait(pe, bt_out, t)
                    if j == 0:
                        wait(pe, sm_out, v + 1)
                    for b in range(4):
                        mm = pe.transpose(ps_b[:, b * P:(b + 1) * P], qkn[:, s, b * P:(b + 1) * P], ident[:, :])
                    mm.then_inc(bt_done, 1)

                def gram(j):
                    t, s = GROUP * v + j, j % 2
                    wait(pe, eo_done, 2 * (t + 1))
                    wait(pe, g_out, 4 * (t - 1))
                    for p in range(2):
                        mm = pe.matmul(ps_g[s][:, 256 * p:256 * (p + 1)], bT[:, s, 2 + p, :],
                                       k_eo[:, s, p].rearrange("p e t -> p (e t)"), start=True, stop=True)
                    mm.then_inc(g_done, 1)

                if here:
                    use(0)
                    use(1)
                if tiles:
                    wait(pe, mix_done, v + 1)
                    wait_apart(pe, loaded, bt_out, GROUP * v)
                    for j in range(GROUP):
                        mm = pe.transpose(ps_b[:, j * SM:(j + 1) * SM], sm_row[:, r, j * P:(j + 1) * P], ident[0:SM, 0:SM])
                    mm.then_inc(sm_done, 1)
                if here:
                    use(2)
                if tiles:
                    to_tokens(0)
                if here:
                    use(3)
                    use(4)
                if tiles:
                    to_tokens(1)
                if here:
                    use(5)
                if tiles:
                    back(0)
                if here:
                    use(6)
                if tiles:
                    to_tokens(2)
                    gram(0)
                if here:
                    use(7)
                if tiles:
                    back(1)
                if here:
                    use(8)
                if tiles:
                    to_tokens(3)
                    gram(1)
                if here:
                    use(9)
                if tiles:
                    back(2)
                if here:
                    use(10)
                if tiles:
                    gram(2)
                    back(3)
                    gram(3)

            pipelined(pe, NG, DEPTH, step)


def delta_rule(nc, x_res, small, rec, t_mat, w):
    with ExitStack() as ctx:
        def sb(name, shape, dt=F32):
            return ctx.enter_context(nc.sbuf_tensor("u_" + name, shape, dt))

        def psum(name):
            return ctx.enter_context(nc.psum_tensor("u_" + name, [P, 512], F32))

        def sem(name):
            return ctx.enter_context(nc.semaphore("u_" + name))

        H = NH1
        w_o = sb("w_o", [P, KD, D])
        rms = sb("rms", [P, 1])
        ident = sb("ident", [P, P])
        causal = sb("causal", [P, P])
        lower = sb("lower", [P, P])
        step16 = sb("step16", [P, P])
        block16 = sb("block16", [P, P // SUB])
        half = sb("half", [P, H])

        kve = sb("kve", [P, 4, 3, D])
        qkT = sb("qkT", [P, 4, 4, P])
        eo = sb("eo", [P, 4, 4, 2, P])
        x16 = sb("x16", [P, 4, H, SUB])
        X = sb("X", [P, 2, H, P])
        XT = sb("XT", [P, 2, H, P])
        kb = sb("kb", [P, 2, D])
        vb = sb("vb", [P, 2, H, P])
        L = sb("L", [P, H, P])
        stm = sb("stm", [P, 2, H, P])
        Z = [sb(f"Z{n}", [P, H, P]) for n in range(3)]
        wT = sb("wT", [P, 2, P])
        u = sb("u", [P, H, P])
        S = sb("S", [P, 2, 2, P])
        diff = sb("diff", [P, D])
        mixed = sb("mixed", [P, D])
        o2 = sb("o2", [P, D])
        sq = sb("sq", [P, D])
        ss = sb("ss", [P, H])
        ms = sb("ms", [P, H])
        rn = sb("rn", [P, H])
        o3 = sb("o3", [P, 2, D])
        oT = sb("oT", [P, KD, P])
        b_z, b_x, b_xt, b_w, b_u, b_o, b_s, b_y = [psum(f"bank{n}") for n in range(8)]

        def heads(ap):
            return ap[:, :].rearrange("p (h c) -> p h c", h=H)

        loaded = sem("loaded")
        zeroed = sem("zeroed")
        scaled = sem("scaled")
        rec_in = [sem(f"rec_in{k}") for k in range(4)]
        x0_done = sem("x0_done")
        kb_done = sem("kb_done")
        vb_done = sem("vb_done")
        g_done = sem("g_done")
        l_done = sem("l_done")
        st_done = sem("st_done")
        stm_done = sem("stm_done")
        xt0_done = sem("xt0_done")
        xt0_out = sem("xt0_out")
        z_done = sem("z_done")
        z_out = sem("z_out")
        x_done = sem("x_done")
        x_out = sem("x_out")
        xt_done = sem("xt_done")
        xt_out16 = sem("xt_out16")
        xt_out = sem("xt_out")
        w_done = sem("w_done")
        w_out = sem("w_out")
        u_done = sem("u_done")
        u_out = sem("u_out")
        s_done = sem("s_done")
        s_out = sem("s_out")
        o_done = sem("o_done")
        diff_done = sem("diff_done")
        mixed_done = sem("mixed_done")
        o2_done = sem("o2_done")
        sq_done = sem("sq_done")
        ss_done = sem("ss_done")
        ms_done = sem("ms_done")
        rn_done = sem("rn_done")
        o3_done = sem("o3_done")
        ot_done = sem("ot_done")
        ot_out = sem("ot_out")
        y_done = sem("y_done")
        y_out = sem("y_out")
        block = ctx.enter_context(nc.Block())
        DEPTH = 4
        N_LOADS = 8

        @block.sync
        def _(sp):
            sp.dma_start(w_o[:, :, :], w["Wo"].rearrange("(k p) n -> p k n", p=P)).then_inc(loaded, 16)
            for e in range(2):
                sp.dma_start(rms[64 * e:64 * e + 64, :], w["rms_w"]).then_inc(loaded, 16)
            sp.dma_start(ident[:, :], w["c_ident"]).then_inc(loaded, 16)
            sp.dma_start(causal[:, :], w["c_causal"]).then_inc(loaded, 16)
            sp.dma_start(lower[:, :], w["c_lower"]).then_inc(loaded, 16)
            sp.dma_start(step16[:, :], w["c_step16"]).then_inc(loaded, 16)
            sp.dma_start(block16[:, :], w["c_block16"]).then_inc(loaded, 16)
            sp.wait_ge(zeroed, 6)

            def step(i, k):
                t = i
                if has(t, NT):
                    wait_apart(sp, loaded, o_done, t - 3)
                    wait_apart(sp, loaded, diff_done, t - 3)
                    row = rec[bass.ds(t * P, P), :]
                    sp.dma_start(x16[:, k], t_mat[bass.ds(t * P, P), :].rearrange("p (h c) -> p h c", h=H)).then_inc(rec_in[k], 16)
                    sp.dma_start(kve[:, k], row[:, 0:3 * D].rearrange("p (n c) -> p n c", n=3)).then_inc(rec_in[k], 16)
                    cols = row[:, 3 * D:5 * D].rearrange("p (b t) -> p b t", b=4)
                    sp.dma_start(qkT[:, k], cols).then_inc(rec_in[k], 16)
                    for e in range(2):
                        r = slice(64 * e, 64 * e + 64)
                        sp.dma_start(eo[r, k, :, e, :], cols[r]).then_inc(rec_in[k], 16)

            pipelined(sp, NT, DEPTH, step, unroll=4)

        @block.gpsimd
        def _(pool):
            pool.memset(half[:, :], -0.5).then_inc(zeroed, 1)
            pool.memset(eo[:, :, :, :, :], 0.0).then_inc(zeroed, 1)
            pool.memset(vb[:, :, :, :], 0.0).then_inc(zeroed, 1)
            pool.memset(u[:, :, :], 0.0).then_inc(zeroed, 1)
            pool.memset(S[:, :, :, :], 0.0).then_inc(zeroed, 1)
            for n in (1, 2):
                pool.memset(Z[n][:, :, :], 0.0).then_inc(zeroed, 1)
            pool.wait_ge(loaded, 16 * N_LOADS)
            pool.wait_ge(zeroed, 7)

            def step(i, k):
                t, s, q = i - 1, (k - 1) % 4, (k - 1) % 2
                if has(t, NT):
                    wait_apart(pool, loaded, rec_in[s], 20 * (t - s) + 80)
                    wait_apart(pool, loaded, xt_done, 3 * (t - 1))
                    pool.tensor_tensor(X[:, q].rearrange("p h (b c) -> p h b c", c=SUB),
                                       x16[:, s].unsqueeze(2).broadcast_to([P, H, P // SUB, SUB]),
                                       block16[:, :].unsqueeze(1).unsqueeze(3).broadcast_to([P, H, P // SUB, SUB]),
                                       ALU.mult).then_inc(x0_done, 1)
                    beta = small[:, bass.ds(t, 1), 0:H].rearrange("p a h -> p (a h)").unsqueeze(2).broadcast_to([P, H, DH])
                    wait_apart(pool, loaded, w_done, t - 1)
                    pool.tensor_tensor(kb[:, q, :].rearrange("p (h c) -> p h c", h=H),
                                       kve[:, s, 0, :].rearrange("p (h c) -> p h c", h=H), beta, ALU.mult).then_inc(kb_done, 1)
                    wait_apart(pool, loaded, u_done, t - 1)
                    for e in range(2):
                        pool.tensor_tensor(vb[:, q, e::2, 64 * e:64 * e + 64],
                                           kve[:, s, 1, :].rearrange("p (h c) -> p h c", h=H)[:, e::2, :],
                                           beta[:, e::2, :], ALU.mult).then_inc(vb_done, 1)
                t = i - 3
                if has(t, NT):
                    mix = small[:, bass.ds(t, 1), H:2 * H].rearrange("p a h -> p (a h)").unsqueeze(2).broadcast_to([P, H, DH])
                    wait_apart(pool, loaded, diff_done, t + 1)
                    wait_apart(pool, loaded, o2_done, t)
                    pool.tensor_tensor(mixed[:, :].rearrange("p (h c) -> p h c", h=H),
                                       diff[:, :].rearrange("p (h c) -> p h c", h=H), mix, ALU.mult).then_inc(mixed_done, 1)
                    wait_apart(pool, loaded, ss_done, t + 1)
                    pool.tensor_scalar(ms[:, :], ss[:, :], 1.0 / DH, EPS, ALU.mult, ALU.add).then_inc(ms_done, 1)
                    wait_apart(pool, loaded, ms_done, t + 1)
                    wait_apart(pool, loaded, o3_done, t)
                    pool.tensor_tensor(rn[:, :], ms[:, :], half[:, :], ALU.pow).then_inc(rn_done, 1)

            pipelined(pool, NT, DEPTH, step, unroll=4)

        @block.scalar
        def _(act):
            act.wait_ge(zeroed, 7)

            def step(i, k):
                a, aq = i - 2, k % 2
                b = i - 3
                c = i - 4
                A, B, C = has(a, NT), has(b, NT), has(c, NT)
                if A:
                    wait(act, xt0_done, a + 1)
                    wait(act, w_done, a - 1)
                    wait(act, u_done, a - 1)
                    act.activation(XT[:, aq], heads(b_xt), ACT.Copy).then_inc(xt0_out, 1)
                if B:
                    wait(act, w_done, b + 1)
                    wait(act, u_done, b)
                    act.activation(wT[:, :, :], b_w[:, 0:256].rearrange("p (n t) -> p n t", n=2), ACT.Copy,
                                   scale=-1.0).then_inc(w_out, 1)
                if A:
                    wait(act, z_done, 3 * a + 2)
                    wait(act, xt_done, 3 * (a - 1) + 2)
                    for n in range(2):
                        r, cc = slice(64 * n, 64 * n + 32), slice(64 * n + 32, 64 * n + 64)
                        z = act.activation(Z[1][r, :, cc], heads(b_z)[r, :, cc], ACT.Copy, scale=-1.0)
                    z.then_inc(z_out, 1)
                if B:
                    wait(act, s_done, b + 1)
                    wait(act, o_done, b - 1)
                    wait(act, u_done, b)
                    for e in range(2):
                        r = slice(64 * e, 64 * e + 64)
                        z = act.activation(S[r, (k - 3) % 2, :, r], b_s[r, 0:256].rearrange("p (n c) -> p n c", n=2)[:, :, r],
                                           ACT.Copy)
                    z.then_inc(s_out, 1)
                if A:
                    wait(act, xt_done, 3 * a + 2)
                    for n in range(2):
                        r, cc = slice(64 * n, 64 * n + 32), slice(64 * n + 32, 64 * n + 64)
                        z = act.activation(XT[r, aq, :, cc], heads(b_xt)[r, :, cc], ACT.Copy)
                    z.then_inc(xt_out, 1)
                if C:
                    wait(act, ot_done, c + 1)
                    wait(act, y_done, c)
                    act.activation(oT[:, :, :], b_w[:, 0:256].rearrange("p (n t) -> p n t", n=2), ACT.Copy).then_inc(ot_out, 1)
                if A:
                    wait(act, xt_done, 3 * a + 3)
                    act.activation(XT[0:64, aq, :, 64:128], heads(b_xt)[0:64, :, 64:128], ACT.Copy).then_inc(xt_out, 1)
                if B:
                    wait(act, o2_done, b + 1)
                    wait(act, ss_done, b)
                    act.activation(sq[:, :], o2[:, :], ACT.Square).then_inc(sq_done, 1)

            pipelined(act, NT, DEPTH, step, unroll=4)

        @block.vector
        def _(dve):
            dve.wait_ge(loaded, 16 * N_LOADS)
            dve.tensor_scalar(w_o[:, :, :], w_o[:, :, :], rms[:, 0:1], None, ALU.mult).then_inc(scaled, 1)
            dve.wait_ge(zeroed, 7)

            def step(i, k):
                a, aq = i - 2, k % 2
                b, bs, bq = i - 3, (k - 3) % 4, (k - 3) % 2
                c = i - 4
                A, B, C = has(a, NT), has(b, NT), has(c, NT)
                if A:
                    wait(dve, g_done, a + 1)
                    for h in range(H):
                        g = dve.scalar_tensor_tensor(out=L[:, h, :], in0=heads(b_z)[:, h, :], scalar=small[:, bass.ds(a, 1), h],
                                                     in1=lower[:, :], op0=ALU.mult, op1=ALU.mult)
                    g.then_inc(l_done, 1)
                    wait(dve, st_done, a + 1)
                    wait(dve, o_done, a - 1)
                    dve.tensor_tensor(stm[:, aq], heads(b_x), causal[:, :].unsqueeze(1).broadcast_to([P, H, P]),
                                      ALU.mult).then_inc(stm_done, 1)
                    wait(dve, z_done, 3 * a + 1)
                    dve.tensor_tensor(Z[0][:, :, :], heads(b_z), step16[:, :].unsqueeze(1).broadcast_to([P, H, P]),
                                      ALU.mult).then_inc(z_out, 1)
                if B:
                    wait(dve, u_done, b + 1)
                    wait(dve, s_done, b)
                    wait(dve, o_done, b)
                    uu = u[:, :, :].rearrange("p (n e) c -> p n (e c)", e=2)
                    for e in range(2):
                        z = dve.tensor_copy(u[:, e::2, 64 * e:64 * e + 64],
                                            b_u[:, 0:256].rearrange("p (n e c) -> p n e c", n=2, e=2)[:, :, e, :])
                    z.then_inc(u_out, 1)
                if A:
                    wait(dve, x_done, 2 * a + 1)
                    wait(dve, xt_done, 3 * a + 1)
                    dve.tensor_tensor(XT[:, aq], XT[:, aq], heads(b_xt), ALU.add).then_inc(xt_out16, 1)
                    dve.tensor_tensor(X[:, aq], X[:, aq], heads(b_x), ALU.add).then_inc(x_out, 1)
                    wait(dve, x_done, 2 * a + 2)
                    wait(dve, xt_done, 3 * a + 2)
                    for n in range(2):
                        r, cc = slice(64 * n + 32, 64 * n + 64), slice(64 * n, 64 * n + 32)
                        z = dve.tensor_copy(X[r, aq, :, cc], heads(b_x)[r, :, cc])
                    z.then_inc(x_out, 1)
                    wait(dve, z_done, 3 * a + 3)
                    dve.tensor_scalar(Z[2][0:64, :, 64:128], heads(b_z)[0:64, :, 64:128], -1.0, None, ALU.mult)\
                       .then_inc(z_out, 1)
                if B:
                    wait(dve, o_done, b + 1)
                    wait(dve, mixed_done, b)
                    dve.tensor_tensor(diff[:, :], kve[:, bs, 2, :], b_o[:, 0:D], ALU.subtract).then_inc(diff_done, 1)
                if C:
                    wait(dve, y_done, c + 1)
                    dve.tensor_tensor(tile_of(x_res, c), tile_of(x_res, c), b_y[:, 0:D], ALU.add).then_inc(y_out, 1)
                if B:
                    wait(dve, mixed_done, b + 1)
                    wait(dve, sq_done, b)
                    wait(dve, o3_done, b)
                    dve.tensor_tensor(o2[:, :], b_o[:, 0:D], mixed[:, :], ALU.add).then_inc(o2_done, 1)
                    wait(dve, sq_done, b + 1)
                    wait(dve, ms_done, b)
                    dve.tensor_reduce(ss[:, :], sq[:, :].rearrange("p (h c) -> p h c", h=H), AX.X, ALU.add).then_inc(ss_done, 1)
                    wait(dve, rn_done, b + 1)
                    wait(dve, ot_done, b - 1)
                    dve.tensor_tensor(o3[:, bq, :].rearrange("p (h c) -> p h c", h=H),
                                      o2[:, :].rearrange("p (h c) -> p h c", h=H),
                                      rn[:, :].unsqueeze(2).broadcast_to([P, H, DH]), ALU.mult).then_inc(o3_done, 1)

            pipelined(dve, NT, DEPTH, step, unroll=4)

        @block.tensor
        def _(pe):
            pe.wait_ge(loaded, 16 * N_LOADS)
            pe.wait_ge(zeroed, 7)
            pe.wait_ge(scaled, 1)

            def step(i, k):
                a, asl, aq = i - 2, (k - 2) % 4, k % 2
                b, bs, bq = i - 3, (k - 3) % 4, (k - 3) % 2
                c, cq = i - 4, k % 2
                A, B, C = has(a, NT), has(b, NT), has(c, NT)

                def four(bank, lhs, rhs):
                    for h in range(H):
                        mm = pe.matmul(bank[:, h * P:(h + 1) * P], lhs(h), rhs(h), start=True, stop=True)
                    return mm

                if A:
                    wait(pe, x0_done, a + 1)
                    wait(pe, rec_in[asl], 20 * (a - asl) + 80)
                    wait(pe, z_out, 3 * a)
                    for n in range(2):
                        mm = pe.matmul(b_z[:, 256 * n:256 * n + 256], qkT[:, asl, 2 + n, :],
                                       eo[:, asl, 2 + n].rearrange("p e t -> p (e t)"), start=True, stop=True)
                    mm.then_inc(g_done, 1)
                    wait(pe, x_out, 2 * a)
                    for n in range(2):
                        mm = pe.matmul(b_x[:, 256 * n:256 * n + 256], qkT[:, asl, 2 + n, :],
                                       eo[:, asl, n].rearrange("p e t -> p (e t)"), start=True, stop=True)
                    mm.then_inc(st_done, 1)
                    wait(pe, xt_out, 2 * a)
                    for h in range(H):
                        mm = pe.transpose(b_xt[:, h * P:(h + 1) * P], X[:, aq, h, :], ident[:, :])
                    mm.then_inc(xt0_done, 1)
                if B:
                    wait(pe, kb_done, b + 1)
                    wait(pe, xt_out, 2 * (b + 1))
                    wait(pe, ot_out, b - 1)
                    for h in range(H):
                        e = h % 2
                        mm = pe.matmul(b_w[64 * e:64 * e + 64, (h // 2) * P:(h // 2 + 1) * P], kb[:, bq, h * DH:(h + 1) * DH],
                                       XT[:, bq, h, :], start=True, stop=True)
                    mm.then_inc(w_done, 1)
                    wait(pe, vb_done, 2 * (b + 1))
                    wait(pe, u_out, b)
                    for h in range(H):
                        pe.matmul(b_u[:, (h // 2) * P:(h // 2 + 1) * P], XT[:, bq, h, :], vb[:, bq, h, :], start=(h == 0),
                                  stop=False, skip_group_check=True)
                if A:
                    wait(pe, l_done, a + 1)
                    wait(pe, xt0_out, a + 1)
                    four(b_z, lambda h: L[:, h, :], lambda h: XT[:, aq, h, :]).then_inc(z_done, 1)
                if B:
                    wait(pe, w_out, b + 1)
                    wait(pe, s_out, b)
                    for n in range(2):
                        mm = pe.matmul(b_u[:, n * P:(n + 1) * P], wT[:, n, :], S[:, 1 - bq, n, :], start=False, stop=True,
                                       skip_group_check=True)
                    mm.then_inc(u_done, 1)
                if A:
                    wait(pe, z_out, 3 * a + 1)
                    wait(pe, stm_done, a + 1)
                    four(b_xt, lambda h: X[:, aq, h, :], lambda h: Z[0][:, h, :]).then_inc(xt_done, 1)
                    four(b_x, lambda h: Z[0][:, h, :], lambda h: X[:, aq, h, :]).then_inc(x_done, 1)
                if B:
                    wait(pe, u_out, b + 1)
                    for n in range(2):
                        uu = u[:, 2 * n:2 * n + 2, :].rearrange("p e c -> p (e c)")
                        for e in range(2):
                            mm = pe.matmul(b_s[:, n * P + 64 * e:n * P + 64 * e + 64], kve[:, bs, 0, n * P:(n + 1) * P],
                                           u[:, 2 * n + e, 64 * e:64 * e + 64],
                                           start=(isinstance(b, int) and b == 0 and n == 0 and e == 0), stop=True,
                                           skip_group_check=True)
                    mm.then_inc(s_done, 1)
                if A:
                    wait(pe, xt_out16, a + 1)
                    four(b_z, lambda h: L[:, h, :], lambda h: XT[:, aq, h, :]).then_inc(z_done, 1)
                if B:
                    wait(pe, o2_done, b)
                    for n in range(2):
                        pe.matmul(b_o[:, n * P:(n + 1) * P], qkT[:, bs, n, :], S[:, 1 - bq, n, :], start=(n == 0), stop=False,
                                  skip_group_check=True)
                    wait(pe, stm_done, b + 1)
                    for h in range(H):
                        mm = pe.matmul(b_o[:, (h // 2) * P:(h // 2 + 1) * P], stm[:, bq, h, :], u[:, h, :], start=False,
                                       stop=(h % 2 == 1), skip_group_check=True)
                    mm.then_inc(o_done, 1)
                if A:
                    wait(pe, z_out, 3 * a + 2)
                    wait(pe, x_out, 2 * a + 1)
                    four(b_x, lambda h: Z[1][:, h, :], lambda h: X[:, aq, h, :]).then_inc(x_done, 1)
                    four(b_xt, lambda h: X[:, aq, h, :], lambda h: Z[1][:, h, :]).then_inc(xt_done, 1)
                if C:
                    wait(pe, o3_done, c + 1)
                    wait(pe, w_out, c + 2, NT)
                    for n in range(KD):
                        mm = pe.transpose(b_w[:, n * P:(n + 1) * P], o3[:, cq, n * P:(n + 1) * P], ident[:, :])
                    mm.then_inc(ot_done, 1)
                if A:
                    wait(pe, xt_out, 2 * a + 1)
                    four(b_z, lambda h: L[:, h, :], lambda h: XT[:, aq, h, :]).then_inc(z_done, 1)
                if C:
                    wait(pe, ot_out, c + 1)
                    wait(pe, y_out, c)
                    for n in range(KD):
                        mm = pe.matmul(b_y[:, 0:D], oT[:, n, :], w_o[:, n, :], start=(n == 0), stop=(n == KD - 1))
                    mm.then_inc(y_done, 1)
                if A:
                    wait(pe, z_out, 3 * a + 3)
                    wait(pe, x_out, 2 * a + 2)
                    four(b_xt, lambda h: X[:, aq, h, :], lambda h: Z[2][:, h, :]).then_inc(xt_done, 1)

            pipelined(pe, NT, DEPTH, step, unroll=4)


def gated_output(nc, x_res, out, w):
    with ExitStack() as ctx:
        def sb(name, shape, dt=F32):
            return ctx.enter_context(nc.sbuf_tensor("g_" + name, shape, dt))

        def psum(name):
            return ctx.enter_context(nc.psum_tensor("g_" + name, [P, 512], F32))

        def sem(name):
            return ctx.enter_context(nc.semaphore("g_" + name))

        w_g = sb("w_g", [P, KD, 3, D])
        u_g = sb("u_g", [P, KD, 3, D])
        b_g = sb("b_g", [P, 6])
        c0 = sb("c0", [P, KD])
        c0h = sb("c0h", [P, KD])
        bias = sb("bias", [P, 6])
        w_o = sb("w_o", [P, KD, D])
        u_o = sb("u_o", [P, KD, D])
        b_o = sb("b_o", [P, D])
        ident = sb("ident", [P, P])
        half = sb("half", [P, GROUP])
        stats = sb("stats", [P, GROUP, 6])
        mom = sb("mom", [P, GROUP, 2])
        shifted = sb("shifted", [P, GROUP])
        rstd = sb("rstd", [P, GROUP])
        xn = sb("xn", [P, 2, GROUP, D])
        xT = sb("xT", [P, 2, KD, GW])
        gates = sb("gates", [P, 6, GW])
        cT = sb("cT", [P, 2, KD, GW])
        z = sb("z", [P, 2, D])
        h = sb("h", [P, 2, D])
        res = sb("res", [P, 2, D])
        pp = [psum(f"pp{i}") for i in range(2)]
        py = [psum(f"py{i}") for i in range(2)]
        loaded = sem("loaded")
        ready = sem("ready")
        bias_done = sem("bias_done")
        bias_set = sem("bias_set")
        stats_done = sem("stats_done")
        mom_done = sem("mom_done")
        shift_done = sem("shift_done")
        rstd_done = sem("rstd_done")
        norm_done = sem("norm_done")
        p_done = sem("p_done")
        p_out = sem("p_out")
        keep_done = sem("keep_done")
        new_done = sem("new_done")
        c_done = sem("c_done")
        y_done = sem("y_done")
        z_done = sem("z_done")
        h_done = sem("h_done")
        res_done = sem("res_done")
        sent = [sem(f"sent{i}") for i in range(2)]
        block = ctx.enter_context(nc.Block())
        DEPTH = 2
        N_LOADS = 12

        @block.sync
        def _(sp):
            for n, name in enumerate(("f", "i", "c")):
                sp.dma_start(w_g[:, :, n, :], w[f"w{name}T"].rearrange("(k p) n -> p k n", p=P)).then_inc(loaded, 16)
                sp.dma_start(u_g[:, :, n, :], w[f"u{name}T"].rearrange("(k p) n -> p k n", p=P)).then_inc(loaded, 16)
            sp.dma_start(b_g[:, :], w["b_gates"]).then_inc(loaded, 16)
            sp.dma_start(c0[:, :], w["c0"]).then_inc(loaded, 16)
            sp.dma_start(w_o[:, :, :], w["woT"].rearrange("(k p) n -> p k n", p=P)).then_inc(loaded, 16)
            sp.dma_start(u_o[:, :, :], w["uoT"].rearrange("(k p) n -> p k n", p=P)).then_inc(loaded, 16)
            sp.dma_start(b_o[:, :], w["bo"].partition_broadcast(P)).then_inc(loaded, 16)
            sp.dma_start(ident[:, :], w["c_ident"]).then_inc(loaded, 16)

            def step(i, par):
                v = i - 2
                if has(v, NG):
                    for j in range(GROUP):
                        t, s = GROUP * v + j, j % 2
                        wait_apart(sp, loaded, res_done, t + 1)
                        sp.dma_start(out[bass.ds(t * P, P), :], res[:, s, :]).then_inc(sent[s], 16)

            pipelined(sp, NG, DEPTH, step)
            for s in range(2):
                sp.wait_ge(sent[s], 16 * NT // 2)

        @block.gpsimd
        def _(pool):
            pool.memset(half[:, :], -0.5).then_inc(ready, 1)
            pool.wait_ge(ready, 1)

            def step(i, par):
                if has(i, NG):
                    wait_apart(pool, loaded, mom_done, GROUP * (i + 1))
                    wait_apart(pool, loaded, norm_done, GROUP * i)
                    pool.tensor_scalar(shifted[:, :], mom[:, :, 1], EPS, None, ALU.add).then_inc(shift_done, 1)
                    wait_apart(pool, loaded, shift_done, i + 1)
                    pool.tensor_tensor(rstd[:, :], shifted[:, :], half[:, :], ALU.pow).then_inc(rstd_done, 1)

            pipelined(pool, NG, DEPTH, step)

        @block.scalar
        def _(act):
            act.wait_ge(bias_set, 4)

            def step(i, par):
                u, q = i - 1, (par - 1) % 2
                v = i - 2

                def use(n):
                    bank = pp[n % 2]
                    wait(act, p_done, 8 * u + n + 1)
                    if n < 2:
                        wait(act, y_done, GROUP * (u - 1))
                        act.activation(xT[:, q, n, :], bank[:, :], ACT.Copy).then_inc(p_out, 1)
                    else:
                        b = n - 2
                        wait(act, c_done, 2 * u)
                        act.activation(gates[:, b, :], bank[:, :], ACT.Tanh, bias=bias[:, b:b + 1],
                                       scale=0.5 if b < 4 else 1.0).then_inc(p_out, 1)

                for n in range(8):
                    if has(u, NG):
                        use(n)
                    if n % 2 == 1 and has(v, NG):
                        t, s = GROUP * v + n // 2, (n // 2) % 2
                        wait(act, z_done, t + 1)
                        wait(act, res_done, t - 1)
                        act.activation(h[:, s, :], z[:, s, :], ACT.Tanh).then_inc(h_done, 1)

            pipelined(act, NG, DEPTH, step)

        @block.vector
        def _(dve):
            dve.wait_ge(loaded, 16 * N_LOADS)
            dve.tensor_scalar(c0h[:, :], c0[:, :], 0.5, None, ALU.mult).then_inc(bias_set, 1)
            dve.wait_ge(bias_done, 1)
            dve.tensor_tensor(bias[:, :], pp[0][:, 0:6], b_g[:, :], ALU.add).then_inc(bias_set, 1)
            dve.wait_ge(bias_set, 2)
            dve.tensor_scalar(bias[:, 0:4], bias[:, 0:4], 0.5, None, ALU.mult).then_inc(bias_set, 2)

            def step(i, par):
                u, q = i - 1, (par - 1) % 2
                v = i - 2
                if has(i, NG):
                    for j in range(GROUP):
                        t = GROUP * i + j
                        wait_apart(dve, loaded, norm_done, GROUP * i)
                        dve.bn_stats(stats[:, j, :], tile_of(x_res, t)).then_inc(stats_done, 1)
                    for j in range(GROUP):
                        wait_apart(dve, loaded, stats_done, GROUP * i + j + 1)
                        dve.bn_aggr(mom[:, j, :], stats[:, j, :]).then_inc(mom_done, 1)

                def last(j):
                    t, s = GROUP * v + j, j % 2
                    wait(dve, y_done, t + 1)
                    wait(dve, h_done, t - 1)
                    dve.tensor_tensor(z[:, s, :], py[s][:, 0:D], b_o[:, :], ALU.add).then_inc(z_done, 1)

                def residual(j):
                    t, s = GROUP * v + j, j % 2
                    wait(dve, h_done, t + 1)
                    wait(dve, sent[s], 8 * (GROUP * v + j - s))
                    dve.tensor_tensor(res[:, s, :], h[:, s, :], tile_of(x_res, t), ALU.add).then_inc(res_done, 1)

                if has(v, NG):
                    last(0)
                    last(1)
                    residual(0)
                    last(2)
                    residual(1)
                    last(3)
                    residual(2)
                    residual(3)
                if has(i, NG):
                    wait(dve, rstd_done, i + 1)
                    wait(dve, p_done, 8 * (i - 2) + 2)
                    for j in range(GROUP):
                        dve.tensor_scalar(xn[:, par, j, :], tile_of(x_res, GROUP * i + j), mom[:, j, 0:1], rstd[:, j:j + 1],
                                          ALU.subtract, ALU.mult).then_inc(norm_done, 1)
                if has(u, NG):
                    wait(dve, y_done, GROUP * (u - 1))
                    wait(dve, p_out, 8 * u + 8)
                    for b in range(KD):
                        g = 2 * u + b + 1
                        dve.tensor_scalar(gates[:, b, :], gates[:, b, :], c0h[:, b:b + 1], c0h[:, b:b + 1], ALU.mult,
                                          ALU.add).then_inc(keep_done, 1)
                        dve.scalar_tensor_tensor(out=gates[:, 2 + b, :], in0=gates[:, 2 + b, :], scalar=1.0,
                                                 in1=gates[:, 4 + b, :], op0=ALU.add, op1=ALU.mult).then_inc(new_done, 1)
                        wait(dve, keep_done, g)
                        wait(dve, new_done, g)
                        dve.scalar_tensor_tensor(out=cT[:, q, b, :], in0=gates[:, 2 + b, :], scalar=0.5, in1=gates[:, b, :],
                                                 op0=ALU.mult, op1=ALU.add).then_inc(c_done, 1)

            pipelined(dve, NG, DEPTH, step)

        @block.tensor
        def _(pe):
            pe.wait_ge(loaded, 16 * N_LOADS)
            for n in range(3):
                for b in range(KD):
                    for k in range(KD):
                        mm = pe.matmul(pp[0][:, 2 * n + b:2 * n + b + 1], u_g[:, k, n, b * P:(b + 1) * P], c0[:, k:k + 1],
                                       start=(k == 0), stop=(k == KD - 1))
            mm.then_inc(bias_done, 1)
            pe.wait_ge(bias_set, 4)

            def step(i, par):
                u, q = i - 1, (par - 1) % 2
                v, r = i - 2, par

                def use(n):
                    bank = pp[n % 2]
                    wait(pe, p_out, 8 * u + n - 1)
                    if n < 2:
                        wait(pe, norm_done, GROUP * (u + 1))
                        for j in range(GROUP):
                            mm = pe.transpose(bank[:, j * P:(j + 1) * P], xn[:, q, j, n * P:(n + 1) * P], ident[:, :])
                    else:
                        b = n - 2
                        wait(pe, p_out, 8 * u + 2)
                        for k in range(KD):
                            mm = pe.matmul(bank[:, :], w_g[:, k, b // 2, (b % 2) * P:(b % 2 + 1) * P], xT[:, q, k, :],
                                           start=(k == 0), stop=(k == KD - 1))
                    mm.then_inc(p_done, 1)

                for n in range(8):
                    if has(u, NG):
                        use(n)
                    if n % 2 == 1 and has(v, NG):
                        j = n // 2
                        t, s = GROUP * v + j, j % 2
                        cols = slice(j * P, (j + 1) * P)
                        wait(pe, c_done, 2 * (v + 1))
                        wait(pe, z_done, t - 1)
                        for k in range(KD):
                            pe.matmul(py[s][:, 0:D], xT[:, r, k, cols], w_o[:, k, :], start=(k == 0), stop=False)
                        for k in range(KD):
                            mm = pe.matmul(py[s][:, 0:D], cT[:, r, k, cols], u_o[:, k, :], start=False, stop=(k == KD - 1))
                        mm.then_inc(y_done, 1)

            pipelined(pe, NG, DEPTH, step)


def build(nc, w, out):
    x_slots = nc.dram_tensor("x_slots", [SLOTS, D], F32, kind="Internal").ap()
    y_slots = nc.dram_tensor("y_slots", [SLOTS, D], F32, kind="Internal").ap()
    rec = nc.dram_tensor("rec", [T, REC], F32, kind="Internal").ap()
    l_mat = nc.dram_tensor("l_mat", [T, NH1 * 2 * SUB], F32, kind="Internal").ap()
    t_mat = nc.dram_tensor("t_mat", [T, NH1 * SUB], F32, kind="Internal").ap()
    with ExitStack() as ctx:
        x_res = ctx.enter_context(nc.sbuf_tensor("x_res", [P, NT, D], F32))
        gates = ctx.enter_context(nc.sbuf_tensor("gates", [P, 2, NT], F32))
        slots = ctx.enter_context(nc.sbuf_tensor("slots", [P, 2, NT], U32))
        small = ctx.enter_context(nc.sbuf_tensor("small", [P, NT, 3 * NH1], F32))
        with ExitStack() as first:
            xn2_res = first.enter_context(nc.sbuf_tensor("xn2_res", [P, NT, D], F32))
            logits = first.enter_context(nc.sbuf_tensor("logits", [P, NT, E], F32))
            tile_expert = first.enter_context(nc.sbuf_tensor("tile_expert", [P, SLOT_TILES], I32))
            w13 = first.enter_context(nc.sbuf_tensor("w13", [P, 2, KD, E, HID], F32))
            w2 = first.enter_context(nc.sbuf_tensor("w2", [P, len(HB), E, D], F32))
            with nc.semaphore("layer0_first") as first_sem:
                pass
            linear_attention(nc, x_res, xn2_res, logits, w13, w2, x_slots, w)
            route(nc, xn2_res, logits, gates, slots, tile_expert, x_slots, w)
            experts(nc, tile_expert, x_slots, y_slots, w13, w2, w)
            with nc.semaphore("layer0_last") as last_sem:
                pass
            with nc.Block() as block:
                @block.gpsimd
                def _(pool):
                    pool.sem_clear(range(first_sem.num, last_sem.num + 1))
        delta_inputs(nc, x_res, gates, slots, y_slots, small, rec, l_mat, t_mat, w)
        delta_rule(nc, x_res, small, rec, t_mat, w)
        gated_output(nc, x_res, out, w)


def constants():
    p = np.arange(P)
    row, col = p[:, None], p[None, :]
    f = np.float32
    return {
        "c_ident": np.eye(P, dtype=f),
        "c_causal": (row <= col).astype(f),
        "c_lower": (col < row).astype(f),
        "c_strict": (row < col).astype(f),
        "c_ones": np.ones((P, P), f),
        "c_eo": (row // 16 % 2 == np.arange(2)).astype(f),
        "c_head": (row // 16 == col // 16).astype(f),
        "c_pair": (row // DH == np.arange(2)).astype(f),
        "c_step16": -((col // SUB % 2 == 1) & (row // SUB == col // SUB - 1)).astype(f),
        "c_block16": (row // SUB == np.arange(P // SUB)).astype(f),
        "c_prio": np.arange(E, 0, -1).astype(f),
        "c_follows": np.tile((np.arange(NT) > 0).astype(f), (E, 1)),
        "c_edges": (P * np.arange(NT)).astype(f),
        "c_numbers": np.arange(SLOT_TILES).astype(f),
    }


def laid_out(inputs):
    a = {k: np.asarray(v) for k, v in inputs.items()}
    l0, f0, l1, f1 = (lambda n, p=p: a[p + n] for p in ("L0_attn_", "L0_ffn_", "L1_attn_", "L1_ffn_"))

    def columns(*vectors):
        return np.concatenate(vectors).reshape(-1, P).T

    k, q, v = np.split(l0("b1"), 3)
    w = {
        "x": l0("x").reshape(T, D), "W1": l0("W1"), "W2": l0("W2"), "b2": l0("b2"),
        "b_qk": columns(q, k), "b_kv": np.concatenate([k, v]),
        "w_rT": f0("w_router").T, "w1": f0("w1"), "w2": f0("w2"), "w3": f0("w3"),
        "rms_w": l1("rms_w").reshape(DH, 1), "Wo": l1("Wo"),
        "b_gates": columns(f1("bf"), f1("bi"), f1("bc")), "c0": columns(f1("in_c")),
        "woT": f1("wo").T, "uoT": f1("uo").T, "bo": f1("bo"),
    }
    for name in ("Wq", "Wk", "Wv", "Wb", "Wdec", "Wmix", "conv_q", "conv_k", "conv_v", "conv_mix", "mix_bias"):
        w[name] = l1(name)
    for g in "fic":
        w[f"w{g}T"] = f1("w" + g).T
        w[f"u{g}T"] = f1("u" + g).T
    return {name: np.ascontiguousarray(v) for name, v in {**w, **constants()}.items()}


def kernel(**inputs):
    import concourse.bacc as bacc
    from concourse.bass_utils import run_bass_kernel_spmd

    nc = bacc.Bacc("TRN2", target_bir_lowering=False, num_devices=1)
    arrays = {f"in_{name}": a for name, a in laid_out(inputs).items()}
    w = {name[3:]: nc.dram_tensor(name, a.shape, mybir.dt.from_np(a.dtype), kind="ExternalInput").ap()
         for name, a in arrays.items()}
    out = nc.dram_tensor("out_dram", (T, D), F32, kind="ExternalOutput").ap()
    build(nc, w, out)
    r = run_bass_kernel_spmd(nc, [arrays], core_ids=[0])
    return r.results[0]["out_dram"].reshape(1, T, D)
```

```python
from contextlib import ExitStack

import numpy as np
import concourse.bass as bass
from concourse import mybir

F32 = mybir.dt.float32
I32 = mybir.dt.int32
U32 = mybir.dt.uint32
ALU = mybir.AluOpType
ACT = mybir.ActivationFunctionType
AX = mybir.AxisListType

P = 128
T = 4096
D = 256
NT = T // P
KD = D // P
EPS = 1e-5

NH0 = 16
E = 8
HID = 352
HB = [(0, 128), (128, 128), (256, 96)]
SLOT_TILES = 2 * T // P + E - 1
SLOTS = SLOT_TILES * P
NH1 = 4
DH = 64


def wait(eng, sem, value, cap=None):
    if isinstance(value, int):
        if cap is not None:
            value = min(value, cap)
        if value <= 0:
            return
    eng.wait_ge(sem, value)


def wait_apart(eng, loaded, sem, value, cap=None):
    if not isinstance(value, int):
        eng.to_reg(value)
        eng.wait_ge(loaded, 1)
    wait(eng, sem, value, cap)


def pipelined(eng, n, depth, step, ahead=0, unroll=2):
    lo = -(-(depth + 1) // unroll) * unroll
    hi = n - ahead - (n - ahead - lo) % unroll
    for i in range(lo):
        step(i, i % unroll)
    with eng.Fori(lo // unroll, hi // unroll) as turn:
        for k in range(unroll):
            step(unroll * turn + k, k)
    for i in range(hi, n + depth):
        step(i, i % unroll)


def has(t, n):
    return not isinstance(t, int) or 0 <= t < n


def tile_of(ap, t):
    return ap[:, bass.ds(t, 1), :].rearrange("p a d -> p (a d)")


def linear_attention(nc, x_res, xn2_res, logits, consts, w13, w2, x_slots, w):
    with ExitStack() as ctx:
        def sb(name, shape, dt=F32):
            return ctx.enter_context(nc.sbuf_tensor(name, shape, dt))

        def psum(name, shape):
            return ctx.enter_context(nc.psum_tensor(name, shape, F32))

        def sem(name):
            return ctx.enter_context(nc.semaphore(name))

        w_qk = sb("w_qk", [P, KD, 512])
        w_kv = sb("w_kv", [P, KD, 512])
        w_o = sb("w_o", [P, KD, D])
        w_r = sb("w_r", [P, KD, E])
        b_qk = sb("b_qk", [P, 4])
        b_kv = sb("b_kv", [P, 512])
        b_o = sb("b_o", [P, D])
        ident = sb("ident0", [P, P])
        causal = sb("causal0", [P, P])
        eo_mask = sb("eo_mask", [P, 2])
        head_mask = sb("head_mask", [P, P])

        half = sb("a_half", [P, 1])
        loaded = sem("a_loaded")
        ln1_stats = sb("ln1_stats", [P, 2, 6])
        ln1_moments = sb("ln1_moments", [P, 2, 2])
        ln1_shifted = sb("ln1_shifted", [P, 2, 1])
        ln1_rstd = sb("ln1_rstd", [P, 2, 1])
        ln1_stats_done = sem("ln1_stats_done")
        ln1_moments_done = sem("ln1_moments_done")
        ln1_shifted_done = sem("ln1_shifted_done")
        ln1_rstd_done = sem("ln1_rstd_done")
        ln1_done = sem("ln1_done")
        ln2_stats = sb("ln2_stats", [P, 2, 6])
        ln2_moments = sb("ln2_moments", [P, 2, 2])
        ln2_shifted = sb("ln2_shifted", [P, 2, 1])
        ln2_rstd = sb("ln2_rstd", [P, 2, 1])
        ln2_stats_done = sem("ln2_stats_done")
        ln2_moments_done = sem("ln2_moments_done")
        ln2_shifted_done = sem("ln2_shifted_done")
        ln2_rstd_done = sem("ln2_rstd_done")
        ln2_done = sem("ln2_done")
        xn = sb("a_xn", [P, 2, D])
        xnT = sb("a_xnT", [P, 2, KD, P])
        qkT = sb("a_qkT", [P, 2, 4, P])
        qeo = sb("a_qeo", [P, 2, 2, 2, P])
        k_tok = sb("a_ktok", [P, 2, D])
        vpad = sb("a_vpad", [P, 2, 8, 2, 32])
        stm = sb("a_stm", [P, 16, P])
        s_bd = sb("a_sbd", [P, 2, 2, P])
        oT = sb("a_oT", [P, 2, KD, P])
        xn2 = sb("a_xn2", [P, 2, D])
        xn2T = sb("a_xn2T", [P, 2, KD, P])

        ps_sc = psum("ps_sc", [P, 2048])
        ps_qk = psum("ps_qk", [P, 512])
        ps_kv = psum("ps_kv", [P, 512])
        ps_t = psum("ps_t", [P, 512])
        ps_s = psum("ps_s", [P, 512])
        ps_oo = ps_qk[:, 0:256].rearrange("p (h q) -> p h q", h=2)
        ps_y = ps_kv[:, 0:256]
        ps_lg = ps_kv[:, 256:256 + E]
        ps_tn = ps_t[:, 0:256].rearrange("p (k t) -> p k t", k=KD)
        ps_t2 = ps_t[:, 256:512].rearrange("p (k t) -> p k t", k=KD)

        x_in = sem("a_x_in")
        x_rest_in = sem("a_x_rest_in")
        zeroed = sem("a_zeroed")
        zeros = sb("a_zeros", [P, 8 * D])
        early = sem("a_early")
        t1_done = sem("a_t1")
        t1_out = sem("a_t1o")
        qk_done = sem("a_qk")
        kv_done = sem("a_kv")
        qk_out = sem("a_qko")
        kv_out = sem("a_kvo")
        qeo_done = sem("a_qeo_s")
        sc_done = sem("a_sc")
        st_done = sem("a_st")
        s_out = sem("a_so")
        stm_done = sem("a_stm_s")
        av_done = sem("a_av")
        o_out = sem("a_oo")
        y_done = sem("a_y")
        res_done = sem("a_res")
        xb_done = sem("a_xb")
        kept = sem("a_kept")
        t2_done = sem("a_t2")
        t2_out = sem("a_t2o")
        lg_done = sem("a_lg")
        lg_out = sem("a_lgo")
        block = ctx.enter_context(nc.Block())
        DEPTH = 6
        N_LOADS = 13

        @block.sync
        def _(sp):
            for c in range(8):
                sp.dma_start(x_res[:, 4 * c:4 * c + 4, :],
                             w["x"].rearrange("(t p) d -> p t d", p=P)[:, 4 * c:4 * c + 4, :]).then_inc(x_rest_in if c else x_in, 16)
                if c == 0:
                    w1 = w["W1"].rearrange("(k p) n -> p k n", p=P)
                    sp.dma_start(ident[:, :], w["c_ident"]).then_inc(loaded, 16)
                    sp.dma_start(w_qk[:, :, 0:256], w1[:, :, 256:512]).then_inc(loaded, 16)
                    sp.dma_start(w_qk[:, :, 256:512], w1[:, :, 0:256]).then_inc(loaded, 16)
                    sp.dma_start(w_kv[:, :, 0:256], w1[:, :, 0:256]).then_inc(loaded, 16)
                    sp.dma_start(w_kv[:, :, 256:512], w1[:, :, 512:768]).then_inc(loaded, 16)
                    sp.dma_start(b_qk[:, :], w["b_qk"]).then_inc(loaded, 16)
                    sp.dma_start(b_kv[:, :], w["b_kv"].partition_broadcast(P)).then_inc(loaded, 16)
                    sp.dma_start(b_o[:, :], w["b2"].partition_broadcast(P)).then_inc(loaded, 16)
                    sp.dma_start(w_o[:, :, :], w["W2"].rearrange("(k p) n -> p k n", p=P)).then_inc(loaded, 16)
                    sp.dma_start(w_r[:, :, :], w["w_rT"].rearrange("(k p) n -> p k n", p=P)).then_inc(loaded, 16)
                    sp.dma_start(causal[:, :], w["c_causal"]).then_inc(loaded, 16)
                    sp.dma_start(eo_mask[:, :], w["c_eo"]).then_inc(loaded, 16)
                    sp.dma_start(head_mask[:, :], w["c_head"]).then_inc(loaded, 16)

            n = load_route_constants(sp, consts, w, early)
            n += load_experts(sp, w13, w2, w, early)
            sp.wait_ge(zeroed, 4)
            n += zero_slots(sp, zeros, x_slots, early)
            sp.wait_ge(early, n)

        @block.gpsimd
        def _(pool):
            pool.memset(zeros[:, :], 0.0).then_inc(zeroed, 1)
            pool.memset(half[:, :], -0.5).then_inc(zeroed, 1)
            pool.memset(vpad[:, :, :, :, :], 0.0).then_inc(zeroed, 1)
            pool.memset(s_bd[:, :, :, :], 0.0).then_inc(zeroed, 1)
            pool.wait_ge(loaded, 16 * N_LOADS)
            pool.wait_ge(zeroed, 4)

            def step(i, par):
                t, q = i - 5, (par - 5) % 2
                if has(t, NT):
                    wait_apart(pool, loaded, ln2_moments_done, t + 1)
                    wait_apart(pool, loaded, ln2_done, t - 1)
                    pool.tensor_scalar(ln2_shifted[:, q, :], ln2_moments[:, q, 1:2], EPS, None,
                                       ALU.add).then_inc(ln2_shifted_done, 1)
                    wait_apart(pool, loaded, ln2_shifted_done, t + 1)
                    pool.tensor_tensor(ln2_rstd[:, q, :], ln2_shifted[:, q, :], half[:, :], ALU.pow).then_inc(ln2_rstd_done, 1)
                t, q = i, par
                if has(t, NT):
                    wait_apart(pool, loaded, ln1_moments_done, t + 1)
                    wait_apart(pool, loaded, ln1_done, t - 1)
                    pool.tensor_scalar(ln1_shifted[:, q, :], ln1_moments[:, q, 1:2], EPS, None,
                                       ALU.add).then_inc(ln1_shifted_done, 1)
                    wait_apart(pool, loaded, ln1_shifted_done, t + 1)
                    pool.tensor_tensor(ln1_rstd[:, q, :], ln1_shifted[:, q, :], half[:, :], ALU.pow).then_inc(ln1_rstd_done, 1)
                t = i - 1
                if has(t, NT):
                    wait_apart(pool, loaded, ln1_done, t + 1)
                    pool.tensor_tensor(tile_of(x_res, t), tile_of(x_res, t), b_o[:, :], ALU.add).then_inc(xb_done, 1)
                t, q = i - 2, (par - 2) % 2
                if has(t, NT):
                    wait_apart(pool, loaded, qk_out, t + 1)
                    wait_apart(pool, loaded, sc_done, t - 1)
                    pool.tensor_tensor(qeo[:, q], qkT[:, q, 0:2, :].unsqueeze(2).broadcast_to([P, 2, 2, P]),
                                       eo_mask[:, :].unsqueeze(1).unsqueeze(3).broadcast_to([P, 2, 2, P]),
                                       ALU.mult).then_inc(qeo_done, 1)
                t, q = i - 6, (par - 6) % 2
                if has(t, NT):
                    wait_apart(pool, loaded, ln2_done, t + 1)
                    pool.tensor_copy(tile_of(xn2_res, t), xn2[:, q, :]).then_inc(kept, 1)

            pipelined(pool, NT, DEPTH, step)

        @block.scalar
        def _(act):
            def step(i, par):
                t, q = i - 4, (par - 4) % 2
                if has(t, NT):
                    act.wait_ge(av_done, t + 1)
                    wait(act, y_done, t - 1)
                    act.activation(oT[:, q], ps_oo, ACT.Copy).then_inc(o_out, 1)
                t, q = i - 6, (par - 6) % 2
                if has(t, NT):
                    act.wait_ge(t2_done, t + 1)
                    wait(act, lg_done, t - 1)
                    act.activation(xn2T[:, q], ps_t2, ACT.Copy).then_inc(t2_out, 1)
                t, q = i - 1, (par - 1) % 2
                if has(t, NT):
                    act.wait_ge(t1_done, t + 1)
                    wait(act, kv_done, t - 1)
                    act.activation(xnT[:, q], ps_tn, ACT.Copy).then_inc(t1_out, 1)
                t = i - 6
                if has(t, NT):
                    act.wait_ge(lg_done, t + 1)
                    act.activation(tile_of(logits, t), ps_lg, ACT.Copy).then_inc(lg_out, 1)

            pipelined(act, NT, DEPTH, step)

        @block.vector
        def _(dve):
            dve.memset(w2[HB[2][1]:P, 2], 0.0)
            dve.wait_ge(loaded, 16 * N_LOADS)
            dve.wait_ge(zeroed, 4)

            def step(i, par):
                t, q = i - 5, (par - 5) % 2
                if has(t, NT):
                    dve.wait_ge(y_done, t + 1)
                    dve.wait_ge(xb_done, t + 1)
                    dve.tensor_tensor(tile_of(x_res, t), tile_of(x_res, t), ps_y, ALU.add).then_inc(res_done, 1)
                    wait_apart(dve, loaded, res_done, t + 1)
                    wait_apart(dve, loaded, ln2_done, t - 1)
                    dve.bn_stats(ln2_stats[:, q, :], tile_of(x_res, t)).then_inc(ln2_stats_done, 1)
                    wait_apart(dve, loaded, ln2_stats_done, t + 1)
                    dve.bn_aggr(ln2_moments[:, q, :], ln2_stats[:, q, :]).then_inc(ln2_moments_done, 1)
                t, q = i, par
                if has(t, NT):
                    if isinstance(t, int) and t == 0:
                        wait(dve, x_in, 16)
                    if isinstance(t, int) and t == 4:
                        wait(dve, x_rest_in, 16 * 7)
                    wait_apart(dve, loaded, ln1_done, t - 1)
                    dve.bn_stats(ln1_stats[:, q, :], tile_of(x_res, t)).then_inc(ln1_stats_done, 1)
                    wait_apart(dve, loaded, ln1_stats_done, t + 1)
                    dve.bn_aggr(ln1_moments[:, q, :], ln1_stats[:, q, :]).then_inc(ln1_moments_done, 1)
                t, q = i - 3, (par - 3) % 2
                if has(t, NT):
                    dve.wait_ge(st_done, t + 1)
                    wait(dve, av_done, t)
                    dve.tensor_tensor(s_bd[:, q], ps_s[:, 0:256].rearrange("p (h c) -> p h c", h=2),
                                      head_mask[:, :].unsqueeze(1).broadcast_to([P, 2, P]), ALU.mult).then_inc(s_out, 1)
                    dve.wait_ge(sc_done, t + 1)
                    dve.tensor_tensor(stm[:, :, :], ps_sc[:, :].rearrange("p (h q) -> p h q", h=16),
                                      causal[:, :].unsqueeze(1).broadcast_to([P, 16, P]), ALU.mult).then_inc(stm_done, 1)
                t, q = i, par
                if has(t, NT):
                    wait(dve, t1_done, t - 1)
                    dve.wait_ge(ln1_rstd_done, t + 1)
                    dve.tensor_scalar(xn[:, q, :], tile_of(x_res, t), ln1_moments[:, q, 0:1], ln1_rstd[:, q, :], ALU.subtract,
                                      ALU.mult).then_inc(ln1_done, 1)
                t, q = i - 5, (par - 5) % 2
                if has(t, NT):
                    wait(dve, t2_done, t - 1)
                    wait(dve, kept, t - 1)
                    dve.wait_ge(ln2_rstd_done, t + 1)
                    dve.tensor_scalar(xn2[:, q, :], tile_of(x_res, t), ln2_moments[:, q, 0:1], ln2_rstd[:, q, :], ALU.subtract,
                                      ALU.mult).then_inc(ln2_done, 1)
                t, q = i - 2, (par - 2) % 2
                if has(t, NT):
                    dve.wait_ge(qk_done, t + 1)
                    wait(dve, av_done, t - 1)
                    wait(dve, qeo_done, t - 1)
                    dve.tensor_tensor(qkT[:, q], ps_qk[:, :].rearrange("p (b t) -> p b t", b=4),
                                      b_qk[:, :].unsqueeze(2).broadcast_to([P, 4, P]), ALU.add).then_inc(qk_out, 1)
                    dve.wait_ge(kv_done, t + 1)
                    dve.tensor_tensor(k_tok[:, q, :], ps_kv[:, 0:256], b_kv[:, 0:256], ALU.add).then_inc(kv_out, 1)
                    for eo in range(2):
                        def part(ap):
                            return ap.rearrange("p (r e d) -> p r e d", e=2, d=16)[:, :, eo, :]
                        dve.tensor_tensor(vpad[:, q, :, eo, 16 * eo:16 * eo + 16], part(ps_kv[:, 256:512]),
                                          part(b_kv[:, 256:512]), ALU.add).then_inc(kv_out, 1)

            pipelined(dve, NT, DEPTH, step)

        @block.tensor
        def _(pe):
            pe.wait_ge(loaded, 16 * N_LOADS)
            pe.wait_ge(zeroed, 4)

            def step(i, par):
                t, q = i - 4, (par - 4) % 2
                if has(t, NT):
                    pe.wait_ge(stm_done, t + 1)
                    pe.wait_ge(kv_out, 3 * (t + 1))
                    wait(pe, s_out, t)
                    wait(pe, qk_out, t + 2, NT)
                    for h in range(2):
                        pe.matmul(ps_oo[:, h, :], s_bd[:, (q + 1) % 2, h, :], qkT[:, q, h, :], start=(h == 0),
                                  stop=False, skip_group_check=True)
                    for h in range(2):
                        for g in range(4):
                            for eo in range(2):
                                mm = pe.matmul(ps_oo[32 * g:32 * g + 32, h, :], vpad[:, q, 4 * h + g, eo, :],
                                               stm[:, 4 * g + 2 * h + eo, :], start=False,
                                               stop=(eo == 1), skip_group_check=True)
                    mm.then_inc(av_done, 1)
                t, q = i - 5, (par - 5) % 2
                if has(t, NT):
                    pe.wait_ge(o_out, t + 1)
                    wait(pe, kv_out, 3 * (t + 3), 3 * NT)
                    wait(pe, lg_out, t - 1)
                    for k in range(KD):
                        mm = pe.matmul(ps_y, oT[:, q, k, :], w_o[:, k, :], start=(k == 0), stop=(k == KD - 1))
                    mm.then_inc(y_done, 1)
                t, q = i - 6, (par - 6) % 2
                if has(t, NT):
                    pe.wait_ge(ln2_done, t + 1)
                    wait(pe, t1_out, t + 5, NT)
                    for k in range(KD):
                        mm = pe.transpose(ps_t2[:, k, :], xn2[:, q, k * P:(k + 1) * P], ident[:, :])
                    mm.then_inc(t2_done, 1)
                t, q = i - 3, (par - 3) % 2
                if has(t, NT):
                    pe.wait_ge(kv_out, 3 * (t + 1))
                    wait(pe, s_out, t)
                    for h in range(2):
                        v_own = vpad[:, q, 4 * h:4 * h + 4].rearrange("p r e (a d) -> p r (e a) d", d=16)[:, :, 0:4:3, :]
                        mm = pe.matmul(ps_s[:, h * P:(h + 1) * P], k_tok[:, q, h * P:(h + 1) * P], v_own,
                                       start=(isinstance(t, int) and t == 0 and h == 0),
                                       stop=True, skip_group_check=True)
                    mm.then_inc(st_done, 1)
                    pe.wait_ge(qeo_done, t + 1)
                    wait(pe, stm_done, t)
                    for h in range(2):
                        for g in range(4):
                            r = slice(32 * g, 32 * g + 32)
                            mm = pe.matmul(ps_sc[:, 512 * g + 256 * h:512 * g + 256 * h + 256], qkT[r, q, 2 + h, :],
                                           qeo[r, q, h].rearrange("p e q -> p (e q)"), start=True, stop=True)
                    mm.then_inc(sc_done, 1)

                t, q = i - 1, (par - 1) % 2
                if has(t, NT):
                    pe.wait_ge(ln1_done, t + 1)
                    wait(pe, t1_out, t)
                    wait(pe, t2_out, t - 4)
                    for k in range(KD):
                        mm = pe.transpose(ps_tn[:, k, :], xn[:, q, k * P:(k + 1) * P], ident[:, :])
                    mm.then_inc(t1_done, 1)
                t, q = i - 6, (par - 6) % 2
                if has(t, NT):
                    pe.wait_ge(t2_out, t + 1)
                    wait(pe, res_done, t + 2, NT)
                    for k in range(KD):
                        mm = pe.matmul(ps_lg, xn2T[:, q, k, :], w_r[:, k, :], start=(k == 0), stop=(k == KD - 1))
                    mm.then_inc(lg_done, 1)
                t, q = i - 2, (par - 2) % 2
                if has(t, NT):
                    pe.wait_ge(t1_out, t + 1)
                    wait(pe, o_out, t - 1)
                    for b in range(4):
                        for k in range(KD):
                            mm = pe.matmul(ps_qk[:, b * P:(b + 1) * P], w_qk[:, k, b * P:(b + 1) * P],
                                           xnT[:, q, k, :], start=(k == 0), stop=(k == KD - 1))
                    mm.then_inc(qk_done, 1)
                    wait(pe, res_done, t - 2)
                    wait(pe, lg_out, t - 3)
                    for k in range(KD):
                        mm = pe.matmul(ps_kv[:, :], xnT[:, q, k, :], w_kv[:, k, :], start=(k == 0), stop=(k == KD - 1))
                    mm.then_inc(kv_done, 1)
            pipelined(pe, NT, DEPTH, step)


def zero_slots(sp, zeros, x_slots, sem):
    for c in range(0, SLOT_TILES, 8):
        n = min(8, SLOT_TILES - c)
        sp.dma_start(x_slots.rearrange("(t p) d -> p t d", p=P)[:, c:c + n, :],
                     zeros[:, 0:n * D].rearrange("p (t d) -> p t d", d=D)).then_inc(sem, 16)
    return 16 * len(range(0, SLOT_TILES, 8))


def load_experts(sp, w13, w2, w, sem):
    for k in range(KD):
        for s, name in enumerate(("w1", "w3")):
            sp.dma_start(w13[:, s, k], w[name].rearrange("e (k p) h -> k p e h", p=P)[k]).then_inc(sem, 16)
    for b, (at, n) in enumerate(HB):
        sp.dma_start(w2[0:n, b], w["w2"][:, at:at + n, :].rearrange("e p d -> p e d")).then_inc(sem, 16)
    return 16 * 7


def route_constants(nc, ctx):
    def sb(name, shape):
        return ctx.enter_context(nc.sbuf_tensor("r_" + name, shape, F32))

    return {
        "ident": sb("ident", [P, P]), "strict": sb("strict", [P, P]), "ones": sb("ones", [P, P]), "prio": sb("prio", [P, E]),
        "follows": sb("follows", [P, E, NT]), "edges": sb("edges", [P, NT]), "numbers": sb("numbers", [P, SLOT_TILES]),
    }


def load_route_constants(sp, consts, w, sem):
    for name in ("ident", "strict", "ones"):
        sp.dma_start(consts[name][:, :], w["c_" + name]).then_inc(sem, 16)
    for name in ("prio", "edges", "numbers"):
        sp.dma_start(consts[name][:, :], w["c_" + name].partition_broadcast(P)).then_inc(sem, 16)
    sp.dma_start(consts["follows"][:, :, :], w["c_follows"].partition_broadcast(P)).then_inc(sem, 16)
    return 16 * 7


def route(nc, consts, xn2_res, logits, gates, slots, tile_expert, x_slots):
    with ExitStack() as ctx:
        def sb(name, shape, dt=F32):
            return ctx.enter_context(nc.sbuf_tensor(name, shape, dt))

        def sem(name):
            return ctx.enter_context(nc.semaphore(name))

        NS = SLOT_TILES
        strict = consts["strict"]
        ones = consts["ones"]
        prio = consts["prio"]
        follows = consts["follows"]
        edges = consts["edges"]
        numbers = consts["numbers"]
        top = sb("r_top", [P, NT])
        p = sb("r_p", [P, NT, E])
        inv = sb("r_inv", [P, NT])
        cand = sb("r_cand", [P, NT, E])
        hot = sb("r_hot", [P, 2, NT, E])
        both = sb("r_both", [P, NT, E])
        tot = sb("r_tot", [P, E, NT])
        incl = sb("r_incl", [P, E, NT])
        full = sb("r_full", [P, E, NT])
        tiles = sb("r_tiles", [P, E])
        ends = sb("r_ends", [P, E])
        place = sb("r_place", [P, NT, E])
        posf = sb("r_posf", [P, 2, NT])
        past = sb("r_past", [P, NS, E])
        tef = sb("r_tef", [P, NS])
        ps = ctx.enter_context(nc.psum_tensor("r_ps", [P, 512], F32))

        shifted = sem("r_shifted")
        exped = sem("r_exped")
        chosen = sem("r_chosen")
        counted = sem("r_counted")
        own = sem("r_own")
        placed = sem("r_placed")
        sent = sem("r_sent")
        block = ctx.enter_context(nc.Block())

        @block.scalar
        def _(act):
            act.wait_ge(shifted, 1)
            act.activation(p[:, :, :], p[:, :, :], ACT.Exp).then_inc(exped, 1)

        @block.tensor
        def _(pe):
            pe.wait_ge(chosen, 1)
            pe.matmul(ps[:, 0:NT * E], strict[:, :], both[:, :, :].rearrange("p t e -> p (t e)"), start=True, stop=True)
            pe.matmul(ps[:, 256:256 + NT * E], ones[:, :], both[:, :, :].rearrange("p t e -> p (t e)"), start=True,
                      stop=True).then_inc(counted, 1)

        @block.vector
        def _(dve):
            count = [0]

            def link(instruction):
                count[0] += 1
                instruction.then_inc(own, 1)
                dve.wait_ge(own, count[0])

            def wide(ap):
                return ap.unsqueeze(2).broadcast_to([P, NT, E])

            link(dve.tensor_reduce(top[:, :], logits[:, :, :], AX.X, ALU.max))
            dve.tensor_tensor(p[:, :, :], logits[:, :, :], wide(top[:, :]), ALU.subtract).then_inc(shifted, 1)
            dve.wait_ge(exped, 1)
            link(dve.tensor_reduce(inv[:, :], p[:, :, :], AX.X, ALU.add))
            link(dve.reciprocal(inv[:, :], inv[:, :]))
            link(dve.tensor_tensor(p[:, :, :], p[:, :, :], wide(inv[:, :]), ALU.mult))
            for s in range(2):
                gate = gates[:, s, :]
                link(dve.tensor_reduce(gate, p[:, :, :], AX.X, ALU.max))
                link(dve.tensor_tensor(cand[:, :, :], p[:, :, :], wide(gate), ALU.is_equal))
                link(dve.tensor_tensor(cand[:, :, :], cand[:, :, :], prio[:, :].unsqueeze(1).broadcast_to([P, NT, E]),
                                       ALU.mult))
                link(dve.tensor_reduce(top[:, :], cand[:, :, :], AX.X, ALU.max))
                link(dve.tensor_tensor(hot[:, s], cand[:, :, :], wide(top[:, :]), ALU.is_equal))
                if s == 0:
                    link(dve.scalar_tensor_tensor(p[:, :, :], hot[:, 0], -2.0, p[:, :, :], ALU.mult, ALU.add))
            dve.tensor_tensor(both[:, :, :], hot[:, 0], hot[:, 1], ALU.add).then_inc(chosen, 1)

            dve.wait_ge(counted, 1)
            link(dve.tensor_copy(tot[:, :, :].rearrange("p e t -> p t e"),
                                 ps[:, 256:512].rearrange("p (t e) -> p t e", e=E)))
            flat = [x[:, :, :].rearrange("p e t -> p (e t)") for x in (incl, follows, tot)]
            link(dve.tensor_tensor_scan(flat[0], flat[1], flat[2], 0.0, ALU.mult, ALU.add))
            link(dve.tensor_tensor(full[:, :, :], incl[:, :, NT - 1:NT].broadcast_to([P, E, NT]),
                                   edges[:, :].unsqueeze(1).broadcast_to([P, E, NT]), ALU.is_gt))
            link(dve.tensor_reduce(tiles[:, :], full[:, :, :], AX.X, ALU.add))
            link(dve.tensor_tensor_scan(ends[:, :], ones[:, 0:E], tiles[:, :], 0.0, ALU.mult, ALU.add))
            link(dve.tensor_tensor(tiles[:, :], ends[:, :], tiles[:, :], ALU.subtract))
            link(dve.tensor_tensor(incl[:, :, :], incl[:, :, :], tot[:, :, :], ALU.subtract))
            link(dve.scalar_tensor_tensor(incl[:, :, :], tiles[:, :].unsqueeze(2).broadcast_to([P, E, NT]), float(P),
                                          incl[:, :, :], ALU.mult, ALU.add))
            link(dve.tensor_tensor(place[:, :, :], ps[:, 0:256].rearrange("p (t e) -> p t e", e=E),
                                   incl[:, :, :].rearrange("p e t -> p t e"), ALU.add))
            for s in range(2):
                link(dve.tensor_tensor(cand[:, :, :], place[:, :, :], hot[:, s], ALU.mult))
                link(dve.tensor_reduce(posf[:, s, :], cand[:, :, :], AX.X, ALU.add))
            dve.tensor_copy(slots[:, :, :], posf[:, :, :]).then_inc(placed, 1)
            link(dve.tensor_tensor(past[:, :, :], numbers[:, :].unsqueeze(2).broadcast_to([P, NS, E]),
                                   ends[:, :].unsqueeze(1).broadcast_to([P, NS, E]), ALU.is_ge))
            link(dve.tensor_reduce(tef[:, :], past[:, :, :], AX.X, ALU.add))
            link(dve.tensor_scalar(tef[:, :], tef[:, :], float(E - 1), None, ALU.min))
            link(dve.tensor_copy(tile_expert[:, :], tef[:, :]))

        @block.gpsimd
        def _(pool):
            pool.wait_ge(placed, 1)
            for t in range(NT):
                for s in range(2):
                    pool.indirect_dma_start(
                        out=x_slots, out_offset=bass.IndirectOffsetOnAxis(ap=slots[:, s, t:t + 1], axis=0),
                        in_=xn2_res[:, t, :], in_offset=None).then_inc(sent, 16)
            pool.wait_ge(sent, 16 * 2 * NT)


def experts(nc, ident, kept, kept_loaded, tile_expert, x_slots, y_slots, w13, w2, w):
    with ExitStack() as ctx:
        def sb(name, shape, dt=F32):
            return ctx.enter_context(nc.sbuf_tensor(name, shape, dt))

        def psum(name):
            return ctx.enter_context(nc.psum_tensor(name, [P, 512], F32))

        def sem(name):
            return ctx.enter_context(nc.semaphore(name))

        x = sb("e_x", [P, 2, D])
        xT = sb("e_xT", [P, 2, KD, P])
        gate = sb("e_gate", [P, 2, HID])
        h = sb("e_h", [P, 2, 3 * P])
        hT = sb("e_hT", [P, 2, 3, P])
        y = sb("e_y", [P, 2, D])
        ps_x = psum("e_ps_x")
        ps_1 = [psum(f"e_ps_1{i}") for i in range(2)]
        ps_3 = [psum(f"e_ps_3{i}") for i in range(2)]
        ps_h = psum("e_ps_h")
        ps_y = psum("e_ps_y")
        zeroed = sem("e_zeroed")
        x_in = [sem(f"e_x_in{i}") for i in range(2)]
        xt_done = sem("e_xt_done")
        xt_out = sem("e_xt_out")
        h_done = sem("e_h_done")
        gate_done = sem("e_gate_done")
        h_out = sem("e_h_out")
        ht_done = sem("e_ht_done")
        ht_out = sem("e_ht_out")
        y_done = sem("e_y_done")
        y_out = sem("e_y_out")
        y_sent = [sem(f"e_y_sent{i}") for i in range(2)]
        block = ctx.enter_context(nc.Block())
        N = SLOT_TILES
        DEPTH = 4

        def rows(ap, t):
            return ap[bass.ds(t * P, P), :]

        @block.sync
        def _(sp):
            def step(i, par):
                t, q = i, par
                if has(t, N):
                    wait_apart(sp, zeroed, xt_done, t - 1)
                    sp.dma_start(x[:, q, :], rows(x_slots, t)).then_inc(x_in[q], 16)

            pipelined(sp, N, DEPTH, step)
            kept_loads = load_delta_weights(sp, kept, w, kept_loaded)
            sp.wait_ge(kept_loaded, kept_loads)

        @block.gpsimd
        def _(pool):
            pool.memset(h[:, :, :], 0.0).then_inc(zeroed, 1)

            def step(i, par):
                t, q = i - 4, par
                if has(t, N):
                    wait_apart(pool, zeroed, y_out, t + 1)
                    pool.dma_start(rows(y_slots, t), y[:, q, :]).then_inc(y_sent[q], 16)

            pipelined(pool, N, DEPTH, step)
            for q in range(2):
                pool.wait_ge(y_sent[q], 16 * ((N + 1 - q) // 2))

        @block.scalar
        def _(act):
            def step(i, par):
                t, q = i - 4, par
                if has(t, N):
                    act.wait_ge(y_done, t + 1)
                    wait(act, y_sent[q], 8 * (t - q))
                    act.activation(y[:, q, :], ps_y[:, 0:D], ACT.Copy).then_inc(y_out, 1)
                t, q = i - 1, 1 - par
                if has(t, N):
                    act.wait_ge(xt_done, t + 1)
                    wait(act, h_done, t - 1)
                    act.activation(xT[:, q], ps_x[:, 0:D].rearrange("p (k t) -> p k t", k=KD),
                                   ACT.Copy).then_inc(xt_out, 1)
                t, q = i - 2, par
                if has(t, N):
                    act.wait_ge(h_done, t + 1)
                    wait(act, h_out, t - 1)
                    act.activation(gate[:, q, :], ps_1[q][:, 0:HID], ACT.Silu).then_inc(gate_done, 1)

            pipelined(act, N, DEPTH, step)

        @block.vector
        def _(dve):
            dve.wait_ge(zeroed, 1)

            def step(i, par):
                t, q = i - 3, 1 - par
                if has(t, N):
                    dve.wait_ge(ht_done, t + 1)
                    wait(dve, y_done, t - 1)
                    dve.tensor_copy(hT[:, q], ps_h[:, 0:3 * P].rearrange("p (b t) -> p b t", b=3)).then_inc(ht_out, 1)
                t, q = i - 2, par
                if has(t, N):
                    dve.wait_ge(gate_done, t + 1)
                    wait(dve, ht_done, t - 1)
                    dve.tensor_tensor(h[:, q, 0:HID], gate[:, q, :], ps_3[q][:, 0:HID], ALU.mult).then_inc(h_out, 1)

            pipelined(dve, N, DEPTH, step)

        @block.tensor
        def _(pe):
            pe.wait_ge(zeroed, 1)

            def expert_of(t):
                return pe.value_load(tile_expert[0:1, bass.ds(t, 1)], min_val=0, max_val=E - 1)

            def step(i, par):
                e_out = expert_of(i - 4) if has(i - 4, N) else None
                e_hidden = expert_of(i - 2) if has(i - 2, N) else None
                t, q = i - 4, par
                if has(t, N):
                    pe.wait_ge(ht_out, t + 1)
                    wait(pe, y_out, t)
                    for b in range(3):
                        mm = pe.matmul(ps_y[:, 0:D], hT[:, q, b, :], w2[:, b, bass.ds(e_out, 1), :],
                                       start=(b == 0), stop=(b == 2))
                    mm.then_inc(y_done, 1)
                t, q = i - 3, 1 - par
                if has(t, N):
                    pe.wait_ge(h_out, t + 1)
                    wait(pe, ht_out, t)
                    for b in range(3):
                        mm = pe.transpose(ps_h[:, b * P:(b + 1) * P], h[:, q, b * P:(b + 1) * P], ident[:, :])
                    mm.then_inc(ht_done, 1)
                t, q = i - 1, 1 - par
                if has(t, N):
                    wait(pe, x_in[q], 8 * (t - q) + 16)
                    wait(pe, xt_out, t)
                    for k in range(KD):
                        mm = pe.transpose(ps_x[:, k * P:(k + 1) * P], x[:, q, k * P:(k + 1) * P], ident[:, :])
                    mm.then_inc(xt_done, 1)
                t, q = i - 2, par
                if has(t, N):
                    pe.wait_ge(xt_out, t + 1)
                    wait(pe, gate_done, t - 1)
                    wait(pe, h_out, t - 1)
                    for s, ps in enumerate((ps_1[q], ps_3[q])):
                        for k in range(KD):
                            mm = pe.matmul(ps[:, 0:HID], xT[:, q, k, :], w13[:, s, k, bass.ds(e_hidden, 1), :],
                                           start=(k == 0), stop=(k == KD - 1))
                    mm.then_inc(h_done, 1)

            pipelined(pe, N, DEPTH, step)


GROUP = 4
NG = NT // GROUP
GW = GROUP * P
CONV = 4
HIST = CONV - 1
SM = 36
PART = [0, 6, NG]
SUB = 16
REC = 5 * D


def delta_weights(nc, ctx):
    def sb(name, shape):
        return ctx.enter_context(nc.sbuf_tensor("d_" + name, shape, F32))

    return {
        "w_p": sb("w_p", [P, KD, 6 * P]), "w_dec": sb("w_dec", [P, KD, NH1]), "w_s": sb("w_s", [P, KD, SM]),
        "taps": sb("taps", [P, 6, CONV]), "taps_m": sb("taps_m", [NH1, CONV]), "mix_b": sb("mix_b", [P, NH1]),
        "ident": sb("ident", [P, P]), "pair_mask": sb("pair_mask", [P, 2]),
        "w_o": sb("w_o", [P, KD, D]), "rms": sb("rms", [P, 1]), "causal": sb("causal", [P, P]),
        "lower": sb("lower", [P, P]), "step16": sb("step16", [P, P]), "block16": sb("block16", [P, P // SUB]),
    }


def load_delta_weights(sp, kept, w, loaded):
    for n, name in enumerate(("Wq", "Wk", "Wv")):
        sp.dma_start(kept["w_p"][:, :, n * D:(n + 1) * D], w[name].rearrange("(k p) n -> p k n", p=P)).then_inc(loaded, 16)
    for n, name in enumerate(("conv_q", "conv_k", "conv_v")):
        sp.dma_start(kept["taps"][:, 2 * n:2 * n + 2, :], w[name].rearrange("(k p) n -> p k n", p=P)).then_inc(loaded, 16)
    for name, of in (("w_dec", "Wdec"), ("w_s", "w_small"), ("w_o", "Wo")):
        sp.dma_start(kept[name][:, :, :], w[of].rearrange("(k p) n -> p k n", p=P)).then_inc(loaded, 16)
    for name, of in (("taps_m", "conv_mix"), ("ident", "c_ident"), ("pair_mask", "c_pair"), ("causal", "c_causal"),
                     ("lower", "c_lower"), ("step16", "c_step16"), ("block16", "c_block16")):
        sp.dma_start(kept[name][:, :], w[of]).then_inc(loaded, 16)
    sp.dma_start(kept["mix_b"][:, :], w["mix_bias"].partition_broadcast(P)).then_inc(loaded, 16)
    for e in range(2):
        sp.dma_start(kept["rms"][DH * e:DH * e + DH, :], w["rms_w"]).then_inc(loaded, 16)
    return 16 * 19


def gate_weights(nc, ctx):
    def sb(name, shape):
        return ctx.enter_context(nc.sbuf_tensor("g_" + name, shape, F32))

    return {
        "w_g": sb("w_g", [P, KD, 3, D]), "u_g": sb("u_g", [P, KD, 3, D]),
        "b_g": sb("b_g", [P, 6]), "c0": sb("c0", [P, KD]),
        "w_o": sb("w_o", [P, KD, D]), "u_o": sb("u_o", [P, KD, D]), "b_o": sb("b_o", [P, D]),
    }


def load_gate_weights(sp, kept, w, loaded):
    for n, name in enumerate(("f", "i", "c")):
        sp.dma_start(kept["w_g"][:, :, n, :], w[f"w{name}T"].rearrange("(k p) n -> p k n", p=P)).then_inc(loaded, 16)
        sp.dma_start(kept["u_g"][:, :, n, :], w[f"u{name}T"].rearrange("(k p) n -> p k n", p=P)).then_inc(loaded, 16)
    sp.dma_start(kept["b_g"][:, :], w["b_gates"]).then_inc(loaded, 16)
    sp.dma_start(kept["c0"][:, :], w["c0"]).then_inc(loaded, 16)
    sp.dma_start(kept["w_o"][:, :, :], w["woT"].rearrange("(k p) n -> p k n", p=P)).then_inc(loaded, 16)
    sp.dma_start(kept["u_o"][:, :, :], w["uoT"].rearrange("(k p) n -> p k n", p=P)).then_inc(loaded, 16)
    sp.dma_start(kept["b_o"][:, :], w["bo"].partition_broadcast(P)).then_inc(loaded, 16)
    return 16 * 11


def inverses_in(got):
    return got[:, :, :, :, :].rearrange("p q j s d -> p (q j) (s d)")\
                             .rearrange("p g (i z c) -> p g i z c", i=SUB, z=2)


def send_inverses(eng, t_out, t_mat, u, s, sent):
    for h in range(NH1):
        r = 64 * s + 16 * h
        dst = t_mat[u * GW:(u + 1) * GW, :].rearrange("(b s i) (h c) -> s h b i c", s=2, i=SUB, h=NH1)
        eng.dma_start(dst[s, h], t_out[r:r + 16, u].rearrange("p i z c -> p i (z c)")).then_inc(sent, 16)


def delta_inputs(nc, kept, loaded, got, t_sent, x_res, gates, slots, y_slots, small, rec, l_mat, t_mat):
    with ExitStack() as ctx:
        def sb(name, shape, dt=F32):
            return ctx.enter_context(nc.sbuf_tensor("d_" + name, shape, dt))

        def psum(name):
            return ctx.enter_context(nc.psum_tensor("d_" + name, [P, 512], F32))

        def sem(name):
            return ctx.enter_context(nc.semaphore("d_" + name))

        w_p = kept["w_p"]
        w_dec = kept["w_dec"]
        w_g = sb("w_g", [P, KD, D])
        w_s = kept["w_s"]
        taps = kept["taps"]
        taps_m = kept["taps_m"]
        mix_b = kept["mix_b"]
        ident = kept["ident"]
        half = sb("half", [P, 8])
        pair_mask = kept["pair_mask"]

        idx = sb("idx", [P, 2, 2, GROUP], U32)
        stats = sb("stats", [P, GROUP, 6])
        mom = sb("mom", [P, GROUP, 2])
        shifted = sb("shifted", [P, GROUP])
        rstd = sb("rstd", [P, GROUP])
        xn = sb("xn", [P, 2, GROUP, D])
        xT = sb("xT", [P, KD, GW])
        cin = sb("cin", [P, 2, 6, HIST + GW])
        cout = sb("cout", [P, 6, GW])
        act_out = sb("act_out", [P, 2, 6, GW])
        dec_t = sb("dec_t", [P, 2, GW])
        dec = sb("dec", [P, 2, GW])
        ema = sb("ema", [P, 2, 2, GW])
        min_ = sb("min", [NH1, 2, HIST + GW])
        mtmp = sb("mtmp", [NH1, GW])
        sm_row = sb("sm_row", [SM, 2, GW])
        sm_t = sb("sm_t", [P, 2, GROUP, NH1])
        sm_m = sb("sm_m", [P, GROUP, NH1])
        sq = sb("sq", [P, 2, 512])
        ss = sb("ss", [P, 2, 8])
        ss_e = sb("ss_e", [P, 2, 8])
        rn = sb("rn", [P, 2, 8])
        qkn = sb("qkn", [P, GROUP, 512])
        ve = sb("ve", [P, GROUP, 512])
        bT = sb("bT", [P, GROUP, 4, P])
        k_eo = sb("k_eo", [P, 2, 2, 2, P])
        l32 = sb("l32", [P, GROUP, NH1, 32])
        l_in = sb("l_in", [P, NG, SUB, SUB])
        t_out = inverses_in(got)
        prod = xn[:, :, :, :].rearrange("p q j (b c) -> p (q j) b c", c=SUB)
        pp = [psum(f"pp{i}") for i in range(2)]
        ps_qk = [psum(f"ps_qk{i}") for i in range(2)]
        ps_ve = psum("ps_ve")
        ps_b = psum("ps_b")
        ps_g = [psum(f"ps_g{i}") for i in range(2)]

        zeroed = sem("zeroed")
        spread = sem("spread")
        idx_done = sem("idx_done")
        got_in = [sem(f"got_in{i}") for i in range(2)]
        first_done = sem("first_done")
        x_done = sem("x_done")
        stats_done = sem("stats_done")
        mom_done = sem("mom_done")
        shift_done = sem("shift_done")
        rstd_done = sem("rstd_done")
        norm_done = sem("norm_done")
        p_done = sem("p_done")
        p_out = sem("p_out")
        carried = sem("carried")
        conv_own = sem("conv_own")
        conv_done = sem("conv_done")
        silu_own = sem("silu_own")
        silu_done = sem("silu_done")
        dec_done = sem("dec_done")
        inp_done = sem("inp_done")
        ema_done = sem("ema_done")
        m_own = sem("m_own")
        mix_done = sem("mix_done")
        sm_done = sem("sm_done")
        sm_out = sem("sm_out")
        sm_add = sem("sm_add")
        sm_tanh = sem("sm_tanh")
        small_done = sem("small_done")
        tt_done = sem("tt_done")
        sq_done = sem("sq_done")
        ve_out = sem("ve_out")
        ss_done = sem("ss_done")
        sse_done = sem("sse_done")
        rn_done = sem("rn_done")
        qkn_done = sem("qkn_done")
        bt_done = sem("bt_done")
        bt_out = sem("bt_out")
        g_done = sem("g_done")
        g_out = sem("g_out")
        sent = [sem(f"sent{i}") for i in range(GROUP)]
        l_sent = [sem(f"l_sent{i}") for i in range(GROUP)]
        l_back = [sem(f"l_back{i}") for i in range(2)]
        unit = sem("unit")
        sub_own = sem("sub_own")
        sub_done = sem("sub_done")
        block = ctx.enter_context(nc.Block())
        DEPTH = 3
        ORDER = [4, 5, "g0", "g1", "s", 0, 1, 2, 3]
        USES = 2 + len(ORDER)

        @block.sync
        def _(sp):
            def step(i, par):
                u = i - 2
                if has(u, NG):
                    for j in range(GROUP):
                        t = GROUP * u + j
                        row = rec[bass.ds(t * P, P), :]
                        wait_apart(sp, loaded, ve_out, t + 1)
                        sp.dma_start(row[:, D:3 * D], ve[:, j, :]).then_inc(sent[j], 16)
                        wait_apart(sp, loaded, qkn_done, t + 1)
                        sp.dma_start(row[:, 0:D], qkn[:, j, D:2 * D]).then_inc(sent[j], 16)
                        wait_apart(sp, loaded, bt_out, t + 1)
                        sp.dma_start(row[:, 3 * D:5 * D], bT[:, j].rearrange("p b t -> p (b t)")).then_inc(sent[j], 16)
                        wait_apart(sp, loaded, g_out, 4 * (t + 1))
                        sp.dma_start(l_mat[bass.ds(t * P, P), :], l32[:, j].rearrange("p h c -> p (h c)")).then_inc(l_sent[j], 16)
                u = i - 2
                if has(u, NG):
                    for j in range(GROUP):
                        wait_apart(sp, loaded, l_sent[j], 16 * (u + 1))
                    back = l_back[1 if isinstance(u, int) and u >= PART[1] else 0]
                    for s in range(2):
                        for h in range(NH1):
                            r = 64 * s + 16 * h
                            src = l_mat[bass.ds(u * GW, GW), :].rearrange("(b s i) (h z c) -> s h z b i c", s=2, i=SUB, h=NH1, z=2)
                            sp.dma_start(l_in[r:r + 16, bass.ds(u, 1)].rearrange("p a i c -> p (a i) c"),
                                         src[s, h, s]).then_inc(back, 16)

            pipelined(sp, NG, DEPTH, step, ahead=1)
            sp.wait_ge(sub_done, 1)
            for u in range(PART[1]):
                send_inverses(sp, t_out, t_mat, u, 0, t_sent[0])
            for j in range(GROUP):
                sp.wait_ge(sent[j], 48 * NG)
            sp.wait_ge(t_sent[0], 16 * 8 * PART[1])

        @block.gpsimd
        def _(pool):
            def gather(u, q, tiles):
                if tiles[0] == 0:
                    wait_apart(pool, loaded, x_done, GROUP * (u - 1))
                    pool.tensor_copy(idx[:, q], slots[:, :, bass.ds(GROUP * u, GROUP)]).then_inc(idx_done, 1)
                    wait_apart(pool, loaded, idx_done, u + 1)
                for j in tiles:
                    for s in range(2):
                        pool.indirect_dma_start(
                            out=got[:, q, j, s, :], out_offset=None, in_=y_slots,
                            in_offset=bass.IndirectOffsetOnAxis(ap=idx[:, q, s, j:j + 1], axis=0)).then_inc(got_in[q], 16)

            gather(0, 0, (0, 1, 2, 3))
            pool.memset(half[:, :], -0.5).then_inc(zeroed, 1)
            pool.memset(cin[:, :, :, 0:HIST], 0.0).then_inc(zeroed, 1)
            pool.memset(min_[:, :, 0:HIST], 0.0).then_inc(zeroed, 1)
            pool.memset(sm_row[:, :, :], 0.0).then_inc(zeroed, 1)
            pool.wait_ge(zeroed, 4)

            def root(t, q):
                wait_apart(pool, loaded, ss_done, t + 1)
                wait_apart(pool, loaded, qkn_done, t - 1)
                pool.tensor_scalar(ss_e[:, q, :], ss[:, q, :], 1e-6, None, ALU.add).then_inc(sse_done, 1)
                wait_apart(pool, loaded, sse_done, t + 1)
                pool.tensor_tensor(rn[:, q, :], ss_e[:, q, :], half[:, :], ALU.pow).then_inc(rn_done, 1)

            def mix_conv(u, q):
                m_in, m_out, m_one = min_[:, q], sm_row[0:NH1, q, :], mtmp[:, :]
                wait_apart(pool, loaded, p_out, USES * u + 2 + 5)
                wait_apart(pool, loaded, sm_done, u - 1)
                pool.tensor_scalar(m_out, m_in[:, 0:GW], taps_m[:, 0:1], None, ALU.mult).then_inc(m_own, 1)
                for c in range(1, CONV):
                    wait_apart(pool, loaded, m_own, 7 * u + 2 * c - 1)
                    pool.tensor_scalar(m_one, m_in[:, c:c + GW], taps_m[:, c:c + 1], None, ALU.mult).then_inc(m_own, 1)
                    wait_apart(pool, loaded, m_own, 7 * u + 2 * c)
                    pool.tensor_tensor(m_out, m_out, m_one, ALU.add).then_inc(m_own, 1)
                wait_apart(pool, loaded, m_own, 7 * u + 7)
                pool.tensor_copy(min_[:, 1 - q, 0:HIST], m_in[:, GW:GW + HIST]).then_inc(mix_done, 1)

            def step(i, par):
                u, q = i - 1, (par - 1) % 2
                t = GROUP * (i - 2)
                tiles = has(i - 2, NG)
                if tiles:
                    root(t, 0)
                if has(i + 1, NG):
                    gather(i + 1, 1 - par, (0,))
                if tiles:
                    root(t + 1, 1)
                if has(i, NG):
                    wait_apart(pool, loaded, mom_done, GROUP * (i + 1))
                    wait_apart(pool, loaded, norm_done, GROUP * i)
                    pool.tensor_scalar(shifted[:, :], mom[:, :, 1], EPS, None, ALU.add).then_inc(shift_done, 1)
                    wait_apart(pool, loaded, shift_done, i + 1)
                    pool.tensor_tensor(rstd[:, :], shifted[:, :], half[:, 0:GROUP], ALU.pow).then_inc(rstd_done, 1)
                if has(i + 1, NG):
                    gather(i + 1, 1 - par, (1,))
                if tiles:
                    root(t + 2, 0)
                if has(u, NG):
                    wait_apart(pool, loaded, p_out, USES * u + 6)
                    wait_apart(pool, loaded, ema_done, 2 * u)
                    pool.tensor_scalar(dec[:, :, :], dec_t[:, :, :], 0.5, 0.5, ALU.mult, ALU.add).then_inc(dec_done, 1)
                if tiles:
                    root(t + 3, 1)
                if has(i + 1, NG):
                    gather(i + 1, 1 - par, (2, 3))
                if isinstance(i, int) and i == NG:
                    pool.wait_ge(x_done, NT)
                    pool.memset(t_out, 0.0).then_inc(unit, 1)
                    pool.wait_ge(unit, 1)
                    pool.memset(t_out.rearrange("p g i z c -> p g (i z c)")[:, :, 0:2 * SUB * SUB:2 * SUB + 1], 1.0)\
                        .then_inc(unit, 1)
                if has(u, NG):
                    wait_apart(pool, loaded, p_out, USES * (u + 1))
                    wait_apart(pool, loaded, conv_done, 6 * u)
                    pool.tensor_copy(cin[:, 1 - q, :, 0:HIST], cin[:, q, :, GW:GW + HIST]).then_inc(carried, 1)
                    mix_conv(u, q)

            pipelined(pool, NG, DEPTH, step, ahead=1)

        @block.scalar
        def _(act):

            def step(i, par):
                u, q = i - 1, (par - 1) % 2
                here = has(u, NG)
                v, r = i - 2, (par - 2) % 2
                tiles = has(v, NG)

                def use(n):
                    bank = pp[n % 2]
                    act.wait_ge(p_done, USES * u + n + 1)
                    if n < 2:
                        wait(act, p_done, USES * u)
                        act.activation(xT[:, n, :], bank[:, :], ACT.Copy).then_inc(p_out, 1)
                        return
                    what = ORDER[n - 2]
                    if what == "s":
                        wait(act, sm_done, u - 1)
                        wait(act, mix_done, u)
                        act.activation(sm_row[32:SM, q, :], bank[32:SM, :], ACT.Copy)
                        act.activation(min_[:, q, HIST:], bank[0:NH1, :], ACT.Copy).then_inc(p_out, 1)
                    elif isinstance(what, str):
                        wait(act, ema_done, 2 * u)
                        act.activation(dec_t[:, int(what[1]), :], bank[:, :], ACT.Tanh, scale=0.5).then_inc(p_out, 1)
                    else:
                        wait(act, conv_done, 6 * (u - 1))
                        wait(act, carried, u - 1)
                        act.activation(cin[:, q, what, HIST:], bank[:, :], ACT.Copy)
                        n = (2, 3, 4, 5, 0, 1)[what]
                        wait(act, silu_done, 6 * (u - 1) + n + 1)
                        act.activation(cout[:, what, :], bank[:, :], ACT.Copy, scale=taps[:, what, HIST:CONV]).then_inc(p_out, 1)

                def silu(u, q, b):
                    n = {4: 0, 5: 1, 0: 2, 1: 3, 2: 4, 3: 5}[b]
                    act.wait_ge(conv_done, 6 * u + n + 1)
                    if b >= 4:
                        wait(act, ema_done, 2 * (u - 1))
                    wait(act, tt_done, GROUP * (u - 1))
                    if b < 4:
                        act.activation(act_out[:, q, b, :], cout[:, b, :], ACT.Silu).then_inc(silu_own, 1)
                        wait(act, silu_own, 4 * u + n - 1)
                        act.activation(act_out[:, q, b, :], act_out[:, q, b, :], ACT.Silu).then_inc(silu_done, 1)
                    else:
                        act.activation(act_out[:, q, b, :], cout[:, b, :], ACT.Silu).then_inc(silu_done, 1)

                def squares(j):
                    t, s = GROUP * v + j, j % 2
                    act.wait_ge(tt_done, t + 1)
                    wait(act, ss_done, t - 1)
                    act.activation(sq[:, s, :], ps_qk[s][:, :], ACT.Square).then_inc(sq_done, 1)
                    wait(act, sent[j], 48 * v)
                    act.activation(ve[:, j, 0:D], ps_ve[:, 0:D], ACT.Copy)
                    act.activation(ve[:, j, D:2 * D], ps_ve[:, D:2 * D], ACT.Copy, scale=-0.5).then_inc(ve_out, 1)

                def back(j):
                    t, s = GROUP * v + j, j % 2
                    act.wait_ge(bt_done, t + 1)
                    wait(act, sent[j], 48 * v)
                    wait(act, g_done, t - 1)
                    for e in range(2):
                        act.activation(k_eo[:, s, :, e, :], ps_b[:, 2 * P:].rearrange("p (b t) -> p b t", b=2),
                                       ACT.Copy, scale=pair_mask[:, e:e + 1])
                    act.activation(bT[:, j], ps_b[:, :].rearrange("p (b t) -> p b t", b=4), ACT.Copy).then_inc(bt_out, 1)

                if here:
                    use(0)
                    use(1)
                if tiles:
                    silu(v, r, 2)
                if here:
                    use(2)
                    use(3)
                if tiles:
                    silu(v, r, 3)
                    squares(0)
                    squares(1)
                if here:
                    use(4)
                    use(5)
                if tiles:
                    back(0)
                if here:
                    use(6)
                if tiles:
                    ps_s = ps_b[:, 0:GROUP * SM].rearrange("p (j c) -> p j c", c=SM)
                    act.wait_ge(sm_done, v + 1)
                    wait(act, small_done, 2 * v)
                    act.activation(sm_t[:, 0], ps_s[:, :, 32:SM], ACT.Tanh, scale=0.5)
                    act.activation(sm_m[:, :, :], ps_s[:, :, 0:NH1], ACT.Silu).then_inc(sm_out, 1)
                if here:
                    silu(u, q, 4)
                if tiles:
                    squares(2)
                    back(1)
                if here:
                    use(7)
                    silu(u, q, 5)
                if tiles:
                    act.wait_ge(sm_add, v + 1)
                    act.activation(sm_t[:, 1], sm_m[:, :, :], ACT.Tanh, scale=0.5).then_inc(sm_tanh, 1)
                    squares(3)
                if here:
                    use(8)
                if tiles:
                    back(2)
                if here:
                    use(9)
                    silu(u, q, 0)
                if tiles:
                    back(3)
                if here:
                    use(10)
                    silu(u, q, 1)

            pipelined(act, NG, DEPTH, step)
            act.wait_ge(sub_done, 1)
            for u in range(PART[1]):
                send_inverses(act, t_out, t_mat, u, 1, t_sent[0])

        @block.vector
        def _(dve):
            dve.tensor_copy(w_g[:, :, :].rearrange("p k (h c) -> p k h c", h=NH1),
                            w_dec[:, :, :].unsqueeze(3).broadcast_to([P, KD, NH1, DH])).then_inc(spread, 1)
            dve.wait_ge(zeroed, 4)

            def rows(n, lo, hi):
                groups = slice(PART[n], PART[n + 1])
                count = PART[n + 1] - PART[n]
                inv = t_out[:, groups, :, 0, :]
                if lo == 1:
                    dve.wait_ge(unit, 2)
                    dve.wait_ge(p_done, USES * (NG - 1) + 2)
                    dve.wait_ge(l_back[n], 16 * 8 * count)
                for row in range(lo, hi):
                    if row > 1:
                        dve.wait_ge(sub_own, 30 * n + 2 * (row - 1))
                    a = prod[:, 0:count, 0:row, 0:row]
                    dve.tensor_tensor(a, l_in[:, groups, row:row + 1, 0:row].broadcast_to([P, count, row, row]),
                                      inv[:, :, 0:row, 0:row].rearrange("p g j k -> p g k j"), ALU.mult).then_inc(sub_own, 1)
                    dve.wait_ge(sub_own, 30 * n + 2 * row - 1)
                    dve.tensor_reduce(inv[:, :, row, 0:row], a, AX.X, ALU.add).then_inc(sub_own, 1)
                if hi == SUB:
                    dve.wait_ge(sub_own, 30 * (n + 1))
                    dve.tensor_copy(t_out[:, groups, :, 1, :], inv.rearrange("p g i c -> p g c i")).then_inc(sub_done, 1)

            def add_experts(i, par, j):
                t = GROUP * i + j
                x = tile_of(x_res, t)
                if j == 0:
                    wait(dve, got_in[par], 16 * 8 * ((i - par) // 2 + 1) if isinstance(i, int) else 64 * (i - par) + 128)
                for s in range(2):
                    dve.scalar_tensor_tensor(out=x, in0=got[:, par, j, s, :], scalar=gates[:, s, bass.ds(t, 1)],
                                             in1=x, op0=ALU.mult, op1=ALU.add).then_inc((first_done, x_done)[s], 1)
                    wait_apart(dve, loaded, (first_done, x_done)[s], t + 1)
                wait_apart(dve, loaded, norm_done, GROUP * i)
                dve.bn_stats(stats[:, j, :], x).then_inc(stats_done, 1)
                wait_apart(dve, loaded, stats_done, t + 1)
                dve.bn_aggr(mom[:, j, :], stats[:, j, :]).then_inc(mom_done, 1)

            def step(i, par):
                u, q = i - 1, (par - 1) % 2
                here = has(u, NG)
                v, r = i - 2, (par - 2) % 2
                tiles = has(v, NG)
                last = isinstance(i, int) and i == NG + 1

                def conv(b):
                    n = {4: 0, 5: 1, 0: 2, 1: 3, 2: 4, 3: 5}[b]
                    use = 2 + ORDER.index(b)
                    dve.wait_ge(p_out, USES * u + use + 1)
                    wait(dve, carried, u)
                    x = cin[:, q, b]
                    for c in range(HIST):
                        if c:
                            wait(dve, conv_own, 12 * u + 2 * n + c)
                        dve.scalar_tensor_tensor(out=cout[:, b, :], in0=x[:, c:c + GW], scalar=taps[:, b, c:c + 1],
                                                 in1=cout[:, b, :], op0=ALU.mult, op1=ALU.add)\
                           .then_inc(conv_own if c < HIST - 1 else conv_done, 1)

                def sums(j):
                    t, s = GROUP * v + j, j % 2
                    dve.wait_ge(sq_done, t + 1)
                    wait(dve, sse_done, t - 1)
                    dve.tensor_reduce(ss[:, s, :], sq[:, s, :].rearrange("p (h c) -> p h c", h=8), AX.X,
                                      ALU.add).then_inc(ss_done, 1)

                def scale(j):
                    t, s = GROUP * v + j, j % 2
                    dve.wait_ge(rn_done, t + 1)
                    wait(dve, bt_done, t - 1)
                    wait(dve, sent[j], 48 * v)
                    dve.tensor_tensor(qkn[:, j, :].rearrange("p (h c) -> p h c", h=8),
                                      ps_qk[s][:, :].rearrange("p (h c) -> p h c", h=8),
                                      rn[:, s, :].unsqueeze(2).broadcast_to([P, 8, DH]), ALU.mult).then_inc(qkn_done, 1)

                def blocks(j):
                    t, s = GROUP * v + j, j % 2
                    dve.wait_ge(g_done, t + 1)
                    dve.wait_ge(small_done, 2 * v + 1)
                    wait(dve, l_sent[j], 16 * v)
                    for k in range(4):
                        rows = slice(32 * k, 32 * k + 32)
                        nb = small[rows, bass.ds(t, 1), 2 * NH1:3 * NH1].rearrange("p a h -> p (a h)")
                        dve.tensor_tensor(l32[rows, j], nb.unsqueeze(2).broadcast_to([32, NH1, 32]),
                                          ps_g[s][rows, :].rearrange("p (h c) -> p h c", h=NH1)[:, :, rows],
                                          ALU.mult).then_inc(g_out, 1)

                if has(i, NG):
                    for j in range(GROUP):
                        add_experts(i, par, j)
                if tiles:
                    sums(0)
                if last:
                    rows(0, 1, 6)
                if here:
                    conv(4)
                if tiles:
                    scale(0)
                    sums(1)
                if last:
                    rows(0, 6, 9)
                if here:
                    conv(5)
                if tiles:
                    scale(1)
                    sums(2)
                if last:
                    rows(0, 9, 11)
                if tiles:
                    dve.wait_ge(sm_out, v + 1)
                    sm = small[:, bass.ds(GROUP * v, GROUP), :]
                    dve.tensor_scalar(sm[:, :, 0:NH1], sm_t[:, 0], 0.5, 0.5, ALU.mult, ALU.add)
                    dve.tensor_scalar(sm[:, :, 2 * NH1:3 * NH1], sm_t[:, 0], -0.5, -0.5, ALU.mult, ALU.add).then_inc(small_done, 1)
                    dve.tensor_tensor(sm_m[:, :, :], sm_m[:, :, :], mix_b[:, :].unsqueeze(1).broadcast_to([P, GROUP, NH1]),
                                      ALU.add).then_inc(sm_add, 1)
                    blocks(0)
                    scale(2)
                    sums(3)
                if last:
                    rows(0, 11, 13)
                if here:
                    conv(0)
                if has(i, NG):
                    dve.wait_ge(rstd_done, i + 1)
                    wait(dve, p_done, USES * (i - 2) + 2)
                    for j in range(GROUP):
                        dve.tensor_scalar(xn[:, par, j, :], tile_of(x_res, GROUP * i + j), mom[:, j, 0:1], rstd[:, j:j + 1],
                                          ALU.subtract, ALU.mult).then_inc(norm_done, 1)
                if tiles:
                    dve.wait_ge(sm_tanh, v + 1)
                    dve.tensor_scalar(sm[:, :, NH1:2 * NH1], sm_t[:, 1], 0.5, 0.5, ALU.mult, ALU.add).then_inc(small_done, 1)
                    blocks(1)
                    scale(3)
                if here:
                    dve.wait_ge(dec_done, u + 1)
                    dve.wait_ge(silu_done, 6 * u + 2)
                    dve.scalar_tensor_tensor(out=dec_t[:, :, :], in0=dec_t[:, :, :], scalar=1.0, in1=act_out[:, q, 4:6, :],
                                             op0=ALU.subtract, op1=ALU.mult).then_inc(inp_done, 1)
                    dve.wait_ge(inp_done, u + 1)
                    wait(dve, tt_done, GROUP * (u - 1))
                    wait(dve, ema_done, 2 * u)
                    for b in range(2):
                        first = isinstance(u, int) and u == 0
                        dve.tensor_tensor_scan(ema[:, q, b, :], dec[:, b, :], dec_t[:, b, :],
                                               0.0 if first else ema[:, 1 - q, b, GW - 1:GW], ALU.mult, ALU.add)\
                           .then_inc(ema_done, 1)
                    conv(1)
                if tiles:
                    blocks(2)
                if here:
                    conv(2)
                if tiles:
                    blocks(3)
                if here:
                    conv(3)
                if last:
                    rows(0, 13, SUB)
                if isinstance(i, int) and i == NG + 2:
                    rows(1, 1, SUB)

            pipelined(dve, NG, DEPTH, step)

        @block.tensor
        def _(pe):
            pe.wait_ge(spread, 1)
            pe.wait_ge(zeroed, 4)

            def step(i, par):
                u, q = i - 1, (par - 1) % 2
                here = has(u, NG)
                v, r = i - 2, (par - 2) % 2
                tiles = has(v, NG)

                def use(n):
                    bank = pp[n % 2]
                    wait(pe, p_out, USES * u + (n - 1 if n else 0))
                    if n < 2:
                        pe.wait_ge(norm_done, GROUP * (u + 1))
                        for j in range(GROUP):
                            mm = pe.transpose(bank[:, j * P:(j + 1) * P], xn[:, q, j, n * P:(n + 1) * P], ident[:, :])
                        mm.then_inc(p_done, 1)
                        return
                    what = ORDER[n - 2]
                    pe.wait_ge(p_out, USES * u + 2)
                    for k in range(KD):
                        if what == "s":
                            lhs, out = w_s[:, k, :], bank[0:SM, :]
                        elif isinstance(what, str):
                            lhs, out = w_g[:, k, int(what[1]) * P:(int(what[1]) + 1) * P], bank[:, :]
                        else:
                            lhs, out = w_p[:, k, what * P:(what + 1) * P], bank[:, :]
                        mm = pe.matmul(out, lhs, xT[:, k, :], start=(k == 0), stop=(k == KD - 1))
                    mm.then_inc(p_done, 1)

                def to_tokens(j):
                    t, s = GROUP * v + j, j % 2
                    pe.wait_ge(silu_done, 6 * (v + 1))
                    pe.wait_ge(ema_done, 2 * (v + 1))
                    wait(pe, qkn_done, t - 1)
                    cols = slice(j * P, (j + 1) * P)
                    for b in range(4):
                        pe.transpose(ps_qk[s][:, b * P:(b + 1) * P], act_out[:, r, b, cols], ident[:, :])
                    wait(pe, ve_out, t)
                    for b in range(2):
                        pe.transpose(ps_ve[:, b * P:(b + 1) * P], act_out[:, r, 4 + b, cols], ident[:, :])
                    for b in range(2):
                        mm = pe.transpose(ps_ve[:, (2 + b) * P:(3 + b) * P], ema[:, r, b, cols], ident[:, :])
                    mm.then_inc(tt_done, 1)

                def back(j):
                    t, s = GROUP * v + j, j % 2
                    pe.wait_ge(qkn_done, t + 1)
                    wait(pe, bt_out, t)
                    if j == 1:
                        pe.wait_ge(sm_out, v + 1)
                    for b in range(4):
                        mm = pe.transpose(ps_b[:, b * P:(b + 1) * P], qkn[:, j, b * P:(b + 1) * P], ident[:, :])
                    mm.then_inc(bt_done, 1)

                def gram(j):
                    t, s = GROUP * v + j, j % 2
                    pe.wait_ge(bt_out, t + 1)
                    wait(pe, g_out, 4 * (t - 1))
                    for p in range(2):
                        mm = pe.matmul(ps_g[s][:, 256 * p:256 * (p + 1)], bT[:, j, 2 + p, :],
                                       k_eo[:, s, p].rearrange("p e t -> p (e t)"), start=True, stop=True)
                    mm.then_inc(g_done, 1)

                if here:
                    use(0)
                    use(1)
                    use(2)
                    use(3)
                if tiles:
                    to_tokens(0)
                    to_tokens(1)
                if here:
                    use(4)
                    use(5)
                if tiles:
                    back(0)
                if here:
                    use(6)
                if tiles:
                    wait_apart(pe, loaded, mix_done, v + 1)
                    wait_apart(pe, loaded, bt_out, GROUP * v + 1)
                    for j in range(GROUP):
                        mm = pe.transpose(ps_b[:, j * SM:(j + 1) * SM], sm_row[:, r, j * P:(j + 1) * P], ident[0:SM, 0:SM])
                    mm.then_inc(sm_done, 1)
                    to_tokens(2)
                    gram(0)
                    back(1)
                if here:
                    use(7)
                if tiles:
                    to_tokens(3)
                    gram(1)
                if here:
                    use(8)
                if tiles:
                    back(2)
                if here:
                    use(9)
                if tiles:
                    gram(2)
                    back(3)
                if here:
                    use(10)
                if tiles:
                    gram(3)

            pipelined(pe, NG, DEPTH, step)


def delta_rule(nc, kept, gate_kept, loaded, got, t_sent, x_res, small, rec, t_mat, w):
    with ExitStack() as ctx:
        def sb(name, shape, dt=F32):
            return ctx.enter_context(nc.sbuf_tensor("u_" + name, shape, dt))

        def psum(name):
            return ctx.enter_context(nc.psum_tensor("u_" + name, [P, 512], F32))

        def sem(name):
            return ctx.enter_context(nc.semaphore("u_" + name))

        H = NH1
        w_o = kept["w_o"]
        rms = kept["rms"]
        ident = kept["ident"]
        causal = kept["causal"]
        lower = kept["lower"]
        step16 = kept["step16"]
        block16 = kept["block16"]
        half = sb("half", [P, H])

        kve = sb("kve", [P, 4, 3, D])
        qkT = sb("qkT", [P, 4, 4, P])
        eo = sb("eo", [P, 4, 4, 2, P])
        x16 = sb("x16", [P, 4, H, 2, SUB])
        X = sb("X", [P, 2, H, P])
        XT = sb("XT", [P, 2, H, P])
        kb = sb("kb", [P, 2, D])
        vb = sb("vb", [P, 2, H, P])
        L = sb("L", [P, H, P])
        stm = sb("stm", [P, 2, H, P])
        Z = [sb(f"Z{n}", [P, H, P]) for n in range(3)]
        wT = sb("wT", [P, 2, P])
        u = sb("u", [P, H, P])
        S = sb("S", [P, 2, 2, P])
        diff = sb("diff", [P, D])
        mixed = sb("mixed", [P, D])
        o2 = sb("o2", [P, D])
        sq = sb("sq", [P, D])
        ss = sb("ss", [P, H])
        ms = sb("ms", [P, H])
        rn = sb("rn", [P, H])
        o3 = sb("o3", [P, 2, D])
        oT = sb("oT", [P, KD, P])
        b_z, b_x, b_xt, b_w, b_u, b_o, b_s, b_y = [psum(f"bank{n}") for n in range(8)]

        def heads(ap):
            return ap[:, :].rearrange("p (h c) -> p h c", h=H)

        gates_loaded = sem("gates_loaded")
        zeroed = sem("zeroed")
        scaled = sem("scaled")
        eo_zeroed = sem("eo_zeroed")
        rec_in = [sem(f"rec_in{k}") for k in range(4)]
        x0_done = sem("x0_done")
        kb_done = sem("kb_done")
        vb_done = sem("vb_done")
        g_done = sem("g_done")
        l_done = sem("l_done")
        st_done = sem("st_done")
        stm_done = sem("stm_done")
        z_done = sem("z_done")
        z_out = sem("z_out")
        x_done = sem("x_done")
        x_out = sem("x_out")
        xt_done = sem("xt_done")
        xt_out16 = sem("xt_out16")
        xt_out = sem("xt_out")
        w_done = sem("w_done")
        w_out = sem("w_out")
        u_done = sem("u_done")
        u_out = sem("u_out")
        s_done = sem("s_done")
        s_out = sem("s_out")
        o_done = sem("o_done")
        diff_done = sem("diff_done")
        mixed_done = sem("mixed_done")
        o2_done = sem("o2_done")
        sq_done = sem("sq_done")
        ss_done = sem("ss_done")
        ms_done = sem("ms_done")
        rn_done = sem("rn_done")
        o3_done = sem("o3_done")
        ot_done = sem("ot_done")
        ot_out = sem("ot_out")
        y_done = sem("y_done")
        y_out = sem("y_out")
        block = ctx.enter_context(nc.Block())
        DEPTH = 4

        @block.sync
        def _(sp):
            sp.wait_ge(eo_zeroed, 1)

            def step(i, k):
                t = i
                if isinstance(t, int) and t == 4:
                    for u in range(PART[1], NG):
                        for s in range(2):
                            send_inverses(sp, inverses_in(got), t_mat, u, s, t_sent[1])
                    sp.wait_ge(t_sent[1], 16 * 8 * (NG - PART[1]))
                if has(t, NT):
                    wait_apart(sp, loaded, o_done, t - 3)
                    wait_apart(sp, loaded, diff_done, t - 3)
                    row = rec[bass.ds(t * P, P), :]
                    sp.dma_start(x16[:, k], t_mat[bass.ds(t * P, P), :].rearrange("p (h z c) -> p h z c", h=H, z=2)).then_inc(rec_in[k], 16)
                    sp.dma_start(kve[:, k], row[:, 0:3 * D].rearrange("p (n c) -> p n c", n=3)).then_inc(rec_in[k], 16)
                    cols = row[:, 3 * D:5 * D].rearrange("p (b t) -> p b t", b=4)
                    sp.dma_start(qkT[:, k], cols).then_inc(rec_in[k], 16)
                    for e in range(2):
                        r = slice(64 * e, 64 * e + 64)
                        sp.dma_start(eo[r, k, :, e, :], cols[r]).then_inc(rec_in[k], 16)

            pipelined(sp, NT, DEPTH, step, unroll=4)
            gate_loads = load_gate_weights(sp, gate_kept, w, gates_loaded)
            sp.wait_ge(gates_loaded, gate_loads)

        @block.gpsimd
        def _(pool):
            pool.memset(half[:, :], -0.5).then_inc(zeroed, 1)
            pool.memset(vb[:, :, :, :], 0.0).then_inc(zeroed, 1)
            pool.memset(u[:, :, :], 0.0).then_inc(zeroed, 1)
            pool.memset(S[:, :, :, :], 0.0).then_inc(zeroed, 1)
            for n in (1, 2):
                pool.memset(Z[n][:, :, :], 0.0).then_inc(zeroed, 1)
            pool.wait_ge(zeroed, 6)

            def step(i, k):
                t, s, q = i - 1, (k - 1) % 4, (k - 1) % 2
                if has(t, NT):
                    wait_apart(pool, loaded, rec_in[s], 20 * (t - s) + 80)
                    wait_apart(pool, loaded, xt_done, 3 * (t - 1))
                    wait_apart(pool, loaded, w_done, t - 1)
                    wait_apart(pool, loaded, u_done, t - 1)
                    for z, diagonal in enumerate((X, XT)):
                        pool.tensor_tensor(diagonal[:, q].rearrange("p h (b c) -> p h b c", c=SUB),
                                           x16[:, s, :, z, :].unsqueeze(2).broadcast_to([P, H, P // SUB, SUB]),
                                           block16[:, :].unsqueeze(1).unsqueeze(3).broadcast_to([P, H, P // SUB, SUB]),
                                           ALU.mult).then_inc(x0_done, 1)
                    beta = small[:, bass.ds(t, 1), 0:H].rearrange("p a h -> p (a h)").unsqueeze(2).broadcast_to([P, H, DH])
                    pool.tensor_tensor(kb[:, q, :].rearrange("p (h c) -> p h c", h=H),
                                       kve[:, s, 0, :].rearrange("p (h c) -> p h c", h=H), beta, ALU.mult).then_inc(kb_done, 1)
                    for e in range(2):
                        pool.tensor_tensor(vb[:, q, e::2, 64 * e:64 * e + 64],
                                           kve[:, s, 1, :].rearrange("p (h c) -> p h c", h=H)[:, e::2, :],
                                           beta[:, e::2, :], ALU.mult).then_inc(vb_done, 1)
                t = i - 3
                if has(t, NT):
                    mix = small[:, bass.ds(t, 1), H:2 * H].rearrange("p a h -> p (a h)").unsqueeze(2).broadcast_to([P, H, DH])
                    wait_apart(pool, loaded, diff_done, t + 1)
                    wait_apart(pool, loaded, o2_done, t)
                    pool.tensor_tensor(mixed[:, :].rearrange("p (h c) -> p h c", h=H),
                                       diff[:, :].rearrange("p (h c) -> p h c", h=H), mix, ALU.mult).then_inc(mixed_done, 1)
                    wait_apart(pool, loaded, ss_done, t + 1)
                    pool.tensor_scalar(ms[:, :], ss[:, :], 1.0 / DH, EPS, ALU.mult, ALU.add).then_inc(ms_done, 1)
                    wait_apart(pool, loaded, ms_done, t + 1)
                    wait_apart(pool, loaded, o3_done, t)
                    pool.tensor_tensor(rn[:, :], ms[:, :], half[:, :], ALU.pow).then_inc(rn_done, 1)

            pipelined(pool, NT, DEPTH, step, unroll=4)

        @block.scalar
        def _(act):
            act.wait_ge(zeroed, 6)

            def step(i, k):
                a, aq = i - 2, k % 2
                b = i - 3
                c = i - 4
                A, B, C = has(a, NT), has(b, NT), has(c, NT)
                if B:
                    act.wait_ge(w_done, b + 1)
                    wait(act, u_done, b)
                    act.activation(wT[:, :, :], b_w[:, 0:256].rearrange("p (n t) -> p n t", n=2), ACT.Copy,
                                   scale=-1.0).then_inc(w_out, 1)
                if A:
                    act.wait_ge(z_done, 3 * a + 2)
                    wait(act, xt_done, 3 * (a - 1) + 2)
                    for n in range(2):
                        r, cc = slice(64 * n, 64 * n + 32), slice(64 * n + 32, 64 * n + 64)
                        z = act.activation(Z[1][r, :, cc], heads(b_z)[r, :, cc], ACT.Copy, scale=-1.0)
                    z.then_inc(z_out, 1)
                if B:
                    act.wait_ge(s_done, b + 1)
                    wait(act, o_done, b - 1)
                    wait(act, u_done, b)
                    for e in range(2):
                        r = slice(64 * e, 64 * e + 64)
                        z = act.activation(S[r, (k - 3) % 2, :, r], b_s[r, 0:256].rearrange("p (n c) -> p n c", n=2)[:, :, r],
                                           ACT.Copy)
                    z.then_inc(s_out, 1)
                if A:
                    act.wait_ge(xt_done, 3 * a + 2)
                    for n in range(2):
                        r, cc = slice(64 * n, 64 * n + 32), slice(64 * n + 32, 64 * n + 64)
                        z = act.activation(XT[r, aq, :, cc], heads(b_xt)[r, :, cc], ACT.Copy)
                    z.then_inc(xt_out, 1)
                if C:
                    act.wait_ge(ot_done, c + 1)
                    wait(act, y_done, c)
                    act.activation(oT[:, :, :], b_w[:, 0:256].rearrange("p (n t) -> p n t", n=2), ACT.Copy).then_inc(ot_out, 1)
                if A:
                    act.wait_ge(xt_done, 3 * a + 3)
                    act.activation(XT[0:64, aq, :, 64:128], heads(b_xt)[0:64, :, 64:128], ACT.Copy).then_inc(xt_out, 1)
                if B:
                    act.wait_ge(o2_done, b + 1)
                    wait(act, ss_done, b)
                    act.activation(sq[:, :], o2[:, :], ACT.Square).then_inc(sq_done, 1)

            pipelined(act, NT, DEPTH, step, unroll=4)

        @block.vector
        def _(dve):
            dve.memset(eo[:, :, :, :, :], 0.0).then_inc(eo_zeroed, 1)
            dve.tensor_scalar(w_o[:, :, :], w_o[:, :, :], rms[:, 0:1], None, ALU.mult).then_inc(scaled, 1)
            dve.wait_ge(zeroed, 6)

            def step(i, k):
                a, aq = i - 2, k % 2
                b, bs, bq = i - 3, (k - 3) % 4, (k - 3) % 2
                c = i - 4
                A, B, C = has(a, NT), has(b, NT), has(c, NT)
                if A:
                    dve.wait_ge(g_done, a + 1)
                    for h in range(H):
                        g = dve.scalar_tensor_tensor(out=L[:, h, :], in0=heads(b_z)[:, h, :], scalar=small[:, bass.ds(a, 1), h],
                                                     in1=lower[:, :], op0=ALU.mult, op1=ALU.mult)
                    g.then_inc(l_done, 1)
                if C:
                    dve.wait_ge(rn_done, c + 1)
                    wait(dve, ot_done, c - 1)
                    dve.tensor_tensor(o3[:, aq, :].rearrange("p (h c) -> p h c", h=H),
                                      o2[:, :].rearrange("p (h c) -> p h c", h=H),
                                      rn[:, :].unsqueeze(2).broadcast_to([P, H, DH]), ALU.mult).then_inc(o3_done, 1)
                if A:
                    dve.wait_ge(st_done, a + 1)
                    wait(dve, o_done, a - 1)
                    dve.tensor_tensor(stm[:, aq], heads(b_x), causal[:, :].unsqueeze(1).broadcast_to([P, H, P]),
                                      ALU.mult).then_inc(stm_done, 1)
                    dve.wait_ge(z_done, 3 * a + 1)
                    dve.tensor_tensor(Z[0][:, :, :], heads(b_z), step16[:, :].unsqueeze(1).broadcast_to([P, H, P]),
                                      ALU.mult).then_inc(z_out, 1)
                if B:
                    dve.wait_ge(u_done, b + 1)
                    wait(dve, s_done, b)
                    wait(dve, o_done, b)
                    for e in range(2):
                        z = dve.tensor_copy(u[:, e::2, 64 * e:64 * e + 64],
                                            b_u[:, 0:256].rearrange("p (n e c) -> p n e c", n=2, e=2)[:, :, e, :])
                    z.then_inc(u_out, 1)
                if A:
                    dve.wait_ge(x_done, 2 * a + 1)
                    dve.wait_ge(xt_done, 3 * a + 1)
                    dve.tensor_tensor(XT[:, aq], XT[:, aq], heads(b_xt), ALU.add).then_inc(xt_out16, 1)
                    dve.tensor_tensor(X[:, aq], X[:, aq], heads(b_x), ALU.add).then_inc(x_out, 1)
                    dve.wait_ge(x_done, 2 * a + 2)
                    dve.wait_ge(xt_done, 3 * a + 2)
                    for n in range(2):
                        r, cc = slice(64 * n + 32, 64 * n + 64), slice(64 * n, 64 * n + 32)
                        z = dve.tensor_copy(X[r, aq, :, cc], heads(b_x)[r, :, cc])
                    z.then_inc(x_out, 1)
                    dve.wait_ge(z_done, 3 * a + 3)
                    dve.tensor_scalar(Z[2][0:64, :, 64:128], heads(b_z)[0:64, :, 64:128], -1.0, None, ALU.mult)\
                       .then_inc(z_out, 1)
                if B:
                    dve.wait_ge(o_done, b + 1)
                    wait(dve, mixed_done, b)
                    dve.tensor_tensor(diff[:, :], kve[:, bs, 2, :], b_o[:, 0:D], ALU.subtract).then_inc(diff_done, 1)
                if C:
                    dve.wait_ge(y_done, c + 1)
                    dve.tensor_tensor(tile_of(x_res, c), tile_of(x_res, c), b_y[:, 0:D], ALU.add).then_inc(y_out, 1)
                if B:
                    dve.wait_ge(mixed_done, b + 1)
                    wait(dve, sq_done, b)
                    wait(dve, o3_done, b)
                    dve.tensor_tensor(o2[:, :], b_o[:, 0:D], mixed[:, :], ALU.add).then_inc(o2_done, 1)
                    dve.wait_ge(sq_done, b + 1)
                    wait(dve, ms_done, b)
                    dve.tensor_reduce(ss[:, :], sq[:, :].rearrange("p (h c) -> p h c", h=H), AX.X, ALU.add).then_inc(ss_done, 1)

            pipelined(dve, NT, DEPTH, step, unroll=4)

        @block.tensor
        def _(pe):
            pe.wait_ge(zeroed, 6)
            pe.wait_ge(eo_zeroed, 1)
            pe.wait_ge(scaled, 1)

            def step(i, k):
                a, asl, aq = i - 2, (k - 2) % 4, k % 2
                b, bs, bq = i - 3, (k - 3) % 4, (k - 3) % 2
                c, cq = i - 4, k % 2
                A, B, C = has(a, NT), has(b, NT), has(c, NT)

                def four(bank, lhs, rhs):
                    for h in range(H):
                        mm = pe.matmul(bank[:, h * P:(h + 1) * P], lhs(h), rhs(h), start=True, stop=True)
                    return mm

                if A:
                    wait(pe, rec_in[asl], 20 * (a - asl) + 80)
                    wait(pe, z_out, 3 * a)
                    for n in range(2):
                        mm = pe.matmul(b_z[:, 256 * n:256 * n + 256], qkT[:, asl, 2 + n, :],
                                       eo[:, asl, 2 + n].rearrange("p e t -> p (e t)"), start=True, stop=True)
                    mm.then_inc(g_done, 1)
                    wait(pe, x_out, 2 * a)
                    for n in range(2):
                        mm = pe.matmul(b_x[:, 256 * n:256 * n + 256], qkT[:, asl, 2 + n, :],
                                       eo[:, asl, n].rearrange("p e t -> p (e t)"), start=True, stop=True)
                    mm.then_inc(st_done, 1)
                if B:
                    pe.wait_ge(kb_done, b + 1)
                    pe.wait_ge(xt_out, 2 * (b + 1))
                    wait(pe, ot_out, b - 1)
                    for h in range(H):
                        e = h % 2
                        mm = pe.matmul(b_w[64 * e:64 * e + 64, (h // 2) * P:(h // 2 + 1) * P], kb[:, bq, h * DH:(h + 1) * DH],
                                       XT[:, bq, h, :], start=True, stop=True)
                    mm.then_inc(w_done, 1)
                    pe.wait_ge(vb_done, 2 * (b + 1))
                    wait(pe, u_out, b)
                    for h in range(H):
                        pe.matmul(b_u[:, (h // 2) * P:(h // 2 + 1) * P], XT[:, bq, h, :], vb[:, bq, h, :], start=(h == 0),
                                  stop=False, skip_group_check=True)
                if A:
                    pe.wait_ge(l_done, a + 1)
                    pe.wait_ge(x0_done, 2 * (a + 1))
                    four(b_z, lambda h: L[:, h, :], lambda h: XT[:, aq, h, :]).then_inc(z_done, 1)
                if B:
                    pe.wait_ge(w_out, b + 1)
                    wait(pe, s_out, b)
                    for n in range(2):
                        mm = pe.matmul(b_u[:, n * P:(n + 1) * P], wT[:, n, :], S[:, 1 - bq, n, :], start=False, stop=True,
                                       skip_group_check=True)
                    mm.then_inc(u_done, 1)
                if C:
                    pe.wait_ge(o3_done, c + 1)
                    wait(pe, w_out, c + 2, NT)
                    for n in range(KD):
                        mm = pe.transpose(b_w[:, n * P:(n + 1) * P], o3[:, cq, n * P:(n + 1) * P], ident[:, :])
                    mm.then_inc(ot_done, 1)
                if A:
                    wait(pe, xt_out, 2 * a)
                    pe.wait_ge(z_out, 3 * a + 1)
                    pe.wait_ge(stm_done, a + 1)
                    four(b_xt, lambda h: X[:, aq, h, :], lambda h: Z[0][:, h, :]).then_inc(xt_done, 1)
                    four(b_x, lambda h: Z[0][:, h, :], lambda h: X[:, aq, h, :]).then_inc(x_done, 1)
                if B:
                    pe.wait_ge(u_out, b + 1)
                    for n in range(2):
                        u_own = u[:, 2 * n:2 * n + 2, :].rearrange("p e (a c) -> p (e a) c", c=DH)[:, 0:4:3, :]
                        mm = pe.matmul(b_s[:, n * P:(n + 1) * P], kve[:, bs, 0, n * P:(n + 1) * P], u_own,
                                       start=(isinstance(b, int) and b == 0 and n == 0), stop=True,
                                       skip_group_check=True)
                    mm.then_inc(s_done, 1)
                    wait(pe, o2_done, b)
                    for n in range(2):
                        pe.matmul(b_o[:, n * P:(n + 1) * P], qkT[:, bs, n, :], S[:, 1 - bq, n, :], start=(n == 0), stop=False,
                                  skip_group_check=True)
                if A:
                    pe.wait_ge(xt_out16, a + 1)
                    four(b_z, lambda h: L[:, h, :], lambda h: XT[:, aq, h, :]).then_inc(z_done, 1)
                if B:
                    pe.wait_ge(stm_done, b + 1)
                    for h in range(H):
                        mm = pe.matmul(b_o[:, (h // 2) * P:(h // 2 + 1) * P], stm[:, bq, h, :], u[:, h, :], start=False,
                                       stop=(h % 2 == 1), skip_group_check=True)
                    mm.then_inc(o_done, 1)
                if A:
                    pe.wait_ge(z_out, 3 * a + 2)
                    pe.wait_ge(x_out, 2 * a + 1)
                    four(b_xt, lambda h: X[:, aq, h, :], lambda h: Z[1][:, h, :]).then_inc(xt_done, 1)
                    four(b_x, lambda h: Z[1][:, h, :], lambda h: X[:, aq, h, :]).then_inc(x_done, 1)
                if A:
                    pe.wait_ge(xt_out, 2 * a + 1)
                    for h in range(H):
                        mm = pe.matmul(b_z[0:64, h * P + 64:(h + 1) * P], L[:, h, 0:64], XT[:, aq, h, 64:128],
                                       start=True, stop=True)
                    mm.then_inc(z_done, 1)
                if C:
                    pe.wait_ge(ot_out, c + 1)
                    wait(pe, y_out, c)
                    for n in range(KD):
                        mm = pe.matmul(b_y[:, 0:D], oT[:, n, :], w_o[:, n, :], start=(n == 0), stop=(n == KD - 1))
                    mm.then_inc(y_done, 1)
                if A:
                    pe.wait_ge(z_out, 3 * a + 3)
                    pe.wait_ge(x_out, 2 * a + 2)
                    for h in range(H):
                        mm = pe.matmul(b_xt[0:64, h * P + 64:(h + 1) * P], X[:, aq, h, 0:64], Z[2][:, h, 64:128],
                                       start=True, stop=True)
                    mm.then_inc(xt_done, 1)

            pipelined(pe, NT, DEPTH, step, unroll=4)


def gated_output(nc, kept, ident, loaded, x_res, out):
    with ExitStack() as ctx:
        def sb(name, shape, dt=F32):
            return ctx.enter_context(nc.sbuf_tensor("g_" + name, shape, dt))

        def psum(name):
            return ctx.enter_context(nc.psum_tensor("g_" + name, [P, 512], F32))

        def sem(name):
            return ctx.enter_context(nc.semaphore("g_" + name))

        w_g = kept["w_g"]
        u_g = kept["u_g"]
        b_g = kept["b_g"]
        c0 = kept["c0"]
        c0h = sb("c0h", [P, KD])
        bias = sb("bias", [P, 6])
        w_o = kept["w_o"]
        u_o = kept["u_o"]
        b_o = kept["b_o"]
        half = sb("half", [P, GROUP])
        stats = sb("stats", [P, GROUP, 6])
        mom = sb("mom", [P, GROUP, 2])
        shifted = sb("shifted", [P, GROUP])
        rstd = sb("rstd", [P, GROUP])
        xn = sb("xn", [P, 2, GROUP, D])
        xT = sb("xT", [P, 2, KD, GW])
        gates = sb("gates", [P, 6, GW])
        cT = sb("cT", [P, 2, KD, GW])
        z = sb("z", [P, 2, D])
        h = sb("h", [P, 2, D])
        res = sb("res", [P, 2, D])
        pp = [psum(f"pp{i}") for i in range(2)]
        py = [psum(f"py{i}") for i in range(2)]
        ready = sem("ready")
        bias_done = sem("bias_done")
        bias_set = sem("bias_set")
        stats_done = sem("stats_done")
        mom_done = sem("mom_done")
        shift_done = sem("shift_done")
        rstd_done = sem("rstd_done")
        norm_done = sem("norm_done")
        p_done = sem("p_done")
        p_out = sem("p_out")
        keep_done = sem("keep_done")
        new_done = sem("new_done")
        c_done = sem("c_done")
        y_done = sem("y_done")
        z_done = sem("z_done")
        h_done = sem("h_done")
        res_done = sem("res_done")
        sent = [sem(f"sent{i}") for i in range(2)]
        block = ctx.enter_context(nc.Block())
        DEPTH = 2
        AFTER = [(), (), (), (0,), (), (1,), (2,), (3,)]

        @block.sync
        def _(sp):
            def step(i, par):
                v = i - 2
                if has(v, NG):
                    for j in range(GROUP):
                        t, s = GROUP * v + j, j % 2
                        wait_apart(sp, loaded, res_done, t + 1)
                        sp.dma_start(out[bass.ds(t * P, P), :], res[:, s, :]).then_inc(sent[s], 16)

            pipelined(sp, NG, DEPTH, step)
            for s in range(2):
                sp.wait_ge(sent[s], 16 * NT // 2)

        @block.gpsimd
        def _(pool):
            pool.memset(half[:, :], -0.5).then_inc(ready, 1)
            pool.wait_ge(ready, 1)

            def step(i, par):
                if has(i, NG):
                    wait_apart(pool, loaded, mom_done, GROUP * (i + 1))
                    wait_apart(pool, loaded, norm_done, GROUP * i)
                    pool.tensor_scalar(shifted[:, :], mom[:, :, 1], EPS, None, ALU.add).then_inc(shift_done, 1)
                    wait_apart(pool, loaded, shift_done, i + 1)
                    pool.tensor_tensor(rstd[:, :], shifted[:, :], half[:, :], ALU.pow).then_inc(rstd_done, 1)

            pipelined(pool, NG, DEPTH, step)

        @block.scalar
        def _(act):
            act.wait_ge(bias_set, 4)

            def step(i, par):
                u, q = i - 1, (par - 1) % 2
                v = i - 2

                def use(n):
                    bank = pp[n % 2]
                    act.wait_ge(p_done, 8 * u + n + 1)
                    if n < 2:
                        wait(act, y_done, GROUP * (u - 1))
                        act.activation(xT[:, q, n, :], bank[:, :], ACT.Copy).then_inc(p_out, 1)
                    else:
                        b = n - 2
                        wait(act, c_done, 2 * u)
                        act.activation(gates[:, b, :], bank[:, :], ACT.Tanh, bias=bias[:, b:b + 1],
                                       scale=0.5 if b < 4 else 1.0).then_inc(p_out, 1)

                for n in range(8):
                    if has(u, NG):
                        use(n)
                    for j in AFTER[n] if has(v, NG) else ():
                        t, s = GROUP * v + j, j % 2
                        act.wait_ge(z_done, t + 1)
                        wait(act, res_done, t - 1)
                        act.activation(h[:, s, :], z[:, s, :], ACT.Tanh).then_inc(h_done, 1)

            pipelined(act, NG, DEPTH, step)

        @block.vector
        def _(dve):
            dve.tensor_scalar(c0h[:, :], c0[:, :], 0.5, None, ALU.mult).then_inc(bias_set, 1)
            dve.wait_ge(bias_done, 1)
            dve.tensor_tensor(bias[:, :], pp[0][:, 0:6], b_g[:, :], ALU.add).then_inc(bias_set, 1)
            dve.wait_ge(bias_set, 2)
            dve.tensor_scalar(bias[:, 0:4], bias[:, 0:4], 0.5, None, ALU.mult).then_inc(bias_set, 2)

            def step(i, par):
                u, q = i - 1, (par - 1) % 2
                v = i - 2
                if has(i, NG):
                    for j in range(GROUP):
                        t = GROUP * i + j
                        wait_apart(dve, loaded, norm_done, GROUP * i)
                        dve.bn_stats(stats[:, j, :], tile_of(x_res, t)).then_inc(stats_done, 1)
                    for j in range(GROUP):
                        wait_apart(dve, loaded, stats_done, GROUP * i + j + 1)
                        dve.bn_aggr(mom[:, j, :], stats[:, j, :]).then_inc(mom_done, 1)

                def last(j):
                    t, s = GROUP * v + j, j % 2
                    dve.wait_ge(y_done, t + 1)
                    wait(dve, h_done, t - 1)
                    dve.tensor_tensor(z[:, s, :], py[s][:, 0:D], b_o[:, :], ALU.add).then_inc(z_done, 1)

                def residual(j):
                    t, s = GROUP * v + j, j % 2
                    dve.wait_ge(h_done, t + 1)
                    wait(dve, sent[s], 8 * (GROUP * v + j - s))
                    dve.tensor_tensor(res[:, s, :], h[:, s, :], tile_of(x_res, t), ALU.add).then_inc(res_done, 1)

                if has(v, NG):
                    last(0)
                    last(1)
                    residual(0)
                if has(i, NG):
                    dve.wait_ge(rstd_done, i + 1)
                    wait(dve, p_done, 8 * (i - 2) + 2)
                    for j in range(GROUP):
                        dve.tensor_scalar(xn[:, par, j, :], tile_of(x_res, GROUP * i + j), mom[:, j, 0:1], rstd[:, j:j + 1],
                                          ALU.subtract, ALU.mult).then_inc(norm_done, 1)
                if has(v, NG):
                    last(2)
                    residual(1)
                    last(3)
                    residual(2)
                    residual(3)
                if has(u, NG):
                    wait(dve, y_done, GROUP * (u - 1))
                    dve.wait_ge(p_out, 8 * u + 8)
                    for b in range(KD):
                        g = 2 * u + b + 1
                        dve.tensor_scalar(gates[:, b, :], gates[:, b, :], c0h[:, b:b + 1], c0h[:, b:b + 1], ALU.mult,
                                          ALU.add).then_inc(keep_done, 1)
                        dve.scalar_tensor_tensor(out=gates[:, 2 + b, :], in0=gates[:, 2 + b, :], scalar=1.0,
                                                 in1=gates[:, 4 + b, :], op0=ALU.add, op1=ALU.mult).then_inc(new_done, 1)
                        wait(dve, keep_done, g)
                        wait(dve, new_done, g)
                        dve.scalar_tensor_tensor(out=cT[:, q, b, :], in0=gates[:, 2 + b, :], scalar=0.5, in1=gates[:, b, :],
                                                 op0=ALU.mult, op1=ALU.add).then_inc(c_done, 1)

            pipelined(dve, NG, DEPTH, step)

        @block.tensor
        def _(pe):
            for n in range(3):
                for b in range(KD):
                    for k in range(KD):
                        mm = pe.matmul(pp[0][:, 2 * n + b:2 * n + b + 1], u_g[:, k, n, b * P:(b + 1) * P], c0[:, k:k + 1],
                                       start=(k == 0), stop=(k == KD - 1))
            mm.then_inc(bias_done, 1)
            pe.wait_ge(bias_set, 4)

            def step(i, par):
                u, q = i - 1, (par - 1) % 2
                v, r = i - 2, par

                def use(n):
                    bank = pp[n % 2]
                    wait(pe, p_out, 8 * u + n - 1)
                    if n < 2:
                        pe.wait_ge(norm_done, GROUP * (u + 1))
                        for j in range(GROUP):
                            mm = pe.transpose(bank[:, j * P:(j + 1) * P], xn[:, q, j, n * P:(n + 1) * P], ident[:, :])
                    else:
                        b = n - 2
                        pe.wait_ge(p_out, 8 * u + 2)
                        for k in range(KD):
                            mm = pe.matmul(bank[:, :], w_g[:, k, b // 2, (b % 2) * P:(b % 2 + 1) * P], xT[:, q, k, :],
                                           start=(k == 0), stop=(k == KD - 1))
                    mm.then_inc(p_done, 1)

                for n in range(8):
                    if has(u, NG):
                        use(n)
                    for j in AFTER[n] if has(v, NG) else ():
                        t, s = GROUP * v + j, j % 2
                        cols = slice(j * P, (j + 1) * P)
                        pe.wait_ge(c_done, 2 * (v + 1))
                        wait(pe, z_done, t - 1)
                        for k in range(KD):
                            pe.matmul(py[s][:, 0:D], xT[:, r, k, cols], w_o[:, k, :], start=(k == 0), stop=False)
                        for k in range(KD):
                            mm = pe.matmul(py[s][:, 0:D], cT[:, r, k, cols], u_o[:, k, :], start=False, stop=(k == KD - 1))
                        mm.then_inc(y_done, 1)

            pipelined(pe, NG, DEPTH, step)


def build(nc, w, out):
    x_slots = nc.dram_tensor("x_slots", [SLOTS, D], F32, kind="Internal").ap()
    y_slots = nc.dram_tensor("y_slots", [SLOTS, D], F32, kind="Internal").ap()
    rec = nc.dram_tensor("rec", [T, REC], F32, kind="Internal").ap()
    l_mat = nc.dram_tensor("l_mat", [T, NH1 * 2 * SUB], F32, kind="Internal").ap()
    t_mat = nc.dram_tensor("t_mat", [T, NH1 * 2 * SUB], F32, kind="Internal").ap()
    with ExitStack() as ctx:
        x_res = ctx.enter_context(nc.sbuf_tensor("x_res", [P, NT, D], F32))
        gates = ctx.enter_context(nc.sbuf_tensor("gates", [P, 2, NT], F32))
        slots = ctx.enter_context(nc.sbuf_tensor("slots", [P, 2, NT], U32))
        small = ctx.enter_context(nc.sbuf_tensor("small", [P, NT, 3 * NH1], F32))
        kept = delta_weights(nc, ctx)
        kept_loaded = ctx.enter_context(nc.semaphore("kept_loaded"))
        with ExitStack() as first:
            xn2_res = first.enter_context(nc.sbuf_tensor("xn2_res", [P, NT, D], F32))
            consts = route_constants(nc, first)
            logits = first.enter_context(nc.sbuf_tensor("logits", [P, NT, E], F32))
            tile_expert = first.enter_context(nc.sbuf_tensor("tile_expert", [P, SLOT_TILES], I32))
            w13 = first.enter_context(nc.sbuf_tensor("w13", [P, 2, KD, E, HID], F32))
            w2 = first.enter_context(nc.sbuf_tensor("w2", [P, len(HB), E, D], F32))
            with nc.semaphore("layer0_first") as first_sem:
                pass
            linear_attention(nc, x_res, xn2_res, logits, consts, w13, w2, x_slots, w)
            route(nc, consts, xn2_res, logits, gates, slots, tile_expert, x_slots)
            experts(nc, consts["ident"], kept, kept_loaded, tile_expert, x_slots, y_slots, w13, w2, w)
            with nc.semaphore("layer0_last") as last_sem:
                pass
            with nc.Block() as block:
                @block.gpsimd
                def _(pool):
                    pool.sem_clear(range(first_sem.num, last_sem.num + 1))
        got = ctx.enter_context(nc.sbuf_tensor("got", [P, 2, GROUP, 2, D], F32))
        t_sent = [ctx.enter_context(nc.semaphore(f"t_sent{n}")) for n in range(2)]
        delta_inputs(nc, kept, kept_loaded, got, t_sent, x_res, gates, slots, y_slots, small, rec, l_mat, t_mat)
        gate_kept = gate_weights(nc, ctx)
        delta_rule(nc, kept, gate_kept, kept_loaded, got, t_sent, x_res, small, rec, t_mat, w)
        gated_output(nc, gate_kept, kept["ident"], kept_loaded, x_res, out)


def constants():
    p = np.arange(P)
    row, col = p[:, None], p[None, :]
    f = np.float32
    return {
        "c_ident": np.eye(P, dtype=f),
        "c_causal": (row <= col).astype(f),
        "c_lower": (col < row).astype(f),
        "c_strict": (row < col).astype(f),
        "c_ones": np.ones((P, P), f),
        "c_eo": (row // 16 % 2 == np.arange(2)).astype(f),
        "c_head": (row // 16 == col // 16).astype(f),
        "c_pair": (row // DH == np.arange(2)).astype(f),
        "c_step16": -((col // SUB % 2 == 1) & (row // SUB == col // SUB - 1)).astype(f),
        "c_block16": (row // SUB == np.arange(P // SUB)).astype(f),
        "c_prio": np.arange(E, 0, -1).astype(f),
        "c_follows": np.tile((np.arange(NT) > 0).astype(f), (E, 1)),
        "c_edges": (P * np.arange(NT)).astype(f),
        "c_numbers": np.arange(SLOT_TILES).astype(f),
    }


def laid_out(inputs):
    a = {k: np.asarray(v) for k, v in inputs.items()}
    l0, f0, l1, f1 = (lambda n, p=p: a[p + n] for p in ("L0_attn_", "L0_ffn_", "L1_attn_", "L1_ffn_"))

    def columns(*vectors):
        return np.concatenate(vectors).reshape(-1, P).T

    k, q, v = np.split(l0("b1"), 3)
    w = {
        "x": l0("x").reshape(T, D), "W1": l0("W1"), "W2": l0("W2"), "b2": l0("b2"),
        "b_qk": columns(q, k), "b_kv": np.concatenate([k, v]),
        "w_rT": f0("w_router").T, "w1": f0("w1"), "w2": f0("w2"), "w3": f0("w3"),
        "rms_w": l1("rms_w").reshape(DH, 1), "Wo": l1("Wo"),
        "b_gates": columns(f1("bf"), f1("bi"), f1("bc")), "c0": columns(f1("in_c")),
        "woT": f1("wo").T, "uoT": f1("uo").T, "bo": f1("bo"),
    }
    w["w_small"] = np.concatenate([l1("Wmix"), np.zeros((D, SM - 2 * NH1), np.float32), l1("Wb")], 1)
    for name in ("Wq", "Wk", "Wv", "Wdec", "conv_q", "conv_k", "conv_v", "conv_mix", "mix_bias"):
        w[name] = l1(name)
    for g in "fic":
        w[f"w{g}T"] = f1("w" + g).T
        w[f"u{g}T"] = f1("u" + g).T
    return {name: np.ascontiguousarray(v) for name, v in {**w, **constants()}.items()}


def kernel(**inputs):
    import concourse.bacc as bacc
    from concourse.bass_utils import run_bass_kernel_spmd

    nc = bacc.Bacc("TRN2", target_bir_lowering=False, num_devices=1)
    arrays = {f"in_{name}": a for name, a in laid_out(inputs).items()}
    w = {name[3:]: nc.dram_tensor(name, a.shape, mybir.dt.from_np(a.dtype), kind="ExternalInput").ap()
         for name, a in arrays.items()}
    out = nc.dram_tensor("out_dram", (T, D), F32, kind="ExternalOutput").ap()
    build(nc, w, out)
    r = run_bass_kernel_spmd(nc, [arrays], core_ids=[0])
    return r.results[0]["out_dram"].reshape(1, T, D)
```
